# Optimizing a Trainium2 kernel written in Bass

```python
import numpy as np
import jax
import jax.numpy as jnp

def _softmax(x, axis=-1):
    return jax.nn.softmax(x, axis=axis)

def _gelu(x):
    return jax.nn.gelu(x, approximate=True)

def _silu(x):
    return jax.nn.silu(x)

def _sigmoid(x):
    return jax.nn.sigmoid(x)

def _layernorm(x, axis=-1, eps=1e-05):
    m = jnp.mean(x, axis=axis, keepdims=True)
    v = jnp.var(x, axis=axis, keepdims=True)
    return (x - m) / jnp.sqrt(v + eps)

def _scatter_add(tgt, idx, src, axis=0):
    return tgt.at[idx].add(src)

def _segment_sum(src, seg, n):
    return jax.ops.segment_sum(src, seg, n)
kernel_name = 'mk_gnn_preln_d2_gnn_r32_f6119f'

def setup_inputs(seed: int=0):
    np.random.seed(seed)
    _w = jnp.asarray

    def _rec_inputs():
        import jax
        import jax.numpy as jnp
        _gk = jax.random.key(seed)
        x = 7.22e-05 + 1 * jax.random.normal(jax.random.fold_in(_gk, 1), (10000, 512), jnp.float32)
        src = jax.random.randint(jax.random.fold_in(_gk, 2), (10000,), 0, 10000, jnp.int32)
        dst = jax.random.randint(jax.random.fold_in(_gk, 3), (10000,), 0, 10000, jnp.int32)
        _o = jnp.argsort(dst, stable=True)
        src = src[_o]
        dst = dst[_o]
        edge_attr_20 = 0.000389844 + 1.00025 * jax.random.normal(jax.random.fold_in(_gk, 12), (10000, 20), jnp.float32)
        edge_attr_4 = -0.00185629 + 0.998788 * jax.random.normal(jax.random.fold_in(_gk, 13), (10000, 4), jnp.float32)
        edge_weight = jax.random.uniform(jax.random.fold_in(_gk, 15), (10000,), jnp.float32, 0.0, 0.999993)
        return (x, src, dst, edge_attr_20, edge_attr_4, edge_weight)
    x, src, dst, edge_attr_20, edge_attr_4, edge_weight = _rec_inputs()

    def _L0_gnn_setup():
        import jax, jax.numpy as jnp
        import numpy as np
        import math
        B = 128
        F = 32
        R = 20
        N = 512
        E = 8192
        LOG2 = 0.6931471805599453
        IS2 = 1.0 / math.sqrt(2.0)
        IS3 = 1.0 / math.sqrt(3.0)
        IS6 = 1.0 / math.sqrt(6.0)

        def ssp(x):
            return jax.nn.softplus(x) - LOG2
        key = jax.random.key(seed)
        ks = jax.random.split(key, 14)
        return dict(x=jax.random.normal(ks[0], (N, 4 * B), jnp.float32), idx_i=jax.random.randint(ks[1], (E,), 0, N), idx_j=jax.random.randint(ks[2], (E,), 0, N), f_ij=jax.random.normal(ks[3], (E, R), jnp.float32), rcut_ij=jax.random.uniform(ks[4], (E,), jnp.float32), Yr_ij=jax.random.normal(ks[5], (E, 4), jnp.float32), w_in2f_s=jax.random.normal(ks[6], (B, F), jnp.float32), w_in2f_v=jax.random.normal(ks[7], (B, F), jnp.float32), W1=jax.random.normal(ks[8], (R, F), jnp.float32) / math.sqrt(R), b1=jnp.zeros((F,), jnp.float32), W2=jax.random.normal(ks[9], (F, 6 * F), jnp.float32) / math.sqrt(F), b2=jnp.zeros((6 * F,), jnp.float32), w_f2o1_s=jax.random.normal(ks[10], (2 * F, B), jnp.float32), w_f2o1_v=jax.random.normal(ks[11], (2 * F, B), jnp.float32), w_f2o2_s=jax.random.normal(ks[12], (B, B), jnp.float32), w_f2o2_v=jax.random.normal(ks[13], (B, B), jnp.float32))
    _L0_gnn_all = _L0_gnn_setup()
    _L0_gnn_in = {k: v for k, v in _L0_gnn_all.items() if k in ('w_in2f_s', 'w_in2f_v', 'W1', 'b1', 'W2', 'b2', 'w_f2o1_s', 'w_f2o1_v', 'w_f2o2_s', 'w_f2o2_v')}
    del _L0_gnn_all

    def _L1_gnn_setup():
        import jax, jax.numpy as jnp
        import numpy as np
        D = 512
        H = 8
        DH = D // H
        F = 64
        L = 2
        N = 625
        E = 10000
        EPS = 1e-05

        def _xavier(key, shape):
            fan_out, fan_in = (shape[-2], shape[-1])
            lim = float(np.sqrt(6.0 / (fan_in + fan_out)))
            return jax.random.uniform(key, shape, jnp.float32, -lim, lim)

        def _batchnorm(x, g, b):
            mu = jnp.mean(x, axis=0)
            var = jnp.mean(jnp.square(x - mu), axis=0)
            return (x - mu) * jax.lax.rsqrt(var + EPS) * g + b

        def _layernorm(x, g, b):
            mu = jnp.mean(x, axis=-1, keepdims=True)
            var = jnp.mean(jnp.square(x - mu), axis=-1, keepdims=True)
            return (x - mu) * jax.lax.rsqrt(var + EPS) * g + b
        key = jax.random.key(seed)
        ks = jax.random.split(key, 12)
        src = jax.random.normal(ks[0], (N, D), jnp.float32)
        edge_index = jax.random.randint(ks[1], (2, E), 0, N)
        return {'src': src, 'edge_index': edge_index, 'Wq': _xavier(ks[2], (L, D, D)), 'bq': jnp.zeros((L, D), jnp.float32), 'Wk': _xavier(ks[3], (L, D, D)), 'Wv': _xavier(ks[4], (L, D, D)), 'Wo': _xavier(ks[5], (L, D, D)), 'bo': jnp.zeros((L, D), jnp.float32), 'W1': _xavier(ks[6], (L, F, D)), 'b1': jnp.zeros((L, F), jnp.float32), 'W2': _xavier(ks[7], (L, D, F)), 'b2': jnp.zeros((L, D), jnp.float32), 'g1': jnp.ones((L, D), jnp.float32), 'beta1': jnp.zeros((L, D), jnp.float32), 'g2': jnp.ones((L, D), jnp.float32), 'beta2': jnp.zeros((L, D), jnp.float32), 'ln_g': jnp.ones((D,), jnp.float32), 'ln_b': jnp.zeros((D,), jnp.float32)}
    _L1_gnn_all = _L1_gnn_setup()
    _L1_gnn_in = {k: v for k, v in _L1_gnn_all.items() if k in ('Wq', 'bq', 'Wk', 'Wv', 'Wo', 'bo', 'W1', 'b1', 'W2', 'b2', 'g1', 'beta1', 'g2', 'beta2', 'ln_g', 'ln_b')}
    del _L1_gnn_all
    return {'x': x, 'src': src, 'dst': dst, 'edge_attr_20': edge_attr_20, 'edge_attr_4': edge_attr_4, 'edge_weight': edge_weight, 'L0_gnn_w_in2f_s': _L0_gnn_in['w_in2f_s'], 'L0_gnn_w_in2f_v': _L0_gnn_in['w_in2f_v'], 'L0_gnn_W1': _L0_gnn_in['W1'], 'L0_gnn_b1': _L0_gnn_in['b1'], 'L0_gnn_W2': _L0_gnn_in['W2'], 'L0_gnn_b2': _L0_gnn_in['b2'], 'L0_gnn_w_f2o1_s': _L0_gnn_in['w_f2o1_s'], 'L0_gnn_w_f2o1_v': _L0_gnn_in['w_f2o1_v'], 'L0_gnn_w_f2o2_s': _L0_gnn_in['w_f2o2_s'], 'L0_gnn_w_f2o2_v': _L0_gnn_in['w_f2o2_v'], 'L1_gnn_Wq': _L1_gnn_in['Wq'], 'L1_gnn_bq': _L1_gnn_in['bq'], 'L1_gnn_Wk': _L1_gnn_in['Wk'], 'L1_gnn_Wv': _L1_gnn_in['Wv'], 'L1_gnn_Wo': _L1_gnn_in['Wo'], 'L1_gnn_bo': _L1_gnn_in['bo'], 'L1_gnn_W1': _L1_gnn_in['W1'], 'L1_gnn_b1': _L1_gnn_in['b1'], 'L1_gnn_W2': _L1_gnn_in['W2'], 'L1_gnn_b2': _L1_gnn_in['b2'], 'L1_gnn_g1': _L1_gnn_in['g1'], 'L1_gnn_beta1': _L1_gnn_in['beta1'], 'L1_gnn_g2': _L1_gnn_in['g2'], 'L1_gnn_beta2': _L1_gnn_in['beta2'], 'L1_gnn_ln_g': _L1_gnn_in['ln_g'], 'L1_gnn_ln_b': _L1_gnn_in['ln_b']}

def reference(x, src, dst, edge_attr_20, edge_attr_4, edge_weight, L0_gnn_w_in2f_s, L0_gnn_w_in2f_v, L0_gnn_W1, L0_gnn_b1, L0_gnn_W2, L0_gnn_b2, L0_gnn_w_f2o1_s, L0_gnn_w_f2o1_v, L0_gnn_w_f2o2_s, L0_gnn_w_f2o2_v, L1_gnn_Wq, L1_gnn_bq, L1_gnn_Wk, L1_gnn_Wv, L1_gnn_Wo, L1_gnn_bo, L1_gnn_W1, L1_gnn_b1, L1_gnn_W2, L1_gnn_b2, L1_gnn_g1, L1_gnn_beta1, L1_gnn_g2, L1_gnn_beta2, L1_gnn_ln_g, L1_gnn_ln_b):
    import jax
    import jax.numpy as jnp

    def _L0_gnn_ref(x, idx_i, idx_j, f_ij, rcut_ij, Yr_ij, w_in2f_s, w_in2f_v, W1, b1, W2, b2, w_f2o1_s, w_f2o1_v, w_f2o2_s, w_f2o2_v):
        import jax, jax.numpy as jnp
        import numpy as np
        import math
        B = 128
        F = 32
        R = 20
        N = 512
        E = 8192
        LOG2 = 0.6931471805599453
        IS2 = 1.0 / math.sqrt(2.0)
        IS3 = 1.0 / math.sqrt(3.0)
        IS6 = 1.0 / math.sqrt(6.0)

        def ssp(x):
            return jax.nn.softplus(x) - LOG2
        n = x.shape[0]
        xs = x[:, :B]
        xv = x[:, B:].reshape(n, B, 3)
        hs = xs @ w_in2f_s / math.sqrt(B)
        hv = jnp.einsum('nbc,bf->nfc', xv, w_in2f_v) / math.sqrt(B)
        s = hs[idx_j]
        v = hv[idx_j]
        ys = Yr_ij[:, 0]
        yv = Yr_ij[:, 1:4]
        t_s1 = s * ys[:, None]
        t_s2 = jnp.einsum('efc,ec->ef', v, yv) * IS3
        t_v1 = s[:, :, None] * yv[:, None, :]
        t_v2 = v * ys[:, None, None]
        t_pv = jnp.cross(v, yv[:, None, :]) * IS2
        ax, ay, az = (v[..., 0], v[..., 1], v[..., 2])
        bx, by, bz = (yv[:, None, 0:1], yv[:, None, 1:2], yv[:, None, 2:3])
        bx, by, bz = (bx[..., 0], by[..., 0], bz[..., 0])
        t_q = jnp.stack([(ax * by + ay * bx) * IS2, (ay * bz + az * by) * IS2, (2.0 * az * bz - ax * bx - ay * by) * IS6, (ax * bz + az * bx) * IS2, (ax * bx - ay * by) * IS2], axis=-1)
        h = ssp(f_ij @ W1 + b1)
        Wij = (h @ W2 + b2) * rcut_ij[:, None]
        Wf = Wij.reshape(-1, F, 6)
        edge = jnp.concatenate([(t_s1 * Wf[..., 0])[..., None], (t_s2 * Wf[..., 1])[..., None], t_v1 * Wf[..., 2:3], t_v2 * Wf[..., 3:4], t_pv * Wf[..., 4:5], t_q * Wf[..., 5:6]], axis=-1)
        agg = jax.ops.segment_sum(edge.reshape(edge.shape[0], -1), idx_i, num_segments=n).reshape(n, F, 16)
        s_in = jnp.concatenate([agg[..., 0], agg[..., 1]], axis=1)
        v_in = jnp.concatenate([agg[..., 2:5], agg[..., 5:8]], axis=1)
        os1 = s_in @ w_f2o1_s / math.sqrt(2 * F)
        ov1 = jnp.einsum('nmc,mb->nbc', v_in, w_f2o1_v) / math.sqrt(2 * F)
        os1 = ssp(os1)
        os2 = os1 @ w_f2o2_s / math.sqrt(B)
        ov2 = jnp.einsum('nbc,bd->ndc', ov1, w_f2o2_v) / math.sqrt(B)
        return jnp.concatenate([os2, ov2.reshape(n, -1)], axis=-1)

    def _L1_gnn_ref(src, edge_index, Wq, bq, Wk, Wv, Wo, bo, W1, b1, W2, b2, g1, beta1, g2, beta2, ln_g, ln_b):
        import jax, jax.numpy as jnp
        import numpy as np
        D = 512
        H = 8
        DH = D // H
        F = 64
        L = 2
        N = 625
        E = 10000
        EPS = 1e-05

        def _xavier(key, shape):
            fan_out, fan_in = (shape[-2], shape[-1])
            lim = float(np.sqrt(6.0 / (fan_in + fan_out)))
            return jax.random.uniform(key, shape, jnp.float32, -lim, lim)

        def _batchnorm(x, g, b):
            mu = jnp.mean(x, axis=0)
            var = jnp.mean(jnp.square(x - mu), axis=0)
            return (x - mu) * jax.lax.rsqrt(var + EPS) * g + b

        def _layernorm(x, g, b):
            mu = jnp.mean(x, axis=-1, keepdims=True)
            var = jnp.mean(jnp.square(x - mu), axis=-1, keepdims=True)
            return (x - mu) * jax.lax.rsqrt(var + EPS) * g + b
        n = src.shape[0]
        scaling = float(DH) ** (-0.5)
        tgt = edge_index[1]
        srcidx = edge_index[0]
        x = src
        for l in range(L):
            q = ((x @ Wq[l].T + bq[l]) * scaling).reshape(n, H, DH)
            k = (x @ Wk[l].T).reshape(n, H, DH)
            v = (x @ Wv[l].T).reshape(n, H, DH)
            scores = jnp.einsum('ehd,ehd->eh', q[tgt], k[srcidx])
            m = jax.ops.segment_max(scores, tgt, num_segments=n)
            p = jnp.exp(scores - m[tgt])
            s = jax.ops.segment_sum(p, tgt, num_segments=n)
            w = p / (s[tgt] + 1e-16)
            agg = jax.ops.segment_sum(w[:, :, None] * v[srcidx], tgt, num_segments=n)
            attn = agg.reshape(n, D) @ Wo[l].T + bo[l]
            x = _batchnorm(x + attn, g1[l], beta1[l])
            ff = jax.nn.relu(x @ W1[l].T + b1[l]) @ W2[l].T + b2[l]
            x = _batchnorm(x + ff, g2[l], beta2[l])
        return _layernorm(x, ln_g, ln_b)
    edge_index = jnp.stack([src, dst])
    h = jnp.maximum(_layernorm(x, axis=-1), 0.0)
    x = x + _L0_gnn_ref(h, src, dst, edge_attr_20, edge_weight, edge_attr_4, L0_gnn_w_in2f_s, L0_gnn_w_in2f_v, L0_gnn_W1, L0_gnn_b1, L0_gnn_W2, L0_gnn_b2, L0_gnn_w_f2o1_s, L0_gnn_w_f2o1_v, L0_gnn_w_f2o2_s, L0_gnn_w_f2o2_v)
    h = jnp.maximum(_layernorm(x, axis=-1), 0.0)
    x = x + _L1_gnn_ref(h, edge_index, L1_gnn_Wq, L1_gnn_bq, L1_gnn_Wk, L1_gnn_Wv, L1_gnn_Wo, L1_gnn_bo, L1_gnn_W1, L1_gnn_b1, L1_gnn_W2, L1_gnn_b2, L1_gnn_g1, L1_gnn_beta1, L1_gnn_g2, L1_gnn_beta2, L1_gnn_ln_g, L1_gnn_ln_b)
    return x

_drawn_inputs = setup_inputs


def setup_inputs(seed=0):
    import zlib

    import numpy as np

    out = dict(_drawn_inputs(seed))
    spreads = {'L0_gnn_b1': (0.0, 0.383),
     'L0_gnn_b2': (0.0, 0.1),
     'L1_gnn_bq': (0.0, 0.632),
     'L1_gnn_bo': (0.0, 0.8),
     'L1_gnn_b1': (0.0, 0.405),
     'L1_gnn_b2': (0.0, 0.8),
     'L1_gnn_g1': (1.0, 0.2),
     'L1_gnn_beta1': (0.0, 0.284),
     'L1_gnn_g2': (1.0, 0.2),
     'L1_gnn_beta2': (0.0, 0.1),
     'L1_gnn_ln_g': (1.0, 0.2),
     'L1_gnn_ln_b': (0.0, 0.1)}
    factors = {}
    for name, (base, spread) in spreads.items():
        noise = np.random.default_rng([zlib.crc32(name.encode()), seed]).standard_normal(out[name].shape)
        drawn = base * np.exp(spread * noise) if base else spread * noise
        out[name] = jnp.asarray(drawn.astype(out[name].dtype))
    for name, factor in factors.items():
        out[name] = (out[name] * factor).astype(out[name].dtype)
    return out
```

```python
import math
from contextlib import ExitStack

import concourse.bass as bass
from concourse import mybir

F32 = mybir.dt.float32
F32R = mybir.dt.float32r
I32 = mybir.dt.int32
ALU = mybir.AluOpType
ACT = mybir.ActivationFunctionType
AXIS = mybir.AxisListType

N = 10000
E = 10000
D = 512
PARTS = 125
TILES = N // PARTS
GROUP = 4
GROUPS = TILES // GROUP
KC = D // 128
WIDE = 112
ROWS_DMA = 32
B = 128
F = 32
R = 20
MSG = 4 * F
AGG = 8 * F
HEADS = 8
HD = D // HEADS
LAYERS = 2
FF = 64
LN_EPS = 1e-5
BN_EPS = 1e-5
LOG2 = 0.6931471805599453
FAR = 16384.0
NEG = -1e30
ds = bass.ds


def rows_dma(engine, out, in_, sem):
    engine.dma_start(out[0:WIDE], in_[0:WIDE]).then_inc(sem, 16)
    engine.dma_start(out[WIDE:PARTS], in_[WIDE:PARTS]).then_inc(sem, 16)


class Chip:

    def __init__(self, nc, ctx):
        self.nc, self.ctx, self.sems, self.counts, self.tensors = nc, ctx, {}, {}, 0

    def sem(self, name):
        if name not in self.sems:
            self.sems[name] = self.ctx.enter_context(self.nc.semaphore(name))
        return self.sems[name]

    def sem2(self, name):
        return [self.sem(f"{name}_0"), self.sem(f"{name}_1")]

    def unique(self, name):
        self.tensors += 1
        return f"{name}_{self.tensors}"

    def counted(self, name, n):
        before = self.counts.get(name, 0)
        self.counts[name] = before + n
        return self.sem(name), before


def tiles_of(dram):
    return dram.rearrange("(p t) d -> p t d", t=TILES)


def bcast(ap, n):
    a = ap.unsqueeze(len(ap.shape))
    return a.to_broadcast([*ap.shape, n])


def setup(chip, sb, ps, T, W, A):
    nc = chip.nc
    raw_vT = sb("raw_vT", [B, 2, 2 * F])
    raw_o2v = sb("raw_o2v", [B, B])
    psV = ps("psV", 1, [128, B])[0]
    made, loads, weights_in = chip.sem("const_made"), chip.sem("edges_in"), chip.sem("weights_in")
    done, cleared = chip.sem("dve_done"), chip.sem("cleared")
    with nc.Block() as block:

        @block.gpsimd
        def _(pool):
            nc.gpsimd.memset(T.dst_ext[:], -1).then_inc(made, 1)
            pool.wait_ge(made, 1)
            pool.sem_inc(made, -1)
            pool.sem_inc(cleared, 1)
            nc.gpsimd.memset(T.ident[:], 0.0).then_inc(made, 1)
            nc.gpsimd.memset(T.lower[:], 1.0).then_inc(made, 1)
            nc.gpsimd.memset(T.zeros[:, 0:TILES * D // GROUPS], 0.0).then_inc(made, 1)
            nc.gpsimd.memset(T.minus_half[:], -0.5).then_inc(made, 1)
            pool.wait_ge(made, 4)
            pool.sem_inc(made, -4)
            nc.gpsimd.affine_select(out=T.ident[:], in_=T.ident[:], compare_op=ALU.not_equal, fill=1.0,
                                    base=0, pattern=[[-1, 128]], channel_multiplier=1).then_inc(made, 1)
            nc.gpsimd.affine_select(out=T.lower[:], in_=T.lower[:], compare_op=ALU.is_gt, fill=0.0,
                                    base=0, pattern=[[-1, PARTS]], channel_multiplier=1).then_inc(made, 1)
            nc.gpsimd.iota(T.spare_i[:], pattern=[[0, 1]], base=N, channel_multiplier=1).then_inc(made, 1)
            pool.wait_ge(made, 3)
            pool.sem_inc(made, -3)
            nc.gpsimd.tensor_copy(T.spare[:], T.spare_i[:]).then_inc(made, 1)
            pool.wait_ge(made, 1)
            pool.sem_inc(made, -1)

        @block.sync
        def _(sp):
            moves = ((raw_vT[:, 0], A.f2o1_vT), (raw_vT[:, 1], A.f2o1_vT), (raw_o2v[:], A.f2o2_v),
                     (W.in2f[:, 0], A.in2f_s), (W.in2f[:, 1], A.in2f_v), (W.f2o1_s[0:2 * F], A.f2o1_s),
                     (W.f2o2_s[:], A.f2o2_s), (W.w1[:], A.w1), (W.b1[:], A.b1.rearrange("(f a) -> f a", a=1)),
                     (W.w2[0:F], A.w2), (W.w2[F:F + 1], A.b2.unsqueeze(0)))
            for out, in_ in moves:
                sp.dma_start(out, in_).then_inc(weights_in, 16)
            sp.wait_ge(cleared, 1)
            sp.sem_inc(cleared, -1)
            moves2 = ((T.src_i[:], A.src.rearrange("(p t) -> p t", t=TILES)),
                      (T.dst_ext[:, 1:TILES + 1], A.dst.rearrange("(p t) -> p t", t=TILES)),
                      (T.dst_ext[1:PARTS, 0:1], A.dst_tiled[TILES - 1:TILES, 0:PARTS - 1].rearrange("t p -> p t")),
                      (T.dst_ext[0:PARTS - 1, TILES + 1:TILES + 2], A.dst_tiled[0:1, 1:PARTS].rearrange("t p -> p t")),
                      (T.ends_i[:, 0], A.dst_tiled[0:1, :].to_broadcast([HEADS, PARTS])),
                      (T.ends_i[:, 1], A.dst_tiled[TILES - 1:TILES, :].to_broadcast([HEADS, PARTS])),
                      (T.rcut[:], A.rcut.rearrange("(p t) -> p t", t=TILES)),
                      (T.y[:], A.y.rearrange("(p t) c -> p t c", t=TILES)),
                      (T.srcq_i[:].rearrange("p t q -> p (t q)"), A.src_tiled.unsqueeze(0).to_broadcast([PARTS, E])))
            for out, in_ in moves2:
                sp.dma_start(out, in_).then_inc(loads, 16)
            sp.wait_ge(loads, 16 * len(moves2))
            sp.sem_inc(loads, -(16 * len(moves2)))

        @block.tensor
        def _(pe):
            pe.wait_ge(weights_in, 16 * 11)
            nc.tensor.matmul(psV[:], raw_vT[:].rearrange("k a m -> k (a m)"), raw_o2v[:], start=True, stop=True)\
                .then_inc(chip.sem("psV_ready"), 1)

        @block.vector
        def _(dve):
            nc.vector.memset(W.vec[:], 0.0).then_inc(done, 1)
            nc.vector.memset(W.f2o1_s[2 * F:128], 0.0).then_inc(done, 1)
            dve.wait_ge(done, 2)
            dve.sem_inc(done, -2)
            dve.wait_ge(weights_in, 16 * 11)
            root = 1.0 / math.sqrt(B)
            nc.vector.tensor_scalar(W.in2f[:], W.in2f[:], root, None, ALU.mult).then_inc(done, 1)
            nc.vector.tensor_scalar(W.f2o2_s[:], W.f2o2_s[:], root, None, ALU.mult).then_inc(done, 1)
            nc.vector.tensor_scalar(W.f2o1_s[0:2 * F], W.f2o1_s[0:2 * F], 1.0 / math.sqrt(2 * F), None, ALU.mult)\
                .then_inc(done, 1)
            dve.wait_ge(chip.sem("psV_ready"), 1)
            dve.sem_inc(chip.sem("psV_ready"), -1)
            for half in range(2):
                rows = slice(64 * half, 64 * half + 64)
                nc.vector.tensor_scalar(W.vec[rows, half], psV[rows], root / math.sqrt(2 * F), None, ALU.mult)\
                    .then_inc(done, 1)
            dve.wait_ge(done, 5)
            dve.sem_inc(done, -5)


def layernorm_stats(chip, dve, tile_of, stats, mv, var_ready):
    nc, done = chip.nc, chip.sem("dve_done")
    for j in range(GROUP):
        nc.vector.bn_stats(out=stats[:, j], in_=tile_of(j)).then_inc(done, 1)
    dve.wait_ge(done, GROUP)
    dve.sem_inc(done, -GROUP)
    for j in range(GROUP):
        nc.vector.bn_aggr(out=mv[:, j], in_=stats[:, j]).then_inc(done, 1)
    dve.wait_ge(done, GROUP)
    dve.sem_inc(done, -GROUP)
    dve.sem_inc(var_ready, 1)


def layernorm_scales(chip, pool, T, mv, rstd, shift, var_ready, normed):
    nc, done = chip.nc, chip.sem("pool_done")
    pool.wait_ge(var_ready, 1)
    pool.sem_inc(var_ready, -1)
    nc.gpsimd.tensor_scalar(rstd, mv[:, :, 1], LN_EPS, None, ALU.add).then_inc(done, 1)
    nc.gpsimd.tensor_scalar(shift, mv[:, :, 0], -1.0, None, ALU.mult).then_inc(done, 1)
    pool.wait_ge(done, 2)
    pool.sem_inc(done, -2)
    nc.gpsimd.tensor_tensor(rstd, rstd, T.minus_half[0:PARTS, 0:1].to_broadcast([PARTS, GROUP]), ALU.pow).then_inc(done, 1)
    pool.wait_ge(done, 1)
    pool.sem_inc(done, -1)
    nc.gpsimd.tensor_tensor(shift, shift, rstd, ALU.mult).then_inc(normed, 1)


def l0_node_messages(chip, sb, ps, x, T, W):
    nc = chip.nc
    xin = sb("xin", [PARTS, 2, GROUP, D])
    stats = sb("stats", [PARTS, GROUP, 6])
    mv = sb("mv", [PARTS, 2, GROUP, 2])
    rstd, shift = sb("rstd", [PARTS, 2, GROUP]), sb("shift", [PARTS, 2, GROUP])
    h = sb("h", [PARTS, 2, D])
    hT = sb("hT", [128, 2, KC, PARTS])
    stage = sb("stage", [PARTS, 2, GROUP, MSG])
    psT = ps("psT", 2, [128, KC, PARTS])
    psM = ps("psM", 2, [128, 4, F])
    loaded, x_free, stored = chip.sem2("x_loaded"), chip.sem2("x_free"), chip.sem2("stored")
    stage_ready = chip.sem2("stage_ready")
    normed, h_ready, psT_ready = chip.sem("normed"), chip.sem("h_ready"), chip.sem("psT_ready")
    hT_ready, hT_free, psM_ready, psM_free = (chip.sem(n) for n in ("hT_ready", "hT_free", "psM_ready", "psM_free"))
    done, var_ready = chip.sem("dve_done"), chip.sem("var_ready")
    xt, table = tiles_of(x), tiles_of(T.messages)

    with nc.Block() as block:

        @block.sync
        def _(sp):
            def load(g, b):
                sp.wait_ge(x_free[b], 1)
                sp.sem_inc(x_free[b], -1)
                rows_dma(sp, xin[:, b], xt[:, ds(g * GROUP, GROUP)], loaded[b])

            def store(g, b):
                sp.wait_ge(stage_ready[b], 1)
                sp.sem_inc(stage_ready[b], -1)
                rows_dma(sp, table[:, ds(g * GROUP, GROUP)], stage[:, b], stored[b])

            def zero(g):
                for zt, cols in tables:
                    n = TILES * cols // GROUPS
                    rows_dma(sp, zt[0:N, :].rearrange("(p t) d -> p (t d)", t=TILES)[:, ds(g * n, n)],
                             T.zeros[:, 0:n], zeroed)

            tables = ((T.agg_l0[0], AGG), (T.agg_l0[1], AGG), (T.agg, D))
            zeroed = chip.sem("zeroed")
            for b in range(2):
                sp.sem_inc(x_free[b], 1)
                sp.sem_inc(stored[b], ROWS_DMA)
                load(b, b)
            with sp.Fori(0, GROUPS // 2 - 1) as i:
                for b in range(2):
                    zero(i * 2 + b)
                    store(i * 2 + b, b)
                    load(i * 2 + 2 + b, b)
            for b in range(2):
                zero(GROUPS - 2 + b)
                store(GROUPS - 2 + b, b)
            for zt, cols in tables:
                rows_dma(sp, zt[N:N + PARTS, :], T.zeros[:, 0:cols], zeroed)
            sp.wait_ge(zeroed, (GROUPS + 1) * len(tables) * ROWS_DMA)
            sp.sem_inc(zeroed, -((GROUPS + 1) * len(tables) * ROWS_DMA))
            for b in range(2):
                sp.wait_ge(x_free[b], 1)
                sp.sem_inc(x_free[b], -1)
                sp.wait_ge(stored[b], ROWS_DMA)
                sp.sem_inc(stored[b], -ROWS_DMA)

        @block.vector
        def _(dve):
            nc.vector.tensor_tensor(T.same_src[:], T.srcq_i[:], bcast(T.src_i[:], PARTS), ALU.is_equal)\
                .then_inc(chip.sem("same_src_made"), 1)
            dve.sem_inc(hT_free, 2)
            dve.sem_inc(psM_free, 2)
            with dve.Fori(0, GROUPS // 2) as i:
                for b in range(2):
                    dve.wait_ge(loaded[b], ROWS_DMA)
                    dve.sem_inc(loaded[b], -ROWS_DMA)
                    layernorm_stats(chip, dve, lambda j: xin[:, b, j], stats, mv[:, b], var_ready)
                    dve.wait_ge(stored[b], ROWS_DMA)
                    dve.sem_inc(stored[b], -ROWS_DMA)
                    for j in range(GROUP):
                        dve.wait_ge(psM_ready, 1)
                        dve.sem_inc(psM_ready, -1)
                        dve.sem_inc(hT_free, 1)
                        nc.vector.tensor_copy(stage[:, b, j], psM[j % 2][0:PARTS].rearrange("p a f -> p (a f)")).then_inc(done, 1)
                        dve.wait_ge(done, 1)
                        dve.sem_inc(done, -1)
                        dve.sem_inc(psM_free, 1)
                    dve.sem_inc(stage_ready[b], 1)
            dve.wait_ge(hT_free, 2)
            dve.sem_inc(hT_free, -2)
            dve.wait_ge(psM_free, 2)
            dve.sem_inc(psM_free, -2)

        @block.scalar
        def _(act):
            with act.Fori(0, GROUPS // 2) as i:
                for b in range(2):
                    act.wait_ge(normed, 1)
                    act.sem_inc(normed, -1)

                    def relu(j):
                        nc.scalar.activation(h[:, j % 2], xin[:, b, j], ACT.Relu, bias=shift[:, b, j:j + 1],
                                             scale=rstd[:, b, j:j + 1]).then_inc(h_ready, 1)
                    relu(0)
                    for j in range(GROUP):
                        if j + 1 < GROUP:
                            relu(j + 1)
                        act.wait_ge(psT_ready, 1)
                        act.sem_inc(psT_ready, -1)
                        act.wait_ge(hT_free, 1)
                        act.sem_inc(hT_free, -1)
                        nc.scalar.activation(hT[:, j % 2], psT[j % 2][:], ACT.Copy).then_inc(hT_ready, 1)

        @block.tensor
        def _(pe):
            with pe.Fori(0, GROUPS // 2) as i:
                for b in range(2):
                    def transpose(j):
                        pe.wait_ge(h_ready, 1)
                        pe.sem_inc(h_ready, -1)
                        if j == GROUP - 1:
                            pe.sem_inc(x_free[b], 1)
                        vectors = h[:, j % 2, B:D].rearrange("p (b c) -> p c b", c=3)
                        for c in range(4):
                            last = nc.tensor.transpose(psT[j % 2][:, c], h[:, j % 2, 0:B] if c == 0 else vectors[:, c - 1],
                                                       T.ident[0:PARTS, 0:PARTS])
                        last.then_inc(psT_ready, 1)

                    transpose(0)
                    for j in range(GROUP):
                        if j + 1 < GROUP:
                            transpose(j + 1)
                        pe.wait_ge(hT_ready, 1)
                        pe.sem_inc(hT_ready, -1)
                        pe.wait_ge(psM_free, 1)
                        pe.sem_inc(psM_free, -1)
                        for c in range(4):
                            last = nc.tensor.matmul(psM[j % 2][0:PARTS, c], hT[:, j % 2, c], W.in2f[:, min(c, 1)],
                                                    start=True, stop=True)
                        last.then_inc(psM_ready, 1)

        @block.gpsimd
        def _(pool):
            pooled = chip.sem("pool_done")
            for to, from_ in ((T.src_f, T.src_i), (T.dst_f, T.dst_ext)):
                nc.gpsimd.tensor_copy(to[:], from_[:]).then_inc(pooled, 1)
            pool.wait_ge(pooled, 2)
            pool.sem_inc(pooled, -2)
            pool.wait_ge(chip.sem("same_src_made"), 1)
            pool.sem_inc(chip.sem("same_src_made"), -1)
            nc.gpsimd.tensor_tensor(T.earlier[:], T.same_src[:],
                                    T.lower[:].unsqueeze(1).to_broadcast([PARTS, TILES, PARTS]), ALU.mult).then_inc(pooled, 1)
            pool.wait_ge(pooled, 1)
            pool.sem_inc(pooled, -1)
            pool.sem_inc(chip.sem("dups_marked"), 1)
            with pool.Fori(0, GROUPS // 2) as i:
                for b in range(2):
                    layernorm_scales(chip, pool, T, mv[:, b], rstd[:, b], shift[:, b], var_ready, normed)
    with nc.Block() as block:

        @block.vector
        def _(dve):
            dve.wait_ge(chip.sem("dups_marked"), 1)
            dve.sem_inc(chip.sem("dups_marked"), -1)
            nc.vector.tensor_reduce(T.dup[:], T.earlier[:], AXIS.X, ALU.add).then_inc(done, 1)
            dve.wait_ge(done, 1)
            dve.sem_inc(done, -1)
            nc.vector.tensor_scalar(T.dup[:], T.dup[:], 1.0, None, ALU.min).then_inc(done, 1)
            nc.vector.tensor_scalar(T.tmp80[:], T.src_f[:], -1.0, T.spare[:, 0:1], ALU.mult, ALU.add).then_inc(done, 1)
            dve.wait_ge(done, 2)
            dve.sem_inc(done, -2)
            nc.vector.tensor_tensor(T.tmp80[:], T.tmp80[:], T.dup[:], ALU.mult).then_inc(done, 1)
            dve.wait_ge(done, 1)
            dve.sem_inc(done, -1)
            nc.vector.tensor_tensor(T.tmp80[:], T.tmp80[:], T.src_f[:], ALU.add).then_inc(done, 1)
            dve.wait_ge(done, 1)
            dve.sem_inc(done, -1)
            nc.vector.tensor_copy(T.scat_i[:], T.tmp80[:]).then_inc(done, 1)
            dve.wait_ge(done, 1)
            dve.sem_inc(done, -1)


def softplus_minus_log2(chip, act, dve, z_in, bias, mag, out, z_ready, mag_free, mag_ready, out_ready, freed):
    nc = chip.nc

    def scalar_half():
        done = chip.sem("act_done")
        act.wait_ge(z_ready, 1)
        act.sem_inc(z_ready, -1)
        act.wait_ge(mag_free, 1)
        act.sem_inc(mag_free, -1)
        nc.scalar.activation(mag, z_in, ACT.Abs, **({} if bias is None else {"bias": bias})).then_inc(done, 1)
        act.wait_ge(done, 1)
        act.sem_inc(done, -1)
        nc.scalar.activation(mag, mag, ACT.Exp, scale=-1.0).then_inc(done, 1)
        act.wait_ge(done, 1)
        act.sem_inc(done, -1)
        nc.scalar.activation(mag, mag, ACT.Ln, bias=1.0).then_inc(mag_ready, 1)

    def vector_half():
        done = chip.sem("dve_done")
        dve.wait_ge(mag_ready, 1)
        dve.sem_inc(mag_ready, -1)
        nc.vector.tensor_scalar(out, z_in, 0.0 if bias is None else bias, 0.0, ALU.add, ALU.max).then_inc(done, 1)
        dve.wait_ge(done, 1)
        dve.sem_inc(done, -1)
        nc.vector.scalar_tensor_tensor(out, mag, -LOG2, out, ALU.add, ALU.add).then_inc(done, 1)
        dve.wait_ge(done, 1)
        dve.sem_inc(done, -1)
        for s in (out_ready, mag_free, *freed):
            dve.sem_inc(s, 1)

    return scalar_half, vector_half


def l0_edges(chip, sb, ps, T, W, edge_radial):
    nc = chip.nc
    msg = sb("msg", [PARTS, 2, GROUP, MSG])
    gather_i = sb("gather_i", [PARTS, 2, GROUP], I32)
    scatter_i = sb("scatter_i", [PARTS, 2, GROUP], I32)
    radial = sb("radial", [R, 2, GROUP * PARTS])
    mag = sb("mag", [F, 2, GROUP * PARTS])
    hidden = sb("hidden", [F + 1, 2, GROUP * PARTS])
    filt = sb("filt", [PARTS, GROUP, 4, F])
    s_filt = sb("s_filt", [PARTS, GROUP, 2, F])
    v_filt = sb("v_filt", [PARTS, GROUP, 3, F])
    v_y = sb("v_y", [PARTS, GROUP, 3, F])
    dot = sb("dot", [PARTS, GROUP, F])
    edge = sb("edge", [PARTS, 2, GROUP, 8, F])
    summed = sb("summed", [PARTS, 2, GROUP, AGG])
    same = sb("same", [PARTS, 2, GROUP, PARTS])
    psH = ps("psH", 2, [F, GROUP * PARTS])
    psW = ps("psW", 2, [128, GROUP, 4 * F])
    psR = ps("psR", 4, [128, 2, AGG])
    done = chip.sem("dve_done")
    names = ("psH_free", "mag_free", "mag_ready", "hidden_ready", "psW_ready", "psW_free", "edge_ready", "edge_free",
             "psR_ready", "psR_free", "msg_free", "summed_ready", "summed_free", "psH_ready", "same_ready")
    s = {n: chip.sem(n) for n in names}
    radial_in, radial_free = chip.sem2("radial_in"), chip.sem2("radial_free")
    msg_in = [chip.counted(f"msg_in_{b}", 0)[0] for b in range(2)]
    added = [chip.counted(f"added_{b}", 0)[0] for b in range(2)]
    seen = chip.sem("seen")
    ones_ready = chip.sem("ones_ready")

    with nc.Block() as block:

        @block.sync
        def _(sp):
            def load(g, b):
                sp.wait_ge(radial_free[b], 1)
                sp.sem_inc(radial_free[b], -1)
                sp.dma_start(radial[:, b], edge_radial[:, ds(g * (GROUP * PARTS), GROUP * PARTS)]).then_inc(radial_in[b], 16)
            for b in range(2):
                sp.sem_inc(radial_free[b], 1)
            with sp.Fori(0, GROUPS // 2) as i:
                for b in range(2):
                    load(i * 2 + b, b)
            for b in range(2):
                sp.wait_ge(radial_free[b], 1)
                sp.sem_inc(radial_free[b], -1)

        @block.tensor
        def _(pe):
            def hidden_of(g, b):
                pe.wait_ge(radial_in[b], 16)
                pe.sem_inc(radial_in[b], -16)
                pe.wait_ge(s["psH_free"], 1)
                pe.sem_inc(s["psH_free"], -1)
                nc.tensor.matmul(psH[b][:], W.w1[:], radial[:, b], start=True, stop=True).then_inc(s["psH_ready"], 1)

            def filters(g, b):
                pe.wait_ge(s["hidden_ready"], 1)
                pe.sem_inc(s["hidden_ready"], -1)
                pe.wait_ge(s["psW_free"], 1)
                pe.sem_inc(s["psW_free"], -1)
                for j in range(GROUP):
                    last = nc.tensor.matmul(psW[b][0:PARTS, j], hidden[:, b, j * PARTS:(j + 1) * PARTS], W.w2[:, 0:4 * F],
                                            start=True, stop=True)
                last.then_inc(s["psW_ready"], 1)

            def sums(g, b):
                pe.wait_ge(s["edge_ready"], 1)
                pe.sem_inc(s["edge_ready"], -1)
                pe.wait_ge(s["same_ready"], 1)
                pe.sem_inc(s["same_ready"], -1)
                pe.wait_ge(s["psR_free"], 1)
                pe.sem_inc(s["psR_free"], -1)
                for j in range(GROUP):
                    last = nc.tensor.matmul(psR[2 * b + j // 2][0:PARTS, j % 2], same[:, b, j],
                                            edge[:, b, j].rearrange("p a f -> p (a f)"), start=True, stop=True)
                last.then_inc(s["psR_ready"], 1)

            pe.wait_ge(ones_ready, 1)
            pe.sem_inc(ones_ready, -1)
            hidden_of(0, 0)
            hidden_of(1, 1)
            filters(0, 0)
            with pe.Fori(0, GROUPS // 2 - 1) as i:
                for b in range(2):
                    hidden_of(i * 2 + b + 2, b)
                    filters(i * 2 + b + 1, 1 - b)
                    sums(i * 2 + b, b)
            filters(GROUPS - 1, 1)
            sums(GROUPS - 2, 0)
            sums(GROUPS - 1, 1)

        def halves(act, dve, b):
            return softplus_minus_log2(chip, act, dve, psH[b][:], W.b1[:, 0:1], mag[:, b], hidden[0:F, b],
                                       s["psH_ready"], s["mag_free"], s["mag_ready"], s["hidden_ready"], [s["psH_free"]])

        @block.scalar
        def _(act):
            act.sem_inc(s["psR_free"], 2)
            act.sem_inc(s["edge_free"], 2)

            def softplus(g, b):
                halves(act, None, b)[0]()
                act.sem_inc(radial_free[b], 1)
                nc.scalar.activation(same[:, b], T.same_src[:, ds(g * GROUP, GROUP)], ACT.Copy).then_inc(s["same_ready"], 1)

            def evacuate(g, b):
                act.wait_ge(s["psR_ready"], 1)
                act.sem_inc(s["psR_ready"], -1)
                act.sem_inc(s["edge_free"], 1)
                act.wait_ge(s["summed_free"], 1)
                act.sem_inc(s["summed_free"], -1)
                adone = chip.sem("act_done")
                for k in range(2):
                    nc.scalar.activation(summed[:, b, 2 * k:2 * k + 2], psR[2 * b + k][0:PARTS], ACT.Copy).then_inc(adone, 1)
                act.wait_ge(adone, 2)
                act.sem_inc(adone, -2)
                act.sem_inc(s["psR_free"], 1)
                act.sem_inc(s["summed_ready"], 1)

            softplus(0, 0)
            with act.Fori(0, GROUPS // 2 - 1) as i:
                for b in range(2):
                    softplus(i * 2 + b + 1, 1 - b)
                    evacuate(i * 2 + b, b)
            softplus(GROUPS - 1, 1)
            evacuate(GROUPS - 2, 0)
            evacuate(GROUPS - 1, 1)
            act.wait_ge(s["psR_free"], 2)
            act.sem_inc(s["psR_free"], -2)
            act.wait_ge(s["summed_free"], 2)
            act.sem_inc(s["summed_free"], -2)

        @block.vector
        def _(dve):
            nc.vector.memset(hidden[F:F + 1], 1.0).then_inc(done, 1)
            dve.wait_ge(done, 1)
            dve.sem_inc(done, -1)
            dve.sem_inc(s["psH_free"], 2)
            dve.sem_inc(s["mag_free"], 2)
            dve.sem_inc(s["psW_free"], 2)
            dve.sem_inc(s["msg_free"], 2)
            dve.sem_inc(ones_ready, 1)

            def half(g, b):
                halves(None, dve, b)[1]()

            def products(g, b, i):
                tiles = ds(g * GROUP, GROUP)
                ys = T.y[:, tiles, 0]
                ys3 = bcast(bcast(ys, 3), F)
                yv = bcast(T.y[:, tiles, 1:4], F)
                rcut = T.rcut[:, tiles]
                dve.wait_ge(s["psW_ready"], 1)
                dve.sem_inc(s["psW_ready"], -1)
                nc.vector.tensor_tensor(filt[:].rearrange("p j k f -> p j (k f)"), psW[b][0:PARTS], bcast(rcut, 4 * F),
                                        ALU.mult).then_inc(done, 1)
                dve.wait_ge(done, 1)
                dve.sem_inc(done, -1)
                dve.sem_inc(s["psW_free"], 1)
                dve.wait_ge(msg_in[b], i * (16 * GROUP) + 16 * GROUP)
                dve.sem_inc(seen, 1)
                m = msg[:, b].rearrange("p j (k f) -> p j k f", k=4)
                scalars = m[:, :, 0:1].to_broadcast([PARTS, GROUP, 2, F])
                nc.vector.tensor_tensor(s_filt[:], scalars, filt[:, :, 0:3:2], ALU.mult).then_inc(done, 1)
                nc.vector.tensor_tensor(v_filt[:], m[:, :, 1:4], filt[:, :, 3:4].to_broadcast([PARTS, GROUP, 3, F]),
                                        ALU.mult).then_inc(done, 1)
                nc.vector.tensor_tensor(v_y[:], m[:, :, 1:4], yv, ALU.mult).then_inc(done, 1)
                dve.wait_ge(done, 3)
                dve.sem_inc(done, -3)
                dve.sem_inc(s["msg_free"], 1)
                dve.wait_ge(s["edge_free"], 1)
                dve.sem_inc(s["edge_free"], -1)
                out = edge[:, b]
                nc.vector.tensor_tensor(out[:, :, 0], s_filt[:, :, 0], bcast(ys, F), ALU.mult).then_inc(done, 1)
                nc.vector.tensor_tensor(out[:, :, 2:8:2], s_filt[:, :, 1:2].to_broadcast([PARTS, GROUP, 3, F]), yv,
                                        ALU.mult).then_inc(done, 1)
                nc.vector.tensor_tensor(out[:, :, 3:8:2], v_filt[:], ys3, ALU.mult).then_inc(done, 1)
                nc.vector.tensor_reduce(dot[:], v_y[:].rearrange("p j c f -> p j f c"), AXIS.X, ALU.add).then_inc(done, 1)
                dve.wait_ge(done, 4)
                dve.sem_inc(done, -4)
                nc.vector.scalar_tensor_tensor(out[:, :, 1], dot[:], 1.0 / math.sqrt(3.0), filt[:, :, 1], ALU.mult,
                                               ALU.mult).then_inc(done, 1)
                dve.wait_ge(done, 1)
                dve.sem_inc(done, -1)
                dve.sem_inc(s["edge_ready"], 1)

            half(0, 0)
            with dve.Fori(0, GROUPS // 2 - 1) as i:
                for b in range(2):
                    half(i * 2 + b + 1, 1 - b)
                    products(i * 2 + b, b, i)
            half(GROUPS - 1, 1)
            for b in range(2):
                products(GROUPS - 2 + b, b, GROUPS // 2 - 1)
            dve.wait_ge(s["psH_free"], 2)
            dve.sem_inc(s["psH_free"], -2)
            dve.wait_ge(s["mag_free"], 2)
            dve.sem_inc(s["mag_free"], -2)
            dve.wait_ge(s["psW_free"], 2)
            dve.sem_inc(s["psW_free"], -2)
            dve.wait_ge(s["edge_free"], 2)
            dve.sem_inc(s["edge_free"], -2)
            dve.wait_ge(s["msg_free"], 2)
            dve.sem_inc(s["msg_free"], -2)

        @block.gpsimd
        def _(pool):
            pooled = chip.sem("pool_done")
            pool.sem_inc(s["summed_free"], 2)

            def gather(g, b):
                pool.wait_ge(s["msg_free"], 1)
                pool.sem_inc(s["msg_free"], -1)
                nc.gpsimd.tensor_copy(gather_i[:, b], T.dst_ext[:, ds(g * GROUP + 1, GROUP)]).then_inc(pooled, 1)
                pool.wait_ge(pooled, 1)
                pool.sem_inc(pooled, -1)
                for j in range(GROUP):
                    nc.gpsimd.indirect_dma_start(out=msg[:, b, j], out_offset=None, in_=T.messages[:, :],
                                                 in_offset=bass.IndirectOffsetOnAxis(ap=gather_i[:, b, j:j + 1], axis=0),
                                                 bounds_check=N - 1).then_inc(msg_in[b], 16)

            def scatter(g, b, first):
                nc.gpsimd.tensor_copy(scatter_i[:, b], T.scat_i[:, ds(g * GROUP, GROUP)]).then_inc(pooled, 1)
                pool.wait_ge(pooled, 1)
                pool.sem_inc(pooled, -1)
                pool.wait_ge(s["summed_ready"], 1)
                pool.sem_inc(s["summed_ready"], -1)
                for j in range(GROUP):
                    if not (first and j < 2):
                        pool.wait_ge(added[j % 2], g * 32 + 16 * (j // 2))
                        pool.sem_inc(seen, 1)
                    if j == 1 and not first:
                        pool.sem_inc(s["summed_free"], 1)
                    nc.gpsimd.indirect_dma_start(out=T.agg_l0[j % 2][:, :],
                                                 out_offset=bass.IndirectOffsetOnAxis(ap=scatter_i[:, b, j:j + 1], axis=0),
                                                 in_=summed[:, b, j], in_offset=None, bounds_check=N + PARTS - 1,
                                                 compute_op=ALU.add).then_inc(added[j % 2], 16)

            gather(0, 0)
            gather(1, 1)
            scatter(0, 0, True)
            with pool.Fori(0, GROUPS // 2 - 1) as i:
                for k, b in enumerate((1, 0)):
                    gather(i * 2 + k + 2, 1 - b)
                    scatter(i * 2 + k + 1, b, False)
            scatter(GROUPS - 1, 1, False)
            for b in range(2):
                pool.wait_ge(added[b], GROUPS * 32)
            pool.sem_inc(s["summed_free"], 1)


def l0_nodes(chip, sb, ps, x, T, W, xT):
    nc = chip.nc
    agg = [sb(f"agg{k}", [PARTS, 2, GROUP, AGG]) for k in range(2)]
    xin = sb("xin_d", [PARTS, 2, GROUP, D])
    aT = sb("aT", [128, 2, GROUP * PARTS])
    mag = sb("mag_d", [128, GROUP * PARTS])
    os1 = sb("os1", [128, GROUP * PARTS])
    stats, mv = sb("stats_d", [PARTS, GROUP, 6]), sb("mv_d", [PARTS, 2, GROUP, 2])
    rstd, shift = sb("rstd_d", [PARTS, 2, GROUP]), sb("shift_d", [PARTS, 2, GROUP])
    h = sb("h_d", [PARTS, 2, D])
    psA = ps("psA", 1, [128, 2, 512])[0]
    psO = ps("psO", 1, [128, GROUP * PARTS])[0]
    psX = ps("psX", 2, [128, 4, B])
    psT = ps("psT_d", 2, [128, KC, PARTS])
    done = chip.sem("dve_done")
    names = ("asum_ready", "psA_ready", "aT_ready", "aT_free", "psO_ready", "mag_free", "mag_ready", "os1_ready",
             "psX_ready", "psX_free", "normed", "h_ready", "psT_ready", "psT_free", "os1_free")
    s = {n: chip.sem(n) for n in names}
    agg_in, agg_free = chip.sem2("agg_in"), chip.sem2("agg_free")
    var_ready = chip.sem("var_ready")
    x_in, x_free, x1_ready, x1_out = (chip.sem2(n) for n in ("x_loaded", "x_free", "x1_ready", "stored"))
    tA, tB, tx, tx1 = (tiles_of(a) for a in (T.agg_l0[0][0:N, :], T.agg_l0[1][0:N, :], x, T.x1))

    with nc.Block() as block:

        @block.sync
        def _(sp):
            def load(g, b):
                sp.wait_ge(agg_free[b], 1)
                sp.sem_inc(agg_free[b], -1)
                rows_dma(sp, agg[0][:, b], tA[:, ds(g * GROUP, GROUP)], agg_in[b])
                rows_dma(sp, agg[1][:, b], tB[:, ds(g * GROUP, GROUP)], agg_in[b])
                sp.wait_ge(x_free[b], 1)
                sp.sem_inc(x_free[b], -1)
                sp.wait_ge(x1_out[b], ROWS_DMA)
                sp.sem_inc(x1_out[b], -ROWS_DMA)
                rows_dma(sp, xin[:, b], tx[:, ds(g * GROUP, GROUP)], x_in[b])

            def store(g, b):
                sp.wait_ge(x1_ready[b], 1)
                sp.sem_inc(x1_ready[b], -1)
                rows_dma(sp, tx1[:, ds(g * GROUP, GROUP)], xin[:, b], x1_out[b])

            for b in range(2):
                sp.sem_inc(agg_free[b], 1)
                sp.sem_inc(x_free[b], 1)
                sp.sem_inc(x1_out[b], ROWS_DMA)
                load(b, b)
            with sp.Fori(0, GROUPS // 2 - 1) as i:
                for b in range(2):
                    store(i * 2 + b, b)
                    load(i * 2 + b + 2, b)
            for b in range(2):
                store(GROUPS - 2 + b, b)
            for b in range(2):
                sp.wait_ge(agg_free[b], 1)
                sp.sem_inc(agg_free[b], -1)
                sp.wait_ge(x_free[b], 1)
                sp.sem_inc(x_free[b], -1)
                sp.wait_ge(x1_out[b], ROWS_DMA)
                sp.sem_inc(x1_out[b], -ROWS_DMA)

        @block.tensor
        def _(pe):
            def out_products(g, b):
                pe.wait_ge(s["os1_ready"], 1)
                pe.sem_inc(s["os1_ready"], -1)
                for j in range(GROUP):
                    cols = slice(j * PARTS, (j + 1) * PARTS)
                    pe.wait_ge(s["psX_free"], 1)
                    pe.sem_inc(s["psX_free"], -1)
                    nc.tensor.matmul(psX[j % 2][0:PARTS, 0], os1[:, cols], W.f2o2_s[:], start=True, stop=True)
                    for c, (half, blk) in enumerate(((1, 0), (0, 1), (1, 1))):
                        last = nc.tensor.matmul(psX[j % 2][0:PARTS, 1 + c], aT[:, blk, cols], W.vec[:, half],
                                                start=True, stop=True)
                    last.then_inc(s["psX_ready"], 1)

            def front(g, b):
                pe.wait_ge(s["asum_ready"], 1)
                pe.sem_inc(s["asum_ready"], -1)
                for blk in range(2):
                    for j in range(GROUP):
                        last = nc.tensor.transpose(psA[:, blk, j * PARTS:(j + 1) * PARTS],
                                                   agg[0][:, b, j, blk * 128:(blk + 1) * 128], T.ident[0:PARTS, 0:PARTS])
                last.then_inc(s["psA_ready"], 1)
                pe.wait_ge(s["aT_ready"], 1)
                pe.sem_inc(s["aT_ready"], -1)
                pe.sem_inc(agg_free[b], 1)
                nc.tensor.matmul(psO[:], W.f2o1_s[:], aT[:, 0], start=True, stop=True).then_inc(s["psO_ready"], 1)

            def h_transposes(g, b):
                for j in range(GROUP):
                    pe.wait_ge(s["h_ready"], 1)
                    pe.sem_inc(s["h_ready"], -1)
                    pe.wait_ge(s["psT_free"], 1)
                    pe.sem_inc(s["psT_free"], -1)
                    for c in range(KC):
                        last = nc.tensor.transpose(psT[j % 2][:, c], h[:, j % 2, c * 128:(c + 1) * 128],
                                                   T.ident[0:PARTS, 0:PARTS])
                    last.then_inc(s["psT_ready"], 1)

            front(0, 0)
            out_products(0, 0)
            front(1, 1)
            with pe.Fori(0, GROUPS // 2 - 1) as i:
                for k, b in enumerate((1, 0)):
                    out_products(i * 2 + 1 + k, b)
                    front(i * 2 + 2 + k, 1 - b)
                    h_transposes(i * 2 + k, 1 - b)
            out_products(GROUPS - 1, 1)
            h_transposes(GROUPS - 2, 0)
            h_transposes(GROUPS - 1, 1)

        def halves(act, dve):
            return softplus_minus_log2(chip, act, dve, psO[:], None, mag[:], os1[:], s["psO_ready"], s["mag_free"],
                                       s["mag_ready"], s["os1_ready"], [])

        @block.scalar
        def _(act):
            act.sem_inc(s["psT_free"], 2)
            adone = chip.sem("act_done")

            def front(g, b):
                act.wait_ge(s["psA_ready"], 1)
                act.sem_inc(s["psA_ready"], -1)
                act.wait_ge(s["aT_free"], 1)
                act.sem_inc(s["aT_free"], -1)
                nc.scalar.activation(aT[:], psA[:, :, 0:GROUP * PARTS], ACT.Copy).then_inc(s["aT_ready"], 1)
                halves(act, None)[0]()

            def back(g, b):
                act.wait_ge(s["normed"], 1)
                act.sem_inc(s["normed"], -1)

                def relu(j):
                    nc.scalar.activation(h[:, j % 2], xin[:, b, j], ACT.Relu, bias=shift[:, b, j:j + 1],
                                         scale=rstd[:, b, j:j + 1]).then_inc(s["h_ready"], 1)
                relu(0)
                for j in range(GROUP):
                    if j + 1 < GROUP:
                        relu(j + 1)
                    act.wait_ge(s["psT_ready"], 1)
                    act.sem_inc(s["psT_ready"], -1)
                    if j == GROUP - 1:
                        act.sem_inc(x_free[b], 1)
                    nc.scalar.activation(xT[:, :, ds((g * GROUP + j) * PARTS, PARTS)], psT[j % 2][:], ACT.Copy)\
                        .then_inc(adone, 1)
                    act.wait_ge(adone, 1)
                    act.sem_inc(adone, -1)
                    act.sem_inc(s["psT_free"], 1)

            front(0, 0)
            front(1, 1)
            with act.Fori(0, GROUPS // 2 - 1) as i:
                for k, b in enumerate((1, 0)):
                    front(i * 2 + 2 + k, 1 - b)
                    back(i * 2 + k, 1 - b)
            back(GROUPS - 2, 0)
            back(GROUPS - 1, 1)
            act.wait_ge(s["psT_free"], 2)
            act.sem_inc(s["psT_free"], -2)

        @block.gpsimd
        def _(pool):
            with pool.Fori(0, GROUPS // 2) as i:
                for b in range(2):
                    layernorm_scales(chip, pool, T, mv[:, b], rstd[:, b], shift[:, b], var_ready, s["normed"])

        @block.vector
        def _(dve):
            dve.sem_inc(s["psX_free"], 2)
            dve.sem_inc(s["mag_free"], 1)
            dve.sem_inc(s["aT_free"], 1)

            def sum_tables(g, b):
                dve.wait_ge(agg_in[b], 2 * ROWS_DMA)
                dve.sem_inc(agg_in[b], -(2 * ROWS_DMA))
                nc.vector.tensor_tensor(agg[0][:, b], agg[0][:, b], agg[1][:, b], ALU.add).then_inc(s["asum_ready"], 1)

            def add_output(g, b):
                dve.wait_ge(x_in[b], ROWS_DMA)
                dve.sem_inc(x_in[b], -ROWS_DMA)
                for j in range(GROUP):
                    dve.wait_ge(s["psX_ready"], 1)
                    dve.sem_inc(s["psX_ready"], -1)
                    if j == GROUP - 1:
                        dve.sem_inc(s["aT_free"], 1)
                    xs, xv = xin[:, b, j, 0:B], xin[:, b, j, B:D].rearrange("p (b c) -> p b c", c=3)
                    out = psX[j % 2][0:PARTS]
                    nc.vector.tensor_tensor(xs, out[:, 0], xs, ALU.add).then_inc(done, 1)
                    nc.vector.tensor_tensor(xv, out[:, 1:4].rearrange("p c b -> p b c"), xv, ALU.add).then_inc(done, 1)
                    dve.wait_ge(done, 2)
                    dve.sem_inc(done, -2)
                    dve.sem_inc(s["psX_free"], 1)
                dve.sem_inc(x1_ready[b], 1)

            def norm(g, b):
                layernorm_stats(chip, dve, lambda j: xin[:, b, j], stats, mv[:, b], var_ready)

            sum_tables(0, 0)
            halves(None, dve)[1]()
            sum_tables(1, 1)
            add_output(0, 0)
            norm(0, 0)
            halves(None, dve)[1]()
            with dve.Fori(0, GROUPS // 2 - 1) as i:
                for k, b in enumerate((1, 0)):
                    g = i * 2 + 1 + k
                    sum_tables(g + 1, 1 - b)
                    add_output(g, b)
                    norm(g, b)
                    halves(None, dve)[1]()
            add_output(GROUPS - 1, 1)
            norm(GROUPS - 1, 1)
            dve.wait_ge(s["psX_free"], 2)
            dve.sem_inc(s["psX_free"], -2)
            dve.wait_ge(s["mag_free"], 1)
            dve.sem_inc(s["mag_free"], -1)
            dve.wait_ge(s["aT_free"], 1)
            dve.sem_inc(s["aT_free"], -1)


def attention_masks(chip, sb, ps, T):
    nc = chip.nc
    alike = sb("alike", [PARTS, TILES + 1])
    ends = sb("ends", [HEADS, 2, PARTS])
    from_before, base, cont_end, ends_here = (sb(n, [PARTS, TILES if k < 2 else 1]) for k, n in
                                              enumerate(("from_before", "base", "cont_end", "ends_here")))
    key, first, fix = sb("key", [PARTS, 1]), sb("first", [PARTS, 1]), sb("fix", [PARTS, 1])
    psF = ps("psF", 1, [128, PARTS])[0]
    done, first_ready = chip.sem("dve_done"), chip.sem("first_ready")

    with nc.Block() as block:

        @block.tensor
        def _(pe):
            pe.wait_ge(first_ready, 1)
            pe.sem_inc(first_ready, -1)
            nc.tensor.matmul(psF[0:PARTS], first[:].to_broadcast([PARTS, PARTS]), T.ident[0:PARTS, 0:PARTS],
                             start=True, stop=True).then_inc(chip.sem("psF_ready"), 1)

        @block.vector
        def _(dve):
            def do(*steps):
                for step in steps:
                    step.then_inc(done, 1)
                dve.wait_ge(done, len(steps))
                dve.sem_inc(done, -(len(steps)))
            tt, ts, stt = nc.vector.tensor_tensor, nc.vector.tensor_scalar, nc.vector.scalar_tensor_tensor
            d = T.dst_f
            last = TILES - 1
            do(tt(alike[:], d[:, 0:TILES + 1], d[:, 1:TILES + 2], ALU.is_equal),
               nc.vector.tensor_copy(ends[:], T.ends_i[:]))
            do(nc.vector.tensor_copy(T.same[:], alike[:, 0:TILES]), nc.vector.tensor_copy(T.same_next[:], alike[:, 1:TILES + 1]),
               nc.vector.tensor_copy(cont_end[:], alike[:, TILES:TILES + 1]))
            do(nc.vector.memset(T.same[:, 0:1], 0.0), nc.vector.memset(T.same_next[:, last:TILES], 0.0))
            do(ts(T.same_neg[:], T.same[:], -NEG, NEG, ALU.mult, ALU.add),
               ts(T.next_neg[:], T.same_next[:], -NEG, NEG, ALU.mult, ALU.add),
               nc.vector.tensor_tensor_scan(from_before[:], alike[:, 0:TILES], alike[:, 0:TILES], 1.0, ALU.mult, ALU.min),
               ts(base[:], d[:, 1:TILES + 1], -1.0, T.spare[:, 0:1], ALU.mult, ALU.add),
               stt(key[:], d[:, TILES:TILES + 1], 1.0, cont_end[:], ALU.add, ALU.mult))
            do(tt(base[:], base[:], from_before[:], ALU.mult), ts(key[:], key[:], -1.0, None, ALU.add),
               tt(ends_here[:], from_before[:, last:TILES], cont_end[:], ALU.mult))
            do(tt(base[:], base[:], d[:, 1:TILES + 1], ALU.add),
               tt(ends_here[:], alike[:, 0:1], ends_here[:], ALU.subtract))
            do(stt(base[:], alike[:, 1:TILES + 1], FAR, base[:], ALU.mult, ALU.add),
               stt(first[:], d[:, 1:2], 2.0, ends_here[:], ALU.add, ALU.mult),
               ts(fix[:], ends_here[:], -FAR, FAR, ALU.mult, ALU.add))
            do(nc.vector.tensor_copy(T.row_i[:], base[:]), ts(first[:], first[:], -2.0, None, ALU.add),
               tt(fix[:], fix[:], d[:, 1:2], ALU.add))
            dve.sem_inc(first_ready, 1)
            do(nc.vector.tensor_copy(T.fix_i[:], fix[:]))
            cont, whole = T.cont, T.whole
            do(nc.vector.memset(cont[:], 0.0))
            do(tt(cont[:, 1:PARTS], ends[:, 1, 0:PARTS - 1], ends[:, 0, 1:PARTS], ALU.is_equal),
               tt(whole[:], ends[:, 0], ends[:, 1], ALU.is_equal))
            do(tt(T.pass_fwd[:], cont[:, 0:PARTS], whole[:], ALU.mult), tt(T.pass_bwd[:], cont[:, 1:PARTS + 1], whole[:], ALU.mult))
            do(ts(T.pass_fwd_neg[:], T.pass_fwd[:], -NEG, NEG, ALU.mult, ALU.add),
               ts(T.pass_bwd_neg[:], T.pass_bwd[:], -NEG, NEG, ALU.mult, ALU.add),
               ts(T.cont_neg[:], cont[:], -NEG, NEG, ALU.mult, ALU.add))
            dve.wait_ge(chip.sem("psF_ready"), 1)
            dve.sem_inc(chip.sem("psF_ready"), -1)
            do(ts(T.carry[:], psF[0:PARTS], key[:, 0:1], None, ALU.is_equal))


def project(chip, sb, ps, T, xT, weight, bias, table, scores):
    nc = chip.nc
    w_high, w_low = sb("w_high", [128, KC, D], F32R), sb("w_low", [128, KC, D], F32R)
    bias_row = None if bias is None else sb("bias_row", [PARTS, D])
    psP = ps("psP", 2, [128, D])
    table_t = tiles_of(table)
    done, adone = chip.sem("dve_done"), chip.sem("act_done")
    names = ("high_done", "split_ready", "split_free", "psP_ready", "psP_free", "w_ready")
    s = {n: chip.sem(n) for n in names}
    row_ready, row_out = chip.sem2("row_ready"), chip.sem2("row_out")

    with ExitStack() as stack:
        raw = stack.enter_context(nc.sbuf_tensor(chip.unique("w_raw"), [128, KC, D], F32))
        with nc.Block() as block:

            @block.sync
            def _(sp):
                sp.dma_start(raw[:], weight.rearrange("(c k) n -> k c n", c=KC)).then_inc(chip.sem("w_in"), 16)
                if bias is not None:
                    sp.dma_start(bias_row[:], bias.unsqueeze(0).to_broadcast([PARTS, D])).then_inc(chip.sem("bias_in"), 16)
                    sp.wait_ge(chip.sem("bias_in"), 16)
                    sp.sem_inc(chip.sem("bias_in"), -16)

            @block.scalar
            def _(act):
                act.wait_ge(chip.sem("w_in"), 16)
                act.sem_inc(chip.sem("w_in"), -16)
                nc.scalar.activation(w_high[:], raw[:], ACT.Copy).then_inc(s["w_ready"], 1)

            @block.vector
            def _(dve):
                dve.wait_ge(s["w_ready"], 1)
                dve.sem_inc(s["w_ready"], -1)
                nc.vector.tensor_tensor(w_low[:], raw[:], w_high[:], ALU.subtract).then_inc(done, 1)
                dve.wait_ge(done, 1)
                dve.sem_inc(done, -1)

    x_high, x_low = sb("x_high", [128, 2, KC, PARTS], F32R), sb("x_low", [128, 2, KC, PARTS], F32R)
    row = sb("row", [PARTS, 2, D])
    if scores is not None:
        on_pool, on_vector_tile, on_vector_end, on_tensor_end, on_scalar_end = scores(chip, sb, ps, T)

    with nc.Block() as block:

        @block.sync
        def _(sp):
            for b in range(2):
                sp.sem_inc(row_out[b], ROWS_DMA)
            with sp.Fori(0, TILES // 2) as i:
                for b in range(2):
                    sp.wait_ge(row_ready[b], 1)
                    sp.sem_inc(row_ready[b], -1)
                    rows_dma(sp, table_t[:, ds(i * 2 + b, 1)].rearrange("p a d -> p (a d)"), row[:, b], row_out[b])
            for b in range(2):
                sp.wait_ge(row_out[b], ROWS_DMA)
                sp.sem_inc(row_out[b], -ROWS_DMA)

        @block.scalar
        def _(act):
            act.sem_inc(s["psP_free"], 2)

            def split(t, b):
                act.wait_ge(s["split_free"], 1)
                act.sem_inc(s["split_free"], -1)
                xs = xT[:, :, ds(t * PARTS, PARTS)]
                nc.scalar.activation(x_high[:, b], xs, ACT.Copy).then_inc(s["high_done"], 1)

            def evacuate(t, b):
                act.wait_ge(s["psP_ready"], 1)
                act.sem_inc(s["psP_ready"], -1)
                act.sem_inc(s["split_free"], 1)
                act.wait_ge(row_out[b], ROWS_DMA)
                act.sem_inc(row_out[b], -ROWS_DMA)
                nc.scalar.activation(row[:, b], psP[b][0:PARTS], ACT.Copy).then_inc(adone, 1)
                act.wait_ge(adone, 1)
                act.sem_inc(adone, -1)
                act.sem_inc(s["psP_free"], 1)
                act.sem_inc(row_ready[b] if bias is None else chip.sem("to_bias"), 1)

            act.sem_inc(s["split_free"], 2)
            split(0, 0)
            split(1, 1)
            with act.Fori(0, TILES // 2 - 1) as i:
                for b in range(2):
                    evacuate(i * 2 + b, b)
                    split(i * 2 + b + 2, b)
            evacuate(TILES - 2, 0)
            evacuate(TILES - 1, 1)
            act.wait_ge(s["psP_free"], 2)
            act.sem_inc(s["psP_free"], -2)
            act.wait_ge(s["split_free"], 2)
            act.sem_inc(s["split_free"], -2)
            if scores is not None:
                on_scalar_end(act)

        @block.gpsimd
        def _(pool):
            if scores is not None:
                on_pool(pool)
            if bias is not None:
                with pool.Fori(0, TILES // 2) as i:
                    for b in range(2):
                        pool.wait_ge(chip.sem("to_bias"), 1)
                        pool.sem_inc(chip.sem("to_bias"), -1)
                        nc.gpsimd.tensor_tensor(row[:, b], row[:, b], bias_row[:], ALU.add).then_inc(row_ready[b], 1)

        @block.vector
        def _(dve):
            def split(t, b):
                dve.wait_ge(s["high_done"], 1)
                dve.sem_inc(s["high_done"], -1)
                xs = xT[:, :, ds(t * PARTS, PARTS)]
                nc.vector.tensor_tensor(x_low[:, b], xs, x_high[:, b], ALU.subtract).then_inc(s["split_ready"], 1)

            with dve.Fori(0, TILES // 2) as i:
                for b in range(2):
                    split(i * 2 + b, b)
                    if scores is not None:
                        on_vector_tile(dve, i, b)
            if scores is not None:
                on_vector_end(dve)

        @block.tensor
        def _(pe):
            with pe.Fori(0, TILES // 2) as i:
                for b in range(2):
                    pe.wait_ge(s["split_ready"], 1)
                    pe.sem_inc(s["split_ready"], -1)
                    pe.wait_ge(s["psP_free"], 1)
                    pe.sem_inc(s["psP_free"], -1)
                    parts = [(x, w, c) for c in range(KC)
                             for x, w in ((x_high, w_high), (x_high, w_low), (x_low, w_high))]
                    for n, (x, w, c) in enumerate(parts):
                        last = nc.tensor.matmul(psP[b][0:PARTS], x[:, b, c], w[:, c], start=n == 0,
                                                stop=n == len(parts) - 1)
                    last.then_inc(s["psP_ready"], 1)
            if scores is not None:
                on_tensor_end(pe)


def scores_and_softmax(chip, sb, ps, T):
    nc = chip.nc
    q, k = sb("q_rows", [PARTS, 2, D]), sb("k_rows", [PARTS, 2, D])
    index = sb("index", [PARTS, 2, 2], I32)
    score = T.weight
    work = [x[:].rearrange("p b d -> p (b d)")[:, 0:HEADS * TILES].rearrange("p (h t) -> p h t", h=HEADS)
            for x in (q, k)]
    edge_cols = sb("edge_cols", [PARTS, 2, HEADS])
    over = T.bn_stats[0:HEADS].rearrange("p m a s -> p (m a s)")[:, 0:6 * PARTS].rearrange("p (n q) -> p n q", n=6)
    psS = ps("psS", 1, [HEADS, 2, PARTS])[0]
    psC = ps("psC", 1, [128, 2, HEADS])[0]
    done = chip.sem("dve_done")
    came, before = zip(*(chip.counted(f"qk_in_{b}", TILES // 2 * 32) for b in range(2)))
    free, seen, pooled = chip.sem("qk_free"), chip.sem("seen"), chip.sem("pool_done")
    cols_ready, psS_ready, rows_ready, psC_ready = (chip.sem(n) for n in ("cols_ready", "psS_ready", "rows_ready", "psC_ready"))

    def on_pool(pool):
        pool.sem_inc(free, 2)
        with pool.Fori(0, TILES // 2) as i:
            for b in range(2):
                pool.wait_ge(free, 1)
                pool.sem_inc(free, -1)
                nc.gpsimd.tensor_copy(index[:, b, 0:1], T.dst_ext[:, ds(i * 2 + b + 1, 1)]).then_inc(pooled, 1)
                nc.gpsimd.tensor_copy(index[:, b, 1:2], T.src_i[:, ds(i * 2 + b, 1)]).then_inc(pooled, 1)
                pool.wait_ge(pooled, 2)
                pool.sem_inc(pooled, -2)
                for n, (rows, table) in enumerate(((q, T.q), (k, T.k))):
                    nc.gpsimd.indirect_dma_start(out=rows[:, b], out_offset=None, in_=table[:, :],
                                                 in_offset=bass.IndirectOffsetOnAxis(ap=index[:, b, n:n + 1], axis=0),
                                                 bounds_check=N - 1).then_inc(came[b], 16)
        pool.wait_ge(free, 2)
        pool.sem_inc(free, -2)

    def on_vector_tile(dve, i, b):
        dve.wait_ge(came[b], i * 32 + (before[b] + 32))
        dve.sem_inc(seen, 1)
        nc.vector.tensor_tensor(q[:, b], q[:, b], k[:, b], ALU.mult).then_inc(done, 1)
        dve.wait_ge(done, 1)
        dve.sem_inc(done, -1)
        nc.vector.tensor_reduce(score[:, :, ds(i * 2 + b, 1)].rearrange("p h a -> p (h a)"),
                                q[:, b].rearrange("p (h d) -> p h d", h=HEADS), AXIS.X, ALU.add).then_inc(done, 1)
        dve.wait_ge(done, 1)
        dve.sem_inc(done, -1)
        dve.sem_inc(free, 1)

    def scan(out, mask, data, op0, op1, backward=False):
        way = slice(None, None, -1) if backward else slice(None)
        return [nc.vector.tensor_tensor_scan(out[:, h, way], mask[:, way], data[:, h, way], 0.0, op0, op1)
                for h in range(HEADS)]

    def on_vector_end(dve):
        def do(*steps):
            for step in steps:
                step.then_inc(done, 1)
            dve.wait_ge(done, len(steps))
            dve.sem_inc(done, -(len(steps)))
        tt, ts, copy = nc.vector.tensor_tensor, nc.vector.tensor_scalar, nc.vector.tensor_copy
        last = TILES - 1
        a, m = work
        do(ts(score[:], score[:], float(HD) ** -0.5, None, ALU.mult))

        def across(first, last_col, maximum):
            do(copy(edge_cols[:, 0], last_col), copy(edge_cols[:, 1], first))
            dve.sem_inc(cols_ready, 1)
            dve.wait_ge(psS_ready, 1)
            dve.sem_inc(psS_ready, -1)
            do(copy(over[:, 0:2], psS[:]))
            if maximum:
                fwd, bwd, op = T.pass_fwd_neg, T.pass_bwd_neg, (ALU.add, ALU.max)
            else:
                fwd, bwd, op = T.pass_fwd, T.pass_bwd, (ALU.mult, ALU.add)
            back = op if maximum else (ALU.mult, ALU.max)
            do(nc.vector.tensor_tensor_scan(over[:, 2], fwd[:], over[:, 0], 0.0, *op),
               nc.vector.tensor_tensor_scan(over[:, 3, ::-1], bwd[:, ::-1], over[:, 1, ::-1], 0.0, *back),
               nc.vector.memset(over[:, 4:6], NEG if maximum else 0.0))
            cont, use = (T.cont_neg, ALU.add) if maximum else (T.cont, ALU.mult)
            do(tt(over[:, 4, 1:PARTS], over[:, 2, 0:PARTS - 1], cont[:, 1:PARTS], use),
               tt(over[:, 5, 0:PARTS - 1], over[:, 3, 1:PARTS], cont[:, 1:PARTS], use))
            dve.sem_inc(rows_ready, 1)
            dve.wait_ge(psC_ready, 1)
            dve.sem_inc(psC_ready, -1)

        do(*scan(a, T.same_neg, score, ALU.add, ALU.max), *scan(m, T.next_neg, score, ALU.add, ALU.max, True))
        across(m[:, :, 0], a[:, :, last], True)
        do(copy(a, score[:]))
        do(tt(a[:, :, 0], psC[0:PARTS, 0], a[:, :, 0], ALU.max))
        do(tt(a[:, :, last], psC[0:PARTS, 1], a[:, :, last], ALU.max))
        do(*scan(m, T.same_neg, a, ALU.add, ALU.max))
        do(*scan(a, T.next_neg, m, ALU.add, ALU.max, True))
        do(tt(score[:], score[:], a, ALU.subtract))
        dve.sem_inc(chip.sem("shifted"), 1)
        dve.wait_ge(chip.sem("exp_ready"), 1)
        dve.sem_inc(chip.sem("exp_ready"), -1)
        do(*scan(a, T.same, score, ALU.mult, ALU.add))
        across(a[:, :, 0], a[:, :, last], False)
        do(copy(m, score[:]))
        do(tt(m[:, :, 0], psC[0:PARTS, 0], m[:, :, 0], ALU.add))
        do(*scan(a, T.same, m, ALU.mult, ALU.add))
        do(*scan(m, T.same_next, a, ALU.mult, ALU.max, True))
        across(m[:, :, 0], a[:, :, last], False)
        do(tt(a[:, :, last], psC[0:PARTS, 1], a[:, :, last], ALU.max))
        do(*scan(m, T.same_next, a, ALU.mult, ALU.max, True))
        do(ts(m, m, 1e-16, None, ALU.add))
        do(nc.vector.reciprocal(m, m))
        do(tt(score[:], score[:], m, ALU.mult))

    def on_tensor_end(pe):
        for _ in range(3):
            pe.wait_ge(cols_ready, 1)
            pe.sem_inc(cols_ready, -1)
            for n in range(2):
                t = nc.tensor.transpose(psS[:, n], edge_cols[:, n], T.ident[0:PARTS, 0:PARTS])
            t.then_inc(psS_ready, 1)
            pe.wait_ge(rows_ready, 1)
            pe.sem_inc(rows_ready, -1)
            for n in range(2):
                t = nc.tensor.transpose(psC[0:PARTS, n], over[:, 4 + n], T.ident[0:HEADS, 0:HEADS])
            t.then_inc(psC_ready, 1)

    def on_scalar_end(act):
        act.wait_ge(chip.sem("shifted"), 1)
        act.sem_inc(chip.sem("shifted"), -1)
        nc.scalar.activation(score[:], score[:], ACT.Exp).then_inc(chip.sem("exp_ready"), 1)

    return on_pool, on_vector_tile, on_vector_end, on_tensor_end, on_scalar_end


def aggregate(chip, sb, ps, T):
    nc = chip.nc
    v, weighted, acc = sb("v_rows", [PARTS, 2, D]), sb("weighted", [PARTS, D]), sb("acc", [PARTS, 2, D])
    v_index, row_index = sb("v_index", [PARTS, 2, 1], I32), sb("row_index", [PARTS, 2, 1], I32)
    psF = ps("psFix", 1, [128, D])[0]
    done, pooled, seen = chip.sem("dve_done"), chip.sem("pool_done"), chip.sem("seen")
    v_in, v_before = zip(*(chip.counted(f"v_in_{b}", TILES // 2 * 16) for b in range(2)))
    out, out_before = zip(*(chip.counted(f"acc_out_{b}", TILES // 2 * 16) for b in range(2)))
    fixed, fixed_before = chip.counted("fixed", 16)
    v_free, acc_ready, acc_free = chip.sem("v_free"), chip.sem("acc_ready"), chip.sem("acc_free")

    with nc.Block() as block:

        @block.gpsimd
        def _(pool):
            pool.sem_inc(acc_free, 2)

            def gather(t, b):
                pool.wait_ge(v_free, 1)
                pool.sem_inc(v_free, -1)
                nc.gpsimd.tensor_copy(v_index[:, b], T.src_i[:, ds(t, 1)]).then_inc(pooled, 1)
                pool.wait_ge(pooled, 1)
                pool.sem_inc(pooled, -1)
                nc.gpsimd.indirect_dma_start(out=v[:, b], out_offset=None, in_=T.v[:, :],
                                             in_offset=bass.IndirectOffsetOnAxis(ap=v_index[:, b], axis=0),
                                             bounds_check=N - 1).then_inc(v_in[b], 16)

            def scatter(t, b, before_it):
                pool.wait_ge(acc_ready, 1)
                pool.sem_inc(acc_ready, -1)
                nc.gpsimd.tensor_copy(row_index[:, b], T.row_i[:, ds(t, 1)]).then_inc(pooled, 1)
                pool.wait_ge(pooled, 1)
                pool.sem_inc(pooled, -1)
                nc.gpsimd.indirect_dma_start(out=T.agg[:, :], out_offset=bass.IndirectOffsetOnAxis(ap=row_index[:, b], axis=0),
                                             in_=acc[:, b], in_offset=None, bounds_check=N + PARTS - 1,
                                             oob_is_err=False).then_inc(out[b], 16)
                if before_it is not None:
                    pool.wait_ge(out[1 - b], before_it)
                    pool.sem_inc(acc_free, 1)

            gather(0, 0)
            gather(1, 1)
            scatter(0, 0, None)
            with pool.Fori(0, TILES // 2 - 1) as i:
                gather(i * 2 + 2, 0)
                scatter(i * 2 + 1, 1, i * 16 + (out_before[0] + 16))
                gather(i * 2 + 3, 1)
                scatter(i * 2 + 2, 0, i * 16 + (out_before[1] + 16))
            scatter(TILES - 1, 1, out_before[0] + TILES // 2 * 16)
            pool.wait_ge(out[1], out_before[1] + TILES // 2 * 16)
            pool.sem_inc(acc_free, 1)
            pool.wait_ge(v_free, 2)
            pool.sem_inc(v_free, -2)
            pool.sem_inc(chip.sem("rows_out"), 1)
            pool.wait_ge(chip.sem("fix_ready"), 1)
            pool.sem_inc(chip.sem("fix_ready"), -1)
            nc.gpsimd.indirect_dma_start(out=T.agg[:, :], out_offset=bass.IndirectOffsetOnAxis(ap=T.fix_i[:, 0:1], axis=0),
                                         in_=weighted[:], in_offset=None, bounds_check=N - 1,
                                         oob_is_err=False).then_inc(fixed, 16)
            pool.wait_ge(fixed, fixed_before + 16)
            pool.sem_inc(seen, 1)

        @block.vector
        def _(dve):
            nc.vector.memset(acc[:, 1], 0.0).then_inc(done, 1)
            dve.wait_ge(done, 1)
            dve.sem_inc(done, -1)
            dve.sem_inc(v_free, 2)
            with dve.Fori(0, TILES // 2) as i:
                for b in range(2):
                    t = ds(i * 2 + b, 1)
                    dve.wait_ge(v_in[b], i * 16 + (v_before[b] + 16))
                    dve.sem_inc(seen, 1)
                    w = T.weight[:, :, t].to_broadcast([PARTS, HEADS, HD])
                    nc.vector.tensor_tensor(weighted[:].rearrange("p (h d) -> p h d", h=HEADS),
                                            v[:, b].rearrange("p (h d) -> p h d", h=HEADS), w, ALU.mult).then_inc(done, 1)
                    dve.wait_ge(done, 1)
                    dve.sem_inc(done, -1)
                    dve.sem_inc(v_free, 1)
                    dve.wait_ge(acc_free, 1)
                    dve.sem_inc(acc_free, -1)
                    nc.vector.scalar_tensor_tensor(acc[:, b], acc[:, 1 - b], T.same[:, t], weighted[:], ALU.mult,
                                                   ALU.add).then_inc(done, 1)
                    dve.wait_ge(done, 1)
                    dve.sem_inc(done, -1)
                    dve.sem_inc(acc_ready, 1)
            dve.wait_ge(acc_free, 2)
            dve.sem_inc(acc_free, -2)
            dve.sem_inc(chip.sem("last_acc"), 1)
            dve.wait_ge(chip.sem("side_in"), ROWS_DMA)
            dve.sem_inc(chip.sem("side_in"), -ROWS_DMA)
            dve.wait_ge(chip.sem("psFix_ready"), 1)
            dve.sem_inc(chip.sem("psFix_ready"), -1)
            nc.vector.tensor_tensor(weighted[:], psF[0:PARTS], v[:, 0], ALU.add).then_inc(chip.sem("fix_ready"), 1)

        @block.sync
        def _(sp):
            sp.wait_ge(chip.sem("rows_out"), 1)
            sp.sem_inc(chip.sem("rows_out"), -1)
            rows_dma(sp, v[:, 0], T.agg[N:N + PARTS, :], chip.sem("side_in"))

        @block.tensor
        def _(pe):
            pe.wait_ge(chip.sem("last_acc"), 1)
            pe.sem_inc(chip.sem("last_acc"), -1)
            nc.tensor.matmul(psF[0:PARTS], T.carry[:], acc[:, 1], start=True, stop=True).then_inc(chip.sem("psFix_ready"), 1)


HALF = 2
HCOLS = HALF * PARTS
HSTEPS = TILES // HALF


def output_projection(chip, sb, ps, T, xT, weight, bias):
    nc = chip.nc
    w_high, w_low = sb("wo_high", [128, KC, D], F32R), sb("wo_low", [128, KC, D], F32R)
    bias_col = sb("bo_col", [128, KC])
    psT, psY = ps("psT_o", 4, [128, 2, HCOLS]), ps("psY", 4, [128, 2, HCOLS])
    agg_t = tiles_of(T.agg[0:N, :])
    done, adone = chip.sem("dve_done"), chip.sem("act_done")
    rows_in, rows_free = chip.sem2("rows_in"), chip.sem2("rows_free")
    names = ("psT_ready", "psT_free", "high_done", "split_ready", "split_free", "psY_ready", "psY_free", "w_ready")
    s = {n: chip.sem(n) for n in names}

    with ExitStack() as stack:
        raw = stack.enter_context(nc.sbuf_tensor(chip.unique("wo_raw"), [128, KC, D], F32))
        with nc.Block() as block:

            @block.sync
            def _(sp):
                sp.dma_start(raw[:], weight.rearrange("(c k) n -> k c n", c=KC)).then_inc(chip.sem("w_in"), 16)
                sp.dma_start(bias_col[:], bias).then_inc(chip.sem("bias_in"), 16)
                sp.wait_ge(chip.sem("bias_in"), 16)
                sp.sem_inc(chip.sem("bias_in"), -16)

            @block.scalar
            def _(act):
                act.wait_ge(chip.sem("w_in"), 16)
                act.sem_inc(chip.sem("w_in"), -16)
                nc.scalar.activation(w_high[:], raw[:], ACT.Copy).then_inc(s["w_ready"], 1)

            @block.vector
            def _(dve):
                dve.wait_ge(s["w_ready"], 1)
                dve.sem_inc(s["w_ready"], -1)
                nc.vector.tensor_tensor(w_low[:], raw[:], w_high[:], ALU.subtract).then_inc(done, 1)
                dve.wait_ge(done, 1)
                dve.sem_inc(done, -1)

    rows = sb("agg_rows", [PARTS, HALF, D])
    a_high, a_low = sb("a_high", [128, 2, KC, HCOLS], F32R), sb("a_low", [128, 2, KC, HCOLS], F32R)
    with nc.Block() as block:

        @block.sync
        def _(sp):
            for b in range(2):
                sp.sem_inc(rows_free[b], 1)
            with sp.Fori(0, HSTEPS) as i:
                for j in range(HALF):
                    sp.wait_ge(rows_free[j], 1)
                    sp.sem_inc(rows_free[j], -1)
                    rows_dma(sp, rows[:, j], agg_t[:, ds(i * HALF + j, 1)].rearrange("p a d -> p (a d)"), rows_in[j])
            for b in range(2):
                sp.wait_ge(rows_free[b], 1)
                sp.sem_inc(rows_free[b], -1)

        @block.tensor
        def _(pe):
            def transposes(b):
                pe.wait_ge(s["psT_free"], 1)
                pe.sem_inc(s["psT_free"], -1)
                for j in range(HALF):
                    pe.wait_ge(rows_in[j], ROWS_DMA)
                    pe.sem_inc(rows_in[j], -ROWS_DMA)
                    for c in range(KC):
                        last = nc.tensor.transpose(psT[2 * b + c // 2][:, c % 2, j * PARTS:(j + 1) * PARTS],
                                                   rows[:, j, c * 128:(c + 1) * 128], T.ident[0:PARTS, 0:PARTS])
                    last.then_inc(s["psT_ready"], 1)

            def products(b):
                pe.wait_ge(s["split_ready"], 1)
                pe.sem_inc(s["split_ready"], -1)
                pe.wait_ge(s["psY_free"], 1)
                pe.sem_inc(s["psY_free"], -1)
                for m in range(KC):
                    parts = [(w, a, c) for c in range(KC) for w, a in ((w_high, a_high), (w_low, a_high), (w_high, a_low))]
                    for n, (w, a, c) in enumerate(parts):
                        last = nc.tensor.matmul(psY[2 * b + m // 2][:, m % 2], w[:, c, m * 128:(m + 1) * 128], a[:, b, c],
                                                start=n == 0, stop=n == len(parts) - 1)
                last.then_inc(s["psY_ready"], 1)

            transposes(0)
            with pe.Fori(0, HSTEPS // 2 - 1) as i:
                transposes(1)
                products(0)
                transposes(0)
                products(1)
            transposes(1)
            products(0)
            products(1)

        @block.scalar
        def _(act):
            act.sem_inc(s["split_free"], 2)
            with act.Fori(0, HSTEPS // 2) as i:
                for b in range(2):
                    for j in range(HALF):
                        act.wait_ge(s["psT_ready"], 1)
                        act.sem_inc(s["psT_ready"], -1)
                        act.sem_inc(rows_free[j], 1)
                    act.wait_ge(s["split_free"], 1)
                    act.sem_inc(s["split_free"], -1)
                    for k in range(2):
                        nc.scalar.activation(a_high[:, b, 2 * k:2 * k + 2], psT[2 * b + k][:], ACT.Copy).then_inc(adone, 1)
                    act.wait_ge(adone, 2)
                    act.sem_inc(adone, -2)
                    act.sem_inc(s["high_done"], 1)
            act.wait_ge(s["split_free"], 2)
            act.sem_inc(s["split_free"], -2)

        @block.vector
        def _(dve):
            dve.sem_inc(s["psT_free"], 2)
            dve.sem_inc(s["psY_free"], 2)

            def split(b):
                dve.wait_ge(s["high_done"], 1)
                dve.sem_inc(s["high_done"], -1)
                for k in range(2):
                    nc.vector.tensor_tensor(a_low[:, b, 2 * k:2 * k + 2], psT[2 * b + k][:], a_high[:, b, 2 * k:2 * k + 2],
                                            ALU.subtract).then_inc(done, 1)
                dve.wait_ge(done, 2)
                dve.sem_inc(done, -2)
                dve.sem_inc(s["psT_free"], 1)
                dve.sem_inc(s["split_ready"], 1)

            def add(step, b):
                dve.wait_ge(s["psY_ready"], 1)
                dve.sem_inc(s["psY_ready"], -1)
                dve.sem_inc(s["split_free"], 1)
                cols = ds(step * HCOLS, HCOLS)
                for m in range(KC):
                    nc.vector.scalar_tensor_tensor(xT[:, m, cols], psY[2 * b + m // 2][:, m % 2], bias_col[:, m:m + 1],
                                                   xT[:, m, cols], ALU.add, ALU.add).then_inc(done, 1)
                dve.wait_ge(done, KC)
                dve.sem_inc(done, -KC)
                dve.sem_inc(s["psY_free"], 1)
                for m in range(KC):
                    nc.vector.bn_stats(out=T.bn_stats[:, m, ds(step, 1)].rearrange("p a s -> p (a s)"),
                                       in_=xT[:, m, cols]).then_inc(done, 1)
                dve.wait_ge(done, KC)
                dve.sem_inc(done, -KC)

            split(0)
            with dve.Fori(0, HSTEPS // 2 - 1) as i:
                split(1)
                add(i * 2, 0)
                split(0)
                add(i * 2 + 1, 1)
            split(1)
            add(HSTEPS - 2, 0)
            add(HSTEPS - 1, 1)
            dve.wait_ge(s["psT_free"], 2)
            dve.sem_inc(s["psT_free"], -2)
            dve.wait_ge(s["psY_free"], 2)
            dve.sem_inc(s["psY_free"], -2)


def batchnorm(chip, sb, T, xT, gain, shift, steps):
    nc = chip.nc
    g, b_ = sb("bn_gain", [128, KC]), sb("bn_shift", [128, KC])
    mv, scale, off = sb("bn_mv", [128, KC, 2]), sb("bn_scale", [128, KC]), sb("bn_off", [128, KC])
    done, adone, pooled = chip.sem("dve_done"), chip.sem("act_done"), chip.sem("pool_done")
    with nc.Block() as block:

        @block.sync
        def _(sp):
            for out, in_ in ((g, gain), (b_, shift)):
                sp.dma_start(out[:], in_).then_inc(chip.sem("bn_in"), 16)

        @block.gpsimd
        def _(pool):
            pool.wait_ge(chip.sem("bn_aggregated"), 1)
            pool.sem_inc(chip.sem("bn_aggregated"), -1)
            pool.wait_ge(chip.sem("bn_in"), 32)
            pool.sem_inc(chip.sem("bn_in"), -32)

            def do(step):
                step.then_inc(pooled, 1)
                pool.wait_ge(pooled, 1)
                pool.sem_inc(pooled, -1)
            do(nc.gpsimd.tensor_scalar(scale[:], mv[:, :, 1], BN_EPS, None, ALU.add))
            do(nc.gpsimd.tensor_tensor(scale[:], scale[:], T.minus_half[:].to_broadcast([128, KC]), ALU.pow))
            do(nc.gpsimd.tensor_tensor(scale[:], scale[:], g[:], ALU.mult))
            do(nc.gpsimd.tensor_tensor(off[:], mv[:, :, 0], scale[:], ALU.mult))
            do(nc.gpsimd.tensor_tensor(off[:], b_[:], off[:], ALU.subtract))
            pool.sem_inc(chip.sem("bn_scales_v"), 1)
            pool.sem_inc(chip.sem("bn_scales_a"), 1)

        @block.vector
        def _(dve):
            for m in range(KC):
                nc.vector.bn_aggr(out=mv[:, m], in_=T.bn_stats[:, m, 0:steps]).then_inc(done, 1)
            dve.wait_ge(done, KC)
            dve.sem_inc(done, -KC)
            dve.sem_inc(chip.sem("bn_aggregated"), 1)
            dve.wait_ge(chip.sem("bn_scales_v"), 1)
            dve.sem_inc(chip.sem("bn_scales_v"), -1)
            for m in range(3):
                width = N if m < 2 else N // 2
                nc.vector.tensor_scalar(xT[:, m, 0:width], xT[:, m, 0:width], scale[:, m:m + 1], off[:, m:m + 1], ALU.mult,
                                        ALU.add).then_inc(done, 1)
            dve.wait_ge(done, 3)
            dve.sem_inc(done, -3)

        @block.scalar
        def _(act):
            act.wait_ge(chip.sem("bn_scales_a"), 1)
            act.sem_inc(chip.sem("bn_scales_a"), -1)
            for m, start in ((3, 0), (2, N // 2)):
                nc.scalar.activation(xT[:, m, start:N], xT[:, m, start:N], ACT.Identity, bias=off[:, m:m + 1],
                                     scale=scale[:, m:m + 1]).then_inc(adone, 1)
            act.wait_ge(adone, 2)
            act.sem_inc(adone, -2)


def feed_forward(chip, sb, ps, T, xT, w1, b1, w2, b2):
    nc = chip.nc
    cols_n = GROUP * PARTS
    w1_high, w1_low = sb("w1_high", [128, KC, 2 * FF], F32R), sb("w1_low", [128, KC, 2 * FF], F32R)
    w2_high, w2_low = sb("w2_high", [2 * FF, D], F32R), sb("w2_low", [2 * FF, D], F32R)
    w1_raw, w2_raw = sb("w1_raw", [128, KC, 2 * FF]), sb("w2_raw", [2 * FF, D])
    b1_col, b2_col = sb("b1_col", [2 * FF, 1]), sb("b2_col", [128, KC])
    x_high, x_low = sb("ff_x_high", [128, KC, cols_n], F32R), sb("ff_x_low", [128, KC, cols_n], F32R)
    hid, parts_ = sb("hid", [2 * FF, cols_n]), sb("hid_parts", [2 * FF, cols_n], F32R)
    psH, psY = ps("psH_f", 1, [128, cols_n])[0], ps("psY_f", 4, [128, cols_n])
    done, adone = chip.sem("dve_done"), chip.sem("act_done")
    names = ("high_done", "split_ready", "split_free", "psH_ready", "psH_free", "hid_ready", "hid_free", "psY_ready", "psY_free")
    s = {n: chip.sem(n) for n in names}

    with nc.Block() as block:

        @block.sync
        def _(sp):
            w1v = w1.rearrange("(c k) n -> k c n", c=KC)
            moves = ((w1_raw[:, :, 0:FF], w1v), (w1_raw[:, :, FF:2 * FF], w1v), (w2_raw[0:FF], w2), (w2_raw[FF:2 * FF], w2),
                     (b1_col[0:FF], b1.unsqueeze(1)), (b1_col[FF:2 * FF], b1.unsqueeze(1)),
                     (b2_col[:], b2))
            for out, in_ in moves:
                sp.dma_start(out, in_).then_inc(chip.sem("w_in"), 16)
            sp.wait_ge(chip.sem("w_in"), 16 * len(moves))
            sp.sem_inc(chip.sem("w_in"), -(16 * len(moves)))
            sp.sem_inc(chip.sem("w_here"), 1)

        @block.scalar
        def _(act):
            act.wait_ge(chip.sem("w_here"), 1)
            act.sem_inc(chip.sem("w_here"), -1)
            nc.scalar.activation(w1_high[:], w1_raw[:], ACT.Copy).then_inc(adone, 1)
            nc.scalar.activation(w2_high[:], w2_raw[:], ACT.Copy).then_inc(adone, 1)
            act.wait_ge(adone, 2)
            act.sem_inc(adone, -2)
            act.sem_inc(chip.sem("w_high"), 1)

        @block.vector
        def _(dve):
            dve.wait_ge(chip.sem("w_high"), 1)
            dve.sem_inc(chip.sem("w_high"), -1)
            nc.vector.tensor_tensor(w1_low[:], w1_raw[:], w1_high[:], ALU.subtract).then_inc(done, 1)
            nc.vector.tensor_tensor(w2_low[:], w2_raw[:], w2_high[:], ALU.subtract).then_inc(done, 1)
            dve.wait_ge(done, 2)
            dve.sem_inc(done, -2)

    with nc.Block() as block:

        @block.scalar
        def _(act):
            act.sem_inc(s["split_free"], 1)

            def split(g):
                act.wait_ge(s["split_free"], 1)
                act.sem_inc(s["split_free"], -1)
                nc.scalar.activation(x_high[:], xT[:, :, ds(g * cols_n, cols_n)], ACT.Copy).then_inc(s["high_done"], 1)

            def hidden():
                act.wait_ge(s["psH_ready"], 1)
                act.sem_inc(s["psH_ready"], -1)
                act.sem_inc(s["split_free"], 1)
                act.wait_ge(s["hid_free"], 1)
                act.sem_inc(s["hid_free"], -1)
                nc.scalar.activation(hid[:], psH[:], ACT.Relu, bias=b1_col[:, 0:1]).then_inc(adone, 1)
                act.wait_ge(adone, 1)
                act.sem_inc(adone, -1)
                act.sem_inc(s["psH_free"], 1)
                nc.scalar.activation(parts_[:], hid[:], ACT.Copy).then_inc(s["hid_ready"], 1)

            act.sem_inc(s["psH_free"], 1)
            split(0)
            with act.Fori(0, GROUPS - 1) as g:
                hidden()
                split(g + 1)
            hidden()
            act.wait_ge(s["psH_free"], 1)
            act.sem_inc(s["psH_free"], -1)
            act.wait_ge(s["split_free"], 1)
            act.sem_inc(s["split_free"], -1)

        @block.gpsimd
        def _(pool):
            with pool.Fori(0, GROUPS) as g:
                pool.wait_ge(s["high_done"], 1)
                pool.sem_inc(s["high_done"], -1)
                nc.gpsimd.tensor_tensor(x_low[:], xT[:, :, ds(g * cols_n, cols_n)], x_high[:], ALU.subtract)\
                    .then_inc(s["split_ready"], 1)

        @block.tensor
        def _(pe):
            with pe.Fori(0, GROUPS) as g:
                pe.wait_ge(s["split_ready"], 1)
                pe.sem_inc(s["split_ready"], -1)
                pe.wait_ge(s["psH_free"], 1)
                pe.sem_inc(s["psH_free"], -1)
                parts = [(w, a, c) for c in range(KC) for w, a in ((w1_high, x_high), (w1_low, x_high), (w1_high, x_low))]
                for n, (w, a, c) in enumerate(parts):
                    last = nc.tensor.matmul(psH[:], w[:, c], a[:, c], start=n == 0, stop=n == len(parts) - 1)
                last.then_inc(s["psH_ready"], 1)
                pe.wait_ge(chip.sem("hid_low_ready"), 1)
                pe.sem_inc(chip.sem("hid_low_ready"), -1)
                for m in range(KC):
                    pe.wait_ge(s["psY_free"], 1)
                    pe.sem_inc(s["psY_free"], -1)
                    out = slice(m * 128, (m + 1) * 128)
                    nc.tensor.matmul(psY[m][:], w2_high[:, out], parts_[:], start=True, stop=False)
                    nc.tensor.matmul(psY[m][:], w2_low[0:FF, out], parts_[0:FF], start=False, stop=True)\
                        .then_inc(s["psY_ready"], 1)

        @block.vector
        def _(dve):
            dve.sem_inc(s["psY_free"], 4)
            dve.sem_inc(s["hid_free"], 1)
            with dve.Fori(0, GROUPS) as g:
                dve.wait_ge(s["hid_ready"], 1)
                dve.sem_inc(s["hid_ready"], -1)
                nc.vector.tensor_tensor(parts_[FF:2 * FF], hid[FF:2 * FF], parts_[FF:2 * FF], ALU.subtract)\
                    .then_inc(chip.sem("hid_low_ready"), 1)
                cols = ds(g * cols_n, cols_n)
                for m in range(KC):
                    dve.wait_ge(s["psY_ready"], 1)
                    dve.sem_inc(s["psY_ready"], -1)
                    if m == KC - 1:
                        dve.sem_inc(s["hid_free"], 1)
                    nc.vector.scalar_tensor_tensor(xT[:, m, cols], psY[m][:], b2_col[:, m:m + 1], xT[:, m, cols], ALU.add,
                                                   ALU.add).then_inc(done, 1)
                    dve.wait_ge(done, 1 if m == 0 else 2)
                    dve.sem_inc(done, -(1 if m == 0 else 2))
                    dve.sem_inc(s["psY_free"], 1)
                    nc.vector.bn_stats(out=T.bn_stats[:, m, ds(g, 1)].rearrange("p a s -> p (a s)"),
                                       in_=xT[:, m, cols]).then_inc(done, 1)
                dve.wait_ge(done, 1)
                dve.sem_inc(done, -1)
            dve.wait_ge(s["psY_free"], 4)
            dve.sem_inc(s["psY_free"], -4)
            dve.wait_ge(s["hid_free"], 1)
            dve.sem_inc(s["hid_free"], -1)


def finish(chip, sb, ps, T, xT, gain, shift, out):
    nc = chip.nc
    x1 = sb("x1", [PARTS, 2, GROUP, D])
    column = sb("column", [128, 2, KC, PARTS])
    gain_row, shift_row = sb("gain_row", [PARTS, D]), sb("shift_row", [PARTS, D])
    z = sb("z", [PARTS, 2, D])
    stats, mv = sb("stats_z", [PARTS, 2, 6]), sb("mv_z", [PARTS, 2, 2])
    rstd, off = sb("rstd_z", [PARTS, 2]), sb("off_z", [PARTS, 2])
    psZ = ps("psZ", 2, [128, D])
    done, adone, pooled = chip.sem("dve_done"), chip.sem("act_done"), chip.sem("pool_done")
    names = ("column_ready", "column_free", "psZ_ready", "psZ_free", "var_ready", "normed", "z_ready", "z_free",
             "sum_ready", "z_first")
    s = {n: chip.sem(n) for n in names}
    x_in, sum_done, stored = (chip.sem2(n) for n in ("x_loaded", "sum_done", "stored"))
    t_in, t_out = tiles_of(T.x1), tiles_of(out)

    with nc.Block() as block:

        @block.sync
        def _(sp):
            for o, i_ in ((gain_row, gain), (shift_row, shift)):
                sp.dma_start(o[:], i_.unsqueeze(0).to_broadcast([PARTS, D])).then_inc(chip.sem("bias_in"), 16)
            sp.wait_ge(chip.sem("bias_in"), 32)
            sp.sem_inc(chip.sem("bias_in"), -32)
            sp.sem_inc(chip.sem("gains_here"), 1)
            sp.sem_inc(chip.sem("shifts_here"), 1)

            def load(g, b):
                sp.wait_ge(stored[b], ROWS_DMA)
                sp.sem_inc(stored[b], -ROWS_DMA)
                rows_dma(sp, x1[:, b], t_in[:, ds(g * GROUP, GROUP)], x_in[b])

            def store(g, b):
                sp.wait_ge(sum_done[b], GROUP)
                sp.sem_inc(sum_done[b], -GROUP)
                rows_dma(sp, t_out[:, ds(g * GROUP, GROUP)], x1[:, b], stored[b])

            for b in range(2):
                sp.sem_inc(stored[b], ROWS_DMA)
                load(b, b)
            with sp.Fori(0, GROUPS // 2 - 1) as i:
                for b in range(2):
                    store(i * 2 + b, b)
                    load(i * 2 + b + 2, b)
            for b in range(2):
                store(GROUPS - 2 + b, b)
            for b in range(2):
                sp.wait_ge(stored[b], ROWS_DMA)
                sp.sem_inc(stored[b], -ROWS_DMA)

        @block.gpsimd
        def _(pool):
            pool.wait_ge(chip.sem("shifts_here"), 1)
            pool.sem_inc(chip.sem("shifts_here"), -1)
            pool.sem_inc(s["column_free"], 2)
            with pool.Fori(0, GROUPS // 2) as i:
                for b in range(2):
                    pool.wait_ge(x_in[b], ROWS_DMA)
                    pool.sem_inc(x_in[b], -ROWS_DMA)
                    for j in range(GROUP):
                        k = j % 2
                        pool.wait_ge(s["var_ready"], 1)
                        pool.sem_inc(s["var_ready"], -1)
                        nc.gpsimd.tensor_scalar(rstd[:, k:k + 1], mv[:, k, 1:2], LN_EPS, None, ALU.add).then_inc(pooled, 1)
                        nc.gpsimd.tensor_scalar(off[:, k:k + 1], mv[:, k, 0:1], -1.0, None, ALU.mult).then_inc(pooled, 1)
                        pool.wait_ge(pooled, 2)
                        pool.sem_inc(pooled, -2)
                        nc.gpsimd.tensor_tensor(rstd[:, k:k + 1], rstd[:, k:k + 1], T.minus_half[0:PARTS], ALU.pow)\
                            .then_inc(pooled, 1)
                        pool.wait_ge(pooled, 1)
                        pool.sem_inc(pooled, -1)
                        nc.gpsimd.tensor_tensor(off[:, k:k + 1], off[:, k:k + 1], rstd[:, k:k + 1], ALU.mult)\
                            .then_inc(s["normed"], 1)
                        nc.gpsimd.tensor_tensor(x1[:, b, j], x1[:, b, j], shift_row[:], ALU.add).then_inc(s["sum_ready"], 1)

        @block.scalar
        def _(act):
            act.sem_inc(s["psZ_free"], 2)

            def column_of(t, k):
                act.wait_ge(s["column_free"], 1)
                act.sem_inc(s["column_free"], -1)
                nc.scalar.activation(column[:, k], xT[:, :, ds(t * PARTS, PARTS)], ACT.Copy).then_inc(s["column_ready"], 1)

            def norm(k):
                act.wait_ge(s["normed"], 1)
                act.sem_inc(s["normed"], -1)
                act.wait_ge(s["z_free"], 1)
                act.sem_inc(s["z_free"], -1)
                nc.scalar.activation(z[:, k], psZ[k][0:PARTS], ACT.Identity, bias=off[:, k:k + 1], scale=rstd[:, k:k + 1])\
                    .then_inc(adone, 1)
                act.wait_ge(adone, 1)
                act.sem_inc(adone, -1)
                act.sem_inc(s["psZ_free"], 1)
                act.sem_inc(s["z_ready"], 1)

            column_of(0, 0)
            column_of(1, 1)
            with act.Fori(0, TILES // 2 - 1) as i:
                for k in range(2):
                    norm(k)
                    column_of(i * 2 + k + 2, k)
            norm(0)
            norm(1)
            act.wait_ge(s["psZ_free"], 2)
            act.sem_inc(s["psZ_free"], -2)
            act.wait_ge(s["column_free"], 2)
            act.sem_inc(s["column_free"], -2)
            act.wait_ge(s["z_free"], 2)
            act.sem_inc(s["z_free"], -2)

        @block.tensor
        def _(pe):
            with pe.Fori(0, TILES // 2) as i:
                for k in range(2):
                    pe.wait_ge(s["column_ready"], 1)
                    pe.sem_inc(s["column_ready"], -1)
                    pe.wait_ge(s["psZ_free"], 1)
                    pe.sem_inc(s["psZ_free"], -1)
                    for c in range(KC):
                        last = nc.tensor.transpose(psZ[k][0:PARTS, c * 128:(c + 1) * 128], column[:, k, c], T.ident[:])
                    last.then_inc(s["psZ_ready"], 1)

        @block.vector
        def _(dve):
            dve.wait_ge(chip.sem("gains_here"), 1)
            dve.sem_inc(chip.sem("gains_here"), -1)
            dve.sem_inc(s["z_free"], 2)

            def statistics(k):
                dve.wait_ge(s["psZ_ready"], 1)
                dve.sem_inc(s["psZ_ready"], -1)
                dve.sem_inc(s["column_free"], 1)
                nc.vector.bn_stats(out=stats[:, k], in_=psZ[k][0:PARTS]).then_inc(done, 1)
                dve.wait_ge(done, 1)
                dve.sem_inc(done, -1)
                nc.vector.bn_aggr(out=mv[:, k], in_=stats[:, k]).then_inc(s["var_ready"], 1)

            def add(b, j):
                k = j % 2
                dve.wait_ge(s["z_ready"], 1)
                dve.sem_inc(s["z_ready"], -1)
                nc.vector.tensor_tensor(z[:, k], z[:, k], gain_row[:], ALU.mult).then_inc(done, 1)
                dve.wait_ge(done, 1)
                dve.sem_inc(done, -1)
                dve.wait_ge(s["sum_ready"], 1)
                dve.sem_inc(s["sum_ready"], -1)
                nc.vector.tensor_tensor(x1[:, b, j], x1[:, b, j], z[:, k], ALU.add).then_inc(done, 1)
                dve.wait_ge(done, 1)
                dve.sem_inc(done, -1)
                dve.sem_inc(sum_done[b], 1)
                dve.sem_inc(s["z_free"], 1)

            statistics(0)
            with dve.Fori(0, GROUPS // 2 - 1) as i:
                for b in range(2):
                    for j in range(GROUP):
                        statistics((j + 1) % 2)
                        add(b, j)
            for b in range(2):
                for j in range(GROUP):
                    if (b, j) != (1, GROUP - 1):
                        statistics((j + 1) % 2)
                    add(b, j)


class Names:
    pass


def program(nc, A, out, scratch):
    ctx = ExitStack()
    with ctx:
        chip = Chip(nc, ctx)

        def allocator(stack):
            def sb(name, shape, dtype=F32):
                return stack.enter_context(nc.sbuf_tensor(chip.unique(name), shape, dtype))

            def ps(name, n, shape):
                size = math.prod(shape[1:])
                banks = -(-size // 512)
                whole = [stack.enter_context(nc.psum_tensor(chip.unique(name), [128, banks * 512], F32)) for k in range(n)]
                pieces = [w[0:shape[0], 0:size] for w in whole]
                return pieces if len(shape) == 2 else [x.rearrange("p (a b) -> p a b", a=shape[1]) for x in pieces]
            return sb, ps

        keep, _ = allocator(ctx)
        T, W = Names(), Names()
        T.messages, T.agg_l0, T.agg, T.x1 = scratch("messages", [N, MSG]), \
            [scratch(f"agg_l0_{k}", [N + PARTS, AGG]) for k in range(2)], scratch("agg", [N + PARTS, D]), scratch("x1_rows", [N, D])
        xT = keep("xT", [128, KC, N])
        rooms = [xT[0:PARTS, c].rearrange("p (t q) -> p t q", t=TILES) for c in range(KC)]
        T.same_src, T.earlier, T.srcq_i, T.zeros = rooms[0], rooms[1], rooms[2].bitcast(I32), xT[0:PARTS, 3]
        T.ident = keep("ident", [128, 128])
        T.minus_half = keep("minus_half", [128, 1])
        T.dst_ext = keep("dst_ext", [PARTS, TILES + 2], I32)
        T.dst_f = keep("dst_f", [PARTS, TILES + 2])
        T.src_i = keep("src_i", [PARTS, TILES], I32)
        T.ends_i = keep("ends_i", [HEADS, 2, PARTS], I32)
        T.spare_i, T.spare = keep("spare_i", [PARTS, 1], I32), keep("spare", [PARTS, 1])
        interaction = ExitStack()
        keep_l0, _ = allocator(interaction)
        W.in2f = keep_l0("w_in2f", [B, 2, F])
        W.f2o1_s, W.f2o2_s, W.vec = keep_l0("w_f2o1_s", [128, B]), keep_l0("w_f2o2_s", [B, B]), keep_l0("w_vec", [128, 2, B])
        W.w1, W.b1, W.w2 = keep_l0("w1", [R, F]), keep_l0("b1", [F, 1]), keep_l0("w2", [F + 1, 6 * F])
        with ExitStack() as edges:
            sb, _ = allocator(edges)
            T.src_f = sb("src_f", [PARTS, TILES])
            T.rcut, T.y = sb("rcut", [PARTS, TILES]), sb("y", [PARTS, TILES, 4])
            T.dup, T.tmp80, T.scat_i = sb("dup", [PARTS, TILES]), sb("tmp80", [PARTS, TILES]), sb("scat_i", [PARTS, TILES], I32)
            T.lower = sb("lower", [PARTS, PARTS])
            with ExitStack() as stage:
                setup(chip, *allocator(stage), T, W, A)
            with ExitStack() as stage:
                l0_node_messages(chip, *allocator(stage), A.x, T, W)
            with ExitStack() as stage:
                l0_edges(chip, *allocator(stage), T, W, A.radial)
        with ExitStack() as stage:
            l0_nodes(chip, *allocator(stage), A.x, T, W, xT)
        interaction.close()

        T.q, T.k, T.v = (scratch(n, [N, D]) for n in ("q", "k", "v"))
        T.same, T.same_next, T.same_neg, T.next_neg = (keep(n, [PARTS, TILES]) for n in ("same", "same_next", "same_neg", "next_neg"))
        T.row_i, T.fix_i, T.carry = keep("row_i", [PARTS, TILES], I32), keep("fix_i", [PARTS, 1], I32), keep("carry", [PARTS, PARTS])
        T.pass_fwd, T.pass_bwd, T.pass_fwd_neg, T.pass_bwd_neg, T.whole = \
            (keep(n, [HEADS, PARTS]) for n in ("pass_fwd", "pass_bwd", "pass_fwd_neg", "pass_bwd_neg", "whole"))
        T.cont, T.cont_neg = keep("cont", [HEADS, PARTS + 1]), keep("cont_neg", [HEADS, PARTS + 1])
        T.weight = keep("weight", [PARTS, HEADS, TILES])
        T.bn_stats = keep("bn_stats", [128, KC, HSTEPS, 6])
        with ExitStack() as stage:
            attention_masks(chip, *allocator(stage), T)
        for layer in range(LAYERS):
            for weight, bias, table, scores in ((A.wk, None, T.k, None), (A.wq, A.bq, T.q, None),
                                                (A.wv, None, T.v, scores_and_softmax)):
                with ExitStack() as stage:
                    project(chip, *allocator(stage), T, xT, weight[layer], None if bias is None else bias[layer], table, scores)
            with ExitStack() as stage:
                aggregate(chip, *allocator(stage), T)
            with ExitStack() as stage:
                output_projection(chip, *allocator(stage), T, xT, A.wo[layer], A.bo[layer])
            with ExitStack() as stage:
                batchnorm(chip, allocator(stage)[0], T, xT, A.g1[layer], A.beta1[layer], HSTEPS)
            with ExitStack() as stage:
                feed_forward(chip, *allocator(stage), T, xT, A.ff1[layer], A.ffb1[layer], A.ff2[layer], A.ffb2[layer])
            with ExitStack() as stage:
                batchnorm(chip, allocator(stage)[0], T, xT, A.g2[layer], A.beta2[layer], GROUPS)
        with ExitStack() as stage:
            finish(chip, *allocator(stage), T, xT, A.ln_g, A.ln_b, out)


def kernel(**inputs):
    import numpy as np
    import concourse.bacc as bacc
    from concourse.bass_utils import run_bass_kernel_spmd

    nc = bacc.Bacc("TRN2", target_bir_lowering=False, num_devices=1)
    g = {k: np.asarray(v) for k, v in inputs.items()}
    laid = {
        "x": g["x"],
        "src": g["src"], "dst": g["dst"],
        "src_tiled": g["src"].reshape(PARTS, TILES).T.reshape(-1),
        "dst_tiled": g["dst"].reshape(PARTS, TILES).T,
        "radial": g["edge_attr_20"].reshape(PARTS, TILES, R).transpose(2, 1, 0).reshape(R, E),
        "y": g["edge_attr_4"], "rcut": g["edge_weight"],
        "in2f_s": g["L0_gnn_w_in2f_s"], "in2f_v": g["L0_gnn_w_in2f_v"],
        "w1": g["L0_gnn_W1"], "b1": g["L0_gnn_b1"],
        "w2": g["L0_gnn_W2"].reshape(F, F, 6).transpose(0, 2, 1).reshape(F, 6 * F),
        "b2": g["L0_gnn_b2"].reshape(F, 6).T.reshape(6 * F),
        "f2o1_s": g["L0_gnn_w_f2o1_s"], "f2o1_vT": g["L0_gnn_w_f2o1_v"].T,
        "f2o2_s": g["L0_gnn_w_f2o2_s"], "f2o2_v": g["L0_gnn_w_f2o2_v"],
        "ln_g": g["L1_gnn_ln_g"], "ln_b": g["L1_gnn_ln_b"], "bq": g["L1_gnn_bq"], "ffb1": g["L1_gnn_b1"],
    }
    for to, name in (("wq", "Wq"), ("wk", "Wk"), ("wv", "Wv"), ("wo", "Wo"), ("ff1", "W1"), ("ff2", "W2")):
        laid[to] = g["L1_gnn_" + name].transpose(0, 2, 1)
    for to, name in (("bo", "bo"), ("ffb2", "b2"), ("g1", "g1"), ("beta1", "beta1"), ("g2", "g2"), ("beta2", "beta2")):
        laid[to] = g["L1_gnn_" + name].reshape(LAYERS, KC, 128).transpose(0, 2, 1)
    arrays, A = {}, Names()
    for name, a in laid.items():
        arrays[f"in_{name}"] = np.ascontiguousarray(a)
        A.__dict__[name] = nc.dram_tensor(f"in_{name}", list(a.shape), mybir.dt.from_np(a.dtype), kind="ExternalInput").ap()
    out = nc.dram_tensor("out", [N, D], F32, kind="ExternalOutput").ap()

    def scratch(name, shape):
        return nc.dram_tensor(name, shape, F32).ap()

    program(nc, A, out, scratch)
    return run_bass_kernel_spmd(nc, [arrays], core_ids=[0]).results[0]["out"]
```

```python
import math
from contextlib import ExitStack

import concourse.bass as bass
from concourse import mybir

F32 = mybir.dt.float32
F32R = mybir.dt.float32r
I32 = mybir.dt.int32
ALU = mybir.AluOpType
ACT = mybir.ActivationFunctionType
AXIS = mybir.AxisListType

N = 10000
E = 10000
D = 512
PARTS = 125
TILES = N // PARTS
GROUP = 4
GROUPS = TILES // GROUP
KC = D // 128
WIDE = 112
ROWS_DMA = 32
B = 128
F = 32
R = 20
MSG = 4 * F
AGG = 8 * F
HEADS = 8
HD = D // HEADS
LAYERS = 2
SLOTS = 3
FF = 64
LN_EPS = 1e-5
BN_EPS = 1e-5
LOG2 = 0.6931471805599453
FAR = 16384.0
NEG = -1e30
ds = bass.ds


def rows_dma(engine, out, in_, sem):
    engine.dma_start(out[0:WIDE], in_[0:WIDE]).then_inc(sem, 16)
    engine.dma_start(out[WIDE:PARTS], in_[WIDE:PARTS]).then_inc(sem, 16)


class Chip:

    def __init__(self, nc, ctx):
        self.nc, self.ctx, self.sems, self.counts, self.tensors = nc, ctx, {}, {}, 0

    def sem(self, name):
        if name not in self.sems:
            self.sems[name] = self.ctx.enter_context(self.nc.semaphore(name))
        return self.sems[name]

    def sem2(self, name):
        return [self.sem(f"{name}_0"), self.sem(f"{name}_1")]

    def unique(self, name):
        self.tensors += 1
        return f"{name}_{self.tensors}"

    def counted(self, name, n):
        before = self.counts.get(name, 0)
        self.counts[name] = before + n
        return self.sem(name), before


def tiles_of(dram):
    return dram.rearrange("(p t) d -> p t d", t=TILES)


def bcast(ap, n):
    a = ap.unsqueeze(len(ap.shape))
    return a.to_broadcast([*ap.shape, n])


def zero_rows(engine, T, table, cols, g, zeroed):
    n = TILES * cols // GROUPS
    rows_dma(engine, table[0:N, :].rearrange("(p t) d -> p (t d)", t=TILES)[:, ds(g * n, n)], T.zeros[:, 0:n], zeroed)


def setup(chip, sb, ps, T, W, A):
    nc = chip.nc
    raw_vT = sb("raw_vT", [B, 2, 2 * F])
    raw_o2v = sb("raw_o2v", [B, B])
    psV = ps("psV", 1, [128, B])[0]
    made, loads, weights_in = chip.sem("const_made"), chip.sem("edges_in"), chip.sem("weights_in")
    done, cleared = chip.sem("dve_done"), chip.sem("cleared")
    with nc.Block() as block:

        @block.gpsimd
        def _(pool):
            nc.gpsimd.memset(T.dst_ext[:], -1).then_inc(made, 1)
            pool.wait_ge(made, 1)
            pool.sem_inc(made, -1)
            pool.sem_inc(cleared, 1)
            nc.gpsimd.memset(T.ident[:], 0.0).then_inc(made, 1)
            nc.gpsimd.memset(T.lower[:], 1.0).then_inc(made, 1)
            nc.gpsimd.memset(T.zeros[:, 0:TILES * D // GROUPS], 0.0).then_inc(made, 1)
            nc.gpsimd.memset(T.minus_half[:], -0.5).then_inc(made, 1)
            pool.wait_ge(made, 4)
            pool.sem_inc(made, -4)
            nc.gpsimd.affine_select(out=T.ident[:], in_=T.ident[:], compare_op=ALU.not_equal, fill=1.0,
                                    base=0, pattern=[[-1, 128]], channel_multiplier=1).then_inc(made, 1)
            nc.gpsimd.affine_select(out=T.lower[:], in_=T.lower[:], compare_op=ALU.is_gt, fill=0.0,
                                    base=0, pattern=[[-1, PARTS]], channel_multiplier=1).then_inc(made, 1)
            nc.gpsimd.iota(T.spare_i[:], pattern=[[0, 1]], base=N, channel_multiplier=1).then_inc(made, 1)
            pool.wait_ge(made, 3)
            pool.sem_inc(made, -3)
            nc.gpsimd.tensor_copy(T.spare[:], T.spare_i[:]).then_inc(made, 1)
            pool.wait_ge(made, 1)
            pool.sem_inc(made, -1)

        @block.sync
        def _(sp):
            moves = ((raw_vT[:, 0], A.f2o1_vT), (raw_vT[:, 1], A.f2o1_vT), (raw_o2v[:], A.f2o2_v),
                     (W.in2f[:, 0], A.in2f_s), (W.in2f[:, 1], A.in2f_v), (W.f2o1_s[0:2 * F], A.f2o1_s),
                     (W.f2o2_s[:], A.f2o2_s), (W.w1[:], A.w1), (W.b1[:], A.b1.rearrange("(f a) -> f a", a=1)),
                     (W.w2[0:F], A.w2), (W.w2[F:F + 1], A.b2.unsqueeze(0)))
            for out, in_ in moves:
                sp.dma_start(out, in_).then_inc(weights_in, 16)
            sp.wait_ge(cleared, 1)
            sp.sem_inc(cleared, -1)
            moves2 = ((T.src_i[:], A.src.rearrange("(p t) -> p t", t=TILES)),
                      (T.dst_ext[:, 1:TILES + 1], A.dst.rearrange("(p t) -> p t", t=TILES)),
                      (T.dst_ext[1:PARTS, 0:1], A.dst_tiled[TILES - 1:TILES, 0:PARTS - 1].rearrange("t p -> p t")),
                      (T.dst_ext[0:PARTS - 1, TILES + 1:TILES + 2], A.dst_tiled[0:1, 1:PARTS].rearrange("t p -> p t")),
                      (T.rcut[:], A.rcut.rearrange("(p t) -> p t", t=TILES)),
                      (T.y[:], A.y.rearrange("(p t) c -> p t c", t=TILES)),
                      (T.srcq_i[:].rearrange("p t q -> p (t q)"), A.src_tiled.unsqueeze(0).to_broadcast([PARTS, E])))
            for out, in_ in moves2:
                sp.dma_start(out, in_).then_inc(loads, 16)
            sp.wait_ge(loads, 16 * len(moves2))
            sp.sem_inc(loads, -(16 * len(moves2)))

        @block.tensor
        def _(pe):
            pe.wait_ge(weights_in, 16 * 11)
            nc.tensor.matmul(psV[:], raw_vT[:].rearrange("k a m -> k (a m)"), raw_o2v[:], start=True, stop=True)\
                .then_inc(chip.sem("psV_ready"), 1)

        @block.vector
        def _(dve):
            nc.vector.memset(W.vec[:], 0.0).then_inc(done, 1)
            nc.vector.memset(W.f2o1_s[2 * F:128], 0.0).then_inc(done, 1)
            dve.wait_ge(done, 2)
            dve.sem_inc(done, -2)
            dve.wait_ge(weights_in, 16 * 11)
            root = 1.0 / math.sqrt(B)
            nc.vector.tensor_scalar(W.in2f[:], W.in2f[:], root, None, ALU.mult).then_inc(done, 1)
            nc.vector.tensor_scalar(W.f2o2_s[:], W.f2o2_s[:], root, None, ALU.mult).then_inc(done, 1)
            nc.vector.tensor_scalar(W.f2o1_s[0:2 * F], W.f2o1_s[0:2 * F], 1.0 / math.sqrt(2 * F), None, ALU.mult)\
                .then_inc(done, 1)
            dve.wait_ge(chip.sem("psV_ready"), 1)
            dve.sem_inc(chip.sem("psV_ready"), -1)
            for half in range(2):
                rows = slice(64 * half, 64 * half + 64)
                nc.vector.tensor_scalar(W.vec[rows, half], psV[rows], root / math.sqrt(2 * F), None, ALU.mult)\
                    .then_inc(done, 1)
            dve.wait_ge(done, 5)
            dve.sem_inc(done, -5)


def layernorm_stats(chip, dve, tile_of, stats, mv, var_ready):
    nc, done = chip.nc, chip.sem("dve_done")
    for j in range(GROUP):
        nc.vector.bn_stats(out=stats[:, j], in_=tile_of(j)).then_inc(done, 1)
    dve.wait_ge(done, GROUP)
    dve.sem_inc(done, -GROUP)
    for j in range(GROUP):
        nc.vector.bn_aggr(out=mv[:, j], in_=stats[:, j]).then_inc(done, 1)
    dve.wait_ge(done, GROUP)
    dve.sem_inc(done, -GROUP)
    dve.sem_inc(var_ready, 1)


def layernorm_scales(chip, pool, T, mv, rstd, shift, var_ready, normed):
    nc, done = chip.nc, chip.sem("pool_done")
    pool.wait_ge(var_ready, 1)
    pool.sem_inc(var_ready, -1)
    nc.gpsimd.tensor_scalar(rstd, mv[:, :, 1], LN_EPS, None, ALU.add).then_inc(done, 1)
    nc.gpsimd.tensor_scalar(shift, mv[:, :, 0], -1.0, None, ALU.mult).then_inc(done, 1)
    pool.wait_ge(done, 2)
    pool.sem_inc(done, -2)
    nc.gpsimd.tensor_tensor(rstd, rstd, T.minus_half[0:PARTS, 0:1].to_broadcast([PARTS, GROUP]), ALU.pow).then_inc(done, 1)
    pool.wait_ge(done, 1)
    pool.sem_inc(done, -1)
    nc.gpsimd.tensor_tensor(shift, shift, rstd, ALU.mult).then_inc(normed, 1)


def l0_node_messages(chip, sb, ps, x, T, W):
    nc = chip.nc
    xin = sb("xin", [PARTS, 2, GROUP, D])
    stats = sb("stats", [PARTS, GROUP, 6])
    mv = sb("mv", [PARTS, 2, GROUP, 2])
    rstd, shift = sb("rstd", [PARTS, 2, GROUP]), sb("shift", [PARTS, 2, GROUP])
    h = sb("h", [PARTS, 2, D])
    hT = sb("hT", [128, 2, KC, PARTS])
    stage = sb("stage", [PARTS, 2, GROUP, MSG])
    psT = ps("psT", 2, [128, KC, PARTS])
    psM = ps("psM", 2, [128, 4, F])
    loaded, x_free, stored = chip.sem2("x_loaded"), chip.sem2("x_free"), chip.sem2("stored")
    stage_ready = chip.sem2("stage_ready")
    normed, h_ready, psT_ready = chip.sem("normed"), chip.sem("h_ready"), chip.sem("psT_ready")
    hT_ready, hT_free, psM_ready, psM_free = (chip.sem(n) for n in ("hT_ready", "hT_free", "psM_ready", "psM_free"))
    done, var_ready = chip.sem("dve_done"), chip.sem("var_ready")
    xt, table = tiles_of(x), tiles_of(T.messages)

    with nc.Block() as block:

        @block.sync
        def _(sp):
            def load(g, b):
                sp.wait_ge(x_free[b], 1)
                sp.sem_inc(x_free[b], -1)
                rows_dma(sp, xin[:, b], xt[:, ds(g * GROUP, GROUP)], loaded[b])

            def store(g, b):
                sp.wait_ge(stage_ready[b], 1)
                sp.sem_inc(stage_ready[b], -1)
                rows_dma(sp, table[:, ds(g * GROUP, GROUP)], stage[:, b], stored[b])

            zeroed = chip.sem("zeroed")
            for b in range(2):
                sp.sem_inc(x_free[b], 1)
                sp.sem_inc(stored[b], ROWS_DMA)
                load(b, b)
            with sp.Fori(0, GROUPS // 2 - 1) as i:
                for b in range(2):
                    load(i * 2 + 2 + b, b)
                    for table_l0 in T.agg_l0:
                        zero_rows(sp, T, table_l0, AGG, i * 2 + b, zeroed)
                    store(i * 2 + b, b)
            for b in range(2):
                for table_l0 in T.agg_l0:
                    zero_rows(sp, T, table_l0, AGG, GROUPS - 2 + b, zeroed)
                store(GROUPS - 2 + b, b)
            for table_l0 in T.agg_l0:
                rows_dma(sp, table_l0[N:N + PARTS, :], T.zeros[:, 0:AGG], zeroed)
            sp.wait_ge(zeroed, (GROUPS + 1) * 2 * ROWS_DMA)
            sp.sem_inc(zeroed, -((GROUPS + 1) * 2 * ROWS_DMA))
            for b in range(2):
                sp.wait_ge(x_free[b], 1)
                sp.sem_inc(x_free[b], -1)
                sp.wait_ge(stored[b], ROWS_DMA)
                sp.sem_inc(stored[b], -ROWS_DMA)

        @block.vector
        def _(dve):
            dve.sem_inc(hT_free, 2)
            dve.sem_inc(psM_free, 2)

            def statistics(b):
                dve.wait_ge(loaded[b], ROWS_DMA)
                dve.sem_inc(loaded[b], -ROWS_DMA)
                layernorm_stats(chip, dve, lambda j: xin[:, b, j], stats, mv[:, b], var_ready)

            def messages(g, b):
                tiles = ds(g * GROUP, GROUP)
                nc.vector.tensor_tensor(T.same_src[:, tiles], T.srcq_i[:, tiles], bcast(T.src_i[:, tiles], PARTS),
                                        ALU.is_equal).then_inc(chip.sem("same_src_made"), 1)
                dve.wait_ge(stored[b], ROWS_DMA)
                dve.sem_inc(stored[b], -ROWS_DMA)
                for j in range(GROUP):
                    dve.wait_ge(psM_ready, 1)
                    dve.sem_inc(psM_ready, -1)
                    dve.sem_inc(hT_free, 1)
                    nc.vector.tensor_copy(stage[:, b, j], psM[j % 2][0:PARTS].rearrange("p a f -> p (a f)")).then_inc(done, 1)
                    dve.wait_ge(done, 1)
                    dve.sem_inc(done, -1)
                    dve.sem_inc(psM_free, 1)
                dve.sem_inc(stage_ready[b], 1)
                dve.wait_ge(chip.sem("dups_marked"), 1)
                dve.sem_inc(chip.sem("dups_marked"), -1)
                nc.vector.tensor_reduce(T.dup[:, tiles], T.earlier[:, tiles], AXIS.X, ALU.add).then_inc(done, 1)
                dve.wait_ge(done, 1)
                dve.sem_inc(done, -1)

            statistics(0)
            with dve.Fori(0, GROUPS // 2 - 1) as i:
                for b in range(2):
                    statistics(1 - b)
                    messages(i * 2 + b, b)
            statistics(1)
            messages(GROUPS - 2, 0)
            messages(GROUPS - 1, 1)
            dve.wait_ge(hT_free, 2)
            dve.sem_inc(hT_free, -2)
            dve.wait_ge(psM_free, 2)
            dve.sem_inc(psM_free, -2)

        @block.scalar
        def _(act):
            with act.Fori(0, GROUPS // 2) as i:
                for b in range(2):
                    act.wait_ge(normed, 1)
                    act.sem_inc(normed, -1)

                    def relu(j):
                        nc.scalar.activation(h[:, j % 2], xin[:, b, j], ACT.Relu, bias=shift[:, b, j:j + 1],
                                             scale=rstd[:, b, j:j + 1]).then_inc(h_ready, 1)
                    relu(0)
                    for j in range(GROUP):
                        if j + 1 < GROUP:
                            relu(j + 1)
                        act.wait_ge(psT_ready, 1)
                        act.sem_inc(psT_ready, -1)
                        act.wait_ge(hT_free, 1)
                        act.sem_inc(hT_free, -1)
                        nc.scalar.activation(hT[:, j % 2], psT[j % 2][:], ACT.Copy).then_inc(hT_ready, 1)

        @block.tensor
        def _(pe):
            with pe.Fori(0, GROUPS // 2) as i:
                for b in range(2):
                    def transpose(j):
                        pe.wait_ge(h_ready, 1)
                        pe.sem_inc(h_ready, -1)
                        if j == GROUP - 1:
                            pe.sem_inc(x_free[b], 1)
                        vectors = h[:, j % 2, B:D].rearrange("p (b c) -> p c b", c=3)
                        for c in range(4):
                            last = nc.tensor.transpose(psT[j % 2][:, c], h[:, j % 2, 0:B] if c == 0 else vectors[:, c - 1],
                                                       T.ident[0:PARTS, 0:PARTS])
                        last.then_inc(psT_ready, 1)

                    transpose(0)
                    for j in range(GROUP):
                        if j + 1 < GROUP:
                            transpose(j + 1)
                        pe.wait_ge(hT_ready, 1)
                        pe.sem_inc(hT_ready, -1)
                        pe.wait_ge(psM_free, 1)
                        pe.sem_inc(psM_free, -1)
                        for c in range(4):
                            last = nc.tensor.matmul(psM[j % 2][0:PARTS, c], hT[:, j % 2, c], W.in2f[:, min(c, 1)],
                                                    start=True, stop=True)
                        last.then_inc(psM_ready, 1)

        @block.gpsimd
        def _(pool):
            pooled = chip.sem("pool_done")
            for to, from_ in ((T.src_f, T.src_i), (T.dst_f, T.dst_ext)):
                nc.gpsimd.tensor_copy(to[:], from_[:]).then_inc(pooled, 1)
            pool.wait_ge(pooled, 2)
            pool.sem_inc(pooled, -2)

            def earlier(g):
                pool.wait_ge(chip.sem("same_src_made"), 1)
                pool.sem_inc(chip.sem("same_src_made"), -1)
                tiles = ds(g * GROUP, GROUP)
                nc.gpsimd.tensor_tensor(T.earlier[:, tiles], T.same_src[:, tiles],
                                        T.lower[:].unsqueeze(1).to_broadcast([PARTS, GROUP, PARTS]), ALU.mult)\
                    .then_inc(chip.sem("dups_marked"), 1)

            def scales(b):
                layernorm_scales(chip, pool, T, mv[:, b], rstd[:, b], shift[:, b], var_ready, normed)

            scales(0)
            with pool.Fori(0, GROUPS // 2 - 1) as i:
                for b in range(2):
                    scales(1 - b)
                    earlier(i * 2 + b)
            scales(1)
            earlier(GROUPS - 2)
            earlier(GROUPS - 1)

    with nc.Block() as block:

        @block.vector
        def _(dve):
            nc.vector.tensor_scalar(T.dup[:], T.dup[:], 1.0, None, ALU.min).then_inc(done, 1)
            nc.vector.tensor_scalar(T.tmp80[:], T.src_f[:], -1.0, T.spare[:, 0:1], ALU.mult, ALU.add).then_inc(done, 1)
            dve.wait_ge(done, 2)
            dve.sem_inc(done, -2)
            nc.vector.tensor_tensor(T.tmp80[:], T.tmp80[:], T.dup[:], ALU.mult).then_inc(done, 1)
            dve.wait_ge(done, 1)
            dve.sem_inc(done, -1)
            nc.vector.tensor_tensor(T.tmp80[:], T.tmp80[:], T.src_f[:], ALU.add).then_inc(done, 1)
            dve.wait_ge(done, 1)
            dve.sem_inc(done, -1)
            nc.vector.tensor_copy(T.scat_i[:], T.tmp80[:]).then_inc(done, 1)
            dve.wait_ge(done, 1)
            dve.sem_inc(done, -1)


def softplus_minus_log2(chip, act, dve, z_in, bias, mag, out, z_ready, mag_free, mag_ready, out_ready, freed):
    nc = chip.nc

    def scalar_half():
        done = chip.sem("act_done")
        act.wait_ge(z_ready, 1)
        act.sem_inc(z_ready, -1)
        act.wait_ge(mag_free, 1)
        act.sem_inc(mag_free, -1)
        nc.scalar.activation(mag, z_in, ACT.Abs, **({} if bias is None else {"bias": bias})).then_inc(done, 1)
        act.wait_ge(done, 1)
        act.sem_inc(done, -1)
        nc.scalar.activation(mag, mag, ACT.Exp, scale=-1.0).then_inc(done, 1)
        act.wait_ge(done, 1)
        act.sem_inc(done, -1)
        nc.scalar.activation(mag, mag, ACT.Ln, bias=1.0).then_inc(mag_ready, 1)

    def vector_half():
        done = chip.sem("dve_done")
        dve.wait_ge(mag_ready, 1)
        dve.sem_inc(mag_ready, -1)
        nc.vector.tensor_scalar(out, z_in, 0.0 if bias is None else bias, 0.0, ALU.add, ALU.max).then_inc(done, 1)
        dve.wait_ge(done, 1)
        dve.sem_inc(done, -1)
        nc.vector.scalar_tensor_tensor(out, mag, -LOG2, out, ALU.add, ALU.add).then_inc(done, 1)
        dve.wait_ge(done, 1)
        dve.sem_inc(done, -1)
        for s in (out_ready, mag_free, *freed):
            dve.sem_inc(s, 1)

    return scalar_half, vector_half


def l0_edges(chip, sb, ps, T, W, edge_radial):
    nc = chip.nc
    msg = sb("msg", [PARTS, 2, GROUP, MSG])
    gather_i = sb("gather_i", [PARTS, 2, GROUP], I32)
    scatter_i = sb("scatter_i", [PARTS, 2, GROUP], I32)
    radial = sb("radial", [R, 2, GROUP * PARTS])
    mag = sb("mag", [F, 2, GROUP * PARTS])
    hidden = sb("hidden", [F + 1, 2, GROUP * PARTS])
    filt = sb("filt", [PARTS, GROUP, 4, F])
    s_filt = sb("s_filt", [PARTS, GROUP, 2, F])
    v_filt = sb("v_filt", [PARTS, GROUP, 3, F])
    v_y = sb("v_y", [PARTS, GROUP, 3, F])
    dot = sb("dot", [PARTS, GROUP, F])
    edge = sb("edge", [PARTS, 2, GROUP, 8, F])
    summed = sb("summed", [PARTS, 2, GROUP, AGG])
    same = sb("same", [PARTS, 2, GROUP, PARTS])
    psH = ps("psH", 2, [F, GROUP * PARTS])
    psW = ps("psW", 2, [128, GROUP, 4 * F])
    psR = ps("psR", 4, [128, 2, AGG])
    done = chip.sem("dve_done")
    names = ("psH_free", "mag_free", "mag_ready", "hidden_ready", "psW_ready", "psW_free", "edge_ready", "edge_free",
             "psR_ready", "psR_free", "msg_free", "summed_ready", "summed_free", "psH_ready", "same_ready")
    s = {n: chip.sem(n) for n in names}
    radial_in, radial_free = chip.sem2("radial_in"), chip.sem2("radial_free")
    msg_in = [chip.counted(f"msg_in_{b}", 0)[0] for b in range(2)]
    added = [chip.counted(f"added_{b}", 0)[0] for b in range(2)]
    seen = chip.sem("seen")
    ones_ready = chip.sem("ones_ready")

    with nc.Block() as block:

        @block.sync
        def _(sp):
            def load(g, b):
                sp.wait_ge(radial_free[b], 1)
                sp.sem_inc(radial_free[b], -1)
                sp.dma_start(radial[:, b], edge_radial[:, ds(g * (GROUP * PARTS), GROUP * PARTS)]).then_inc(radial_in[b], 16)
            for b in range(2):
                sp.sem_inc(radial_free[b], 1)
            zeroed = chip.sem("zeroed")
            with sp.Fori(0, GROUPS // 2) as i:
                for b in range(2):
                    load(i * 2 + b, b)
                    zero_rows(sp, T, T.agg, D, i * 2 + b, zeroed)
            rows_dma(sp, T.agg[N:N + PARTS, :], T.zeros[:, 0:D], zeroed)
            sp.wait_ge(zeroed, (GROUPS + 1) * ROWS_DMA)
            sp.sem_inc(zeroed, -((GROUPS + 1) * ROWS_DMA))
            for b in range(2):
                sp.wait_ge(radial_free[b], 1)
                sp.sem_inc(radial_free[b], -1)

        @block.tensor
        def _(pe):
            def hidden_of(g, b):
                pe.wait_ge(radial_in[b], 16)
                pe.sem_inc(radial_in[b], -16)
                pe.wait_ge(s["psH_free"], 1)
                pe.sem_inc(s["psH_free"], -1)
                nc.tensor.matmul(psH[b][:], W.w1[:], radial[:, b], start=True, stop=True).then_inc(s["psH_ready"], 1)

            def filters(g, b):
                pe.wait_ge(s["hidden_ready"], 1)
                pe.sem_inc(s["hidden_ready"], -1)
                pe.wait_ge(s["psW_free"], 1)
                pe.sem_inc(s["psW_free"], -1)
                for j in range(GROUP):
                    last = nc.tensor.matmul(psW[b][0:PARTS, j], hidden[:, b, j * PARTS:(j + 1) * PARTS], W.w2[:, 0:4 * F],
                                            start=True, stop=True)
                last.then_inc(s["psW_ready"], 1)

            def sums(g, b):
                pe.wait_ge(s["edge_ready"], 1)
                pe.sem_inc(s["edge_ready"], -1)
                pe.wait_ge(s["same_ready"], 1)
                pe.sem_inc(s["same_ready"], -1)
                pe.wait_ge(s["psR_free"], 1)
                pe.sem_inc(s["psR_free"], -1)
                for j in range(GROUP):
                    last = nc.tensor.matmul(psR[2 * b + j // 2][0:PARTS, j % 2], same[:, b, j],
                                            edge[:, b, j].rearrange("p a f -> p (a f)"), start=True, stop=True)
                last.then_inc(s["psR_ready"], 1)

            pe.wait_ge(ones_ready, 1)
            pe.sem_inc(ones_ready, -1)
            hidden_of(0, 0)
            hidden_of(1, 1)
            filters(0, 0)
            with pe.Fori(0, GROUPS // 2 - 1) as i:
                for b in range(2):
                    hidden_of(i * 2 + b + 2, b)
                    filters(i * 2 + b + 1, 1 - b)
                    sums(i * 2 + b, b)
            filters(GROUPS - 1, 1)
            sums(GROUPS - 2, 0)
            sums(GROUPS - 1, 1)

        def halves(act, dve, b):
            return softplus_minus_log2(chip, act, dve, psH[b][:], W.b1[:, 0:1], mag[:, b], hidden[0:F, b],
                                       s["psH_ready"], s["mag_free"], s["mag_ready"], s["hidden_ready"], [s["psH_free"]])

        @block.scalar
        def _(act):
            act.sem_inc(s["psR_free"], 2)
            act.sem_inc(s["edge_free"], 2)

            def softplus(g, b):
                halves(act, None, b)[0]()
                act.sem_inc(radial_free[b], 1)

            def equal_sources(g, b):
                nc.scalar.activation(same[:, b], T.same_src[:, ds(g * GROUP, GROUP)], ACT.Copy).then_inc(s["same_ready"], 1)

            def evacuate(g, b):
                act.wait_ge(s["psR_ready"], 1)
                act.sem_inc(s["psR_ready"], -1)
                act.sem_inc(s["edge_free"], 1)
                act.wait_ge(s["summed_free"], 1)
                act.sem_inc(s["summed_free"], -1)
                adone = chip.sem("act_done")
                for k in range(2):
                    nc.scalar.activation(summed[:, b, 2 * k:2 * k + 2], psR[2 * b + k][0:PARTS], ACT.Copy).then_inc(adone, 1)
                act.wait_ge(adone, 2)
                act.sem_inc(adone, -2)
                act.sem_inc(s["psR_free"], 1)
                act.sem_inc(s["summed_ready"], 1)

            for b in range(2):
                softplus(b, b)
                equal_sources(b, b)
            with act.Fori(0, GROUPS // 2 - 1) as i:
                for b in range(2):
                    softplus(i * 2 + b + 2, b)
                    evacuate(i * 2 + b, b)
                    equal_sources(i * 2 + b + 2, b)
            evacuate(GROUPS - 2, 0)
            evacuate(GROUPS - 1, 1)
            act.wait_ge(s["psR_free"], 2)
            act.sem_inc(s["psR_free"], -2)
            act.wait_ge(s["summed_free"], 2)
            act.sem_inc(s["summed_free"], -2)

        @block.vector
        def _(dve):
            nc.vector.memset(hidden[F:F + 1], 1.0).then_inc(done, 1)
            dve.wait_ge(done, 1)
            dve.sem_inc(done, -1)
            dve.sem_inc(s["psH_free"], 2)
            dve.sem_inc(s["mag_free"], 2)
            dve.sem_inc(s["psW_free"], 2)
            dve.sem_inc(s["msg_free"], 2)
            dve.sem_inc(ones_ready, 1)

            def half(g, b):
                halves(None, dve, b)[1]()

            def products(g, b, i):
                tiles = ds(g * GROUP, GROUP)
                ys = T.y[:, tiles, 0]
                ys3 = bcast(bcast(ys, 3), F)
                yv = bcast(T.y[:, tiles, 1:4], F)
                rcut = T.rcut[:, tiles]
                dve.wait_ge(s["psW_ready"], 1)
                dve.sem_inc(s["psW_ready"], -1)
                nc.vector.tensor_tensor(filt[:].rearrange("p j k f -> p j (k f)"), psW[b][0:PARTS], bcast(rcut, 4 * F),
                                        ALU.mult).then_inc(done, 1)
                dve.wait_ge(done, 1)
                dve.sem_inc(done, -1)
                dve.sem_inc(s["psW_free"], 1)
                dve.wait_ge(msg_in[b], i * (16 * GROUP) + 16 * GROUP)
                dve.sem_inc(seen, 1)
                m = msg[:, b].rearrange("p j (k f) -> p j k f", k=4)
                scalars = m[:, :, 0:1].to_broadcast([PARTS, GROUP, 2, F])
                nc.vector.tensor_tensor(s_filt[:], scalars, filt[:, :, 0:3:2], ALU.mult).then_inc(done, 1)
                nc.vector.tensor_tensor(v_filt[:], m[:, :, 1:4], filt[:, :, 3:4].to_broadcast([PARTS, GROUP, 3, F]),
                                        ALU.mult).then_inc(done, 1)
                nc.vector.tensor_tensor(v_y[:], m[:, :, 1:4], yv, ALU.mult).then_inc(done, 1)
                dve.wait_ge(done, 3)
                dve.sem_inc(done, -3)
                dve.sem_inc(s["msg_free"], 1)
                dve.wait_ge(s["edge_free"], 1)
                dve.sem_inc(s["edge_free"], -1)
                out = edge[:, b]
                nc.vector.tensor_tensor(out[:, :, 0], s_filt[:, :, 0], bcast(ys, F), ALU.mult).then_inc(done, 1)
                nc.vector.tensor_tensor(out[:, :, 2:8:2], s_filt[:, :, 1:2].to_broadcast([PARTS, GROUP, 3, F]), yv,
                                        ALU.mult).then_inc(done, 1)
                nc.vector.tensor_tensor(out[:, :, 3:8:2], v_filt[:], ys3, ALU.mult).then_inc(done, 1)
                nc.vector.tensor_reduce(dot[:], v_y[:].rearrange("p j c f -> p j f c"), AXIS.X, ALU.add).then_inc(done, 1)
                dve.wait_ge(done, 4)
                dve.sem_inc(done, -4)
                nc.vector.scalar_tensor_tensor(out[:, :, 1], dot[:], 1.0 / math.sqrt(3.0), filt[:, :, 1], ALU.mult,
                                               ALU.mult).then_inc(done, 1)
                dve.wait_ge(done, 1)
                dve.sem_inc(done, -1)
                dve.sem_inc(s["edge_ready"], 1)

            half(0, 0)
            half(1, 1)
            with dve.Fori(0, GROUPS // 2 - 1) as i:
                for b in range(2):
                    products(i * 2 + b, b, i)
                    half(i * 2 + b + 2, b)
            for b in range(2):
                products(GROUPS - 2 + b, b, GROUPS // 2 - 1)
            dve.wait_ge(s["psH_free"], 2)
            dve.sem_inc(s["psH_free"], -2)
            dve.wait_ge(s["mag_free"], 2)
            dve.sem_inc(s["mag_free"], -2)
            dve.wait_ge(s["psW_free"], 2)
            dve.sem_inc(s["psW_free"], -2)
            dve.wait_ge(s["edge_free"], 2)
            dve.sem_inc(s["edge_free"], -2)
            dve.wait_ge(s["msg_free"], 2)
            dve.sem_inc(s["msg_free"], -2)

        @block.gpsimd
        def _(pool):
            pooled = chip.sem("pool_done")
            pool.sem_inc(s["summed_free"], 2)

            def gather(g, b):
                pool.wait_ge(s["msg_free"], 1)
                pool.sem_inc(s["msg_free"], -1)
                nc.gpsimd.tensor_copy(gather_i[:, b], T.dst_ext[:, ds(g * GROUP + 1, GROUP)]).then_inc(pooled, 1)
                pool.wait_ge(pooled, 1)
                pool.sem_inc(pooled, -1)
                for j in range(GROUP):
                    nc.gpsimd.indirect_dma_start(out=msg[:, b, j], out_offset=None, in_=T.messages[:, :],
                                                 in_offset=bass.IndirectOffsetOnAxis(ap=gather_i[:, b, j:j + 1], axis=0),
                                                 bounds_check=N - 1).then_inc(msg_in[b], 16)

            def scatter(g, b, first):
                nc.gpsimd.tensor_copy(scatter_i[:, b], T.scat_i[:, ds(g * GROUP, GROUP)]).then_inc(pooled, 1)
                pool.wait_ge(pooled, 1)
                pool.sem_inc(pooled, -1)
                pool.wait_ge(s["summed_ready"], 1)
                pool.sem_inc(s["summed_ready"], -1)
                for j in range(GROUP):
                    if not (first and j < 2):
                        pool.wait_ge(added[j % 2], g * 32 + 16 * (j // 2))
                        pool.sem_inc(seen, 1)
                    if j == 1 and not first:
                        pool.sem_inc(s["summed_free"], 1)
                    nc.gpsimd.indirect_dma_start(out=T.agg_l0[j % 2][:, :],
                                                 out_offset=bass.IndirectOffsetOnAxis(ap=scatter_i[:, b, j:j + 1], axis=0),
                                                 in_=summed[:, b, j], in_offset=None, bounds_check=N + PARTS - 1,
                                                 compute_op=ALU.add).then_inc(added[j % 2], 16)

            gather(0, 0)
            gather(1, 1)
            scatter(0, 0, True)
            with pool.Fori(0, GROUPS // 2 - 1) as i:
                for k, b in enumerate((1, 0)):
                    gather(i * 2 + k + 2, 1 - b)
                    scatter(i * 2 + k + 1, b, False)
            scatter(GROUPS - 1, 1, False)
            for b in range(2):
                pool.wait_ge(added[b], GROUPS * 32)
            pool.sem_inc(s["summed_free"], 1)


def l0_nodes(chip, sb, ps, x, T, W, xT):
    nc = chip.nc
    agg, other = sb("agg_rows", [PARTS, 2, GROUP, AGG]), sb("other_rows", [PARTS, GROUP, AGG])
    xin = sb("xin_d", [PARTS, 2, GROUP, D])
    aT = sb("aT", [128, 2, 2, GROUP * PARTS])
    mag = sb("mag_d", [128, GROUP * PARTS])
    os1 = sb("os1", [128, 2, GROUP * PARTS])
    stats, mv = sb("stats_d", [PARTS, GROUP, 6]), sb("mv_d", [PARTS, 2, GROUP, 2])
    rstd, shift = sb("rstd_d", [PARTS, 2, GROUP]), sb("shift_d", [PARTS, 2, GROUP])
    h = sb("h_d", [PARTS, 2, D])
    psA = ps("psA", 1, [128, 2, 512])[0]
    psO = ps("psO", 1, [128, GROUP * PARTS])[0]
    psX = ps("psX", 2, [128, 4, B])
    psT = ps("psT_d", 2, [128, KC, PARTS])
    done = chip.sem("dve_done")
    names = ("asum_ready", "psA_ready", "aT_ready", "aT_free", "psO_ready", "mag_free", "mag_ready", "os1_ready",
             "psX_ready", "psX_free", "normed", "h_ready", "psT_ready", "psT_free", "other_free")
    s = {n: chip.sem(n) for n in names}
    agg_in, agg_free = chip.sem2("agg_in"), chip.sem2("agg_free")
    var_ready = chip.sem("var_ready")
    x_in, x_free, x1_ready, x1_out = (chip.sem2(n) for n in ("x_loaded", "x_free", "x1_ready", "stored"))
    tA, tB, tx, tx1 = (tiles_of(a) for a in (T.agg_l0[0][0:N, :], T.agg_l0[1][0:N, :], x, T.x1))

    with nc.Block() as block:

        @block.sync
        def _(sp):
            def load_agg(g, b):
                sp.wait_ge(agg_free[b], 1)
                sp.sem_inc(agg_free[b], -1)
                rows_dma(sp, agg[:, b], tA[:, ds(g * GROUP, GROUP)], agg_in[b])
                sp.wait_ge(s["other_free"], 1)
                sp.sem_inc(s["other_free"], -1)
                rows_dma(sp, other[:], tB[:, ds(g * GROUP, GROUP)], agg_in[b])

            def load_x(g, b):
                sp.wait_ge(x_free[b], 1)
                sp.sem_inc(x_free[b], -1)
                sp.wait_ge(x1_out[b], ROWS_DMA)
                sp.sem_inc(x1_out[b], -ROWS_DMA)
                rows_dma(sp, xin[:, b], tx[:, ds(g * GROUP, GROUP)], x_in[b])

            def store(g, b):
                sp.wait_ge(x1_ready[b], 1)
                sp.sem_inc(x1_ready[b], -1)
                rows_dma(sp, tx1[:, ds(g * GROUP, GROUP)], xin[:, b], x1_out[b])

            sp.sem_inc(s["other_free"], 1)
            for b in range(2):
                sp.sem_inc(agg_free[b], 1)
                sp.sem_inc(x_free[b], 1)
                sp.sem_inc(x1_out[b], ROWS_DMA)
                load_agg(b, b)
                load_x(b, b)
            load_agg(2, 0)
            load_agg(3, 1)
            store(0, 0)
            with sp.Fori(0, GROUPS // 2 - 2) as i:
                for k, b in enumerate((1, 0)):
                    load_agg(i * 2 + k + 4, 1 - b)
                    store(i * 2 + k + 1, b)
                    load_x(i * 2 + k + 2, 1 - b)
            store(GROUPS - 3, 1)
            load_x(GROUPS - 2, 0)
            store(GROUPS - 2, 0)
            load_x(GROUPS - 1, 1)
            store(GROUPS - 1, 1)
            sp.wait_ge(s["other_free"], 1)
            sp.sem_inc(s["other_free"], -1)
            for b in range(2):
                sp.wait_ge(agg_free[b], 1)
                sp.sem_inc(agg_free[b], -1)
                sp.wait_ge(x_free[b], 1)
                sp.sem_inc(x_free[b], -1)
                sp.wait_ge(x1_out[b], ROWS_DMA)
                sp.sem_inc(x1_out[b], -ROWS_DMA)

        @block.tensor
        def _(pe):
            def out_product(b, j):
                cols = slice(j * PARTS, (j + 1) * PARTS)
                pe.wait_ge(s["psX_free"], 1)
                pe.sem_inc(s["psX_free"], -1)
                nc.tensor.matmul(psX[j % 2][0:PARTS, 0], os1[:, b, cols], W.f2o2_s[:], start=True, stop=True)
                for c, (half, blk) in enumerate(((1, 0), (0, 1), (1, 1))):
                    last = nc.tensor.matmul(psX[j % 2][0:PARTS, 1 + c], aT[:, b, blk, cols], W.vec[:, half],
                                            start=True, stop=True)
                last.then_inc(s["psX_ready"], 1)

            def agg_transposes(b):
                pe.wait_ge(s["asum_ready"], 1)
                pe.sem_inc(s["asum_ready"], -1)
                for blk in range(2):
                    for j in range(GROUP):
                        last = nc.tensor.transpose(psA[:, blk, j * PARTS:(j + 1) * PARTS],
                                                   agg[:, b, j, blk * 128:(blk + 1) * 128], T.ident[0:PARTS, 0:PARTS])
                last.then_inc(s["psA_ready"], 1)

            def scalars(b):
                pe.wait_ge(s["aT_ready"], 1)
                pe.sem_inc(s["aT_ready"], -1)
                pe.sem_inc(agg_free[b], 1)
                nc.tensor.matmul(psO[:], W.f2o1_s[:], aT[:, b, 0], start=True, stop=True).then_inc(s["psO_ready"], 1)

            def h_transpose(j):
                pe.wait_ge(s["h_ready"], 1)
                pe.sem_inc(s["h_ready"], -1)
                pe.wait_ge(s["psT_free"], 1)
                pe.sem_inc(s["psT_free"], -1)
                for c in range(KC):
                    last = nc.tensor.transpose(psT[j % 2][:, c], h[:, j % 2, c * 128:(c + 1) * 128],
                                               T.ident[0:PARTS, 0:PARTS])
                last.then_inc(s["psT_ready"], 1)

            def step(b, first=False, left=2):
                if left > 1:
                    agg_transposes(b)
                for j in range(GROUP):
                    out_product(b, j)
                if left > 0:
                    pe.wait_ge(s["os1_ready"], 1)
                    pe.sem_inc(s["os1_ready"], -1)
                if left > 1:
                    scalars(b)
                if not first:
                    for j in range(GROUP):
                        h_transpose(j)

            agg_transposes(0)
            scalars(0)
            agg_transposes(1)
            pe.wait_ge(s["os1_ready"], 1)
            pe.sem_inc(s["os1_ready"], -1)
            scalars(1)
            step(0, first=True)
            with pe.Fori(0, GROUPS // 2 - 2):
                step(1)
                step(0)
            step(1)
            step(0, left=1)
            step(1, left=0)
            for j in range(GROUP):
                h_transpose(j)

        def halves(act, dve, b):
            return softplus_minus_log2(chip, act, dve, psO[:], None, mag[:], os1[:, b], s["psO_ready"], s["mag_free"],
                                       s["mag_ready"], s["os1_ready"], [])

        @block.scalar
        def _(act):
            act.sem_inc(s["psT_free"], 2)
            adone = chip.sem("act_done")

            def agg_columns(b):
                act.wait_ge(s["psA_ready"], 1)
                act.sem_inc(s["psA_ready"], -1)
                act.wait_ge(s["aT_free"], 1)
                act.sem_inc(s["aT_free"], -1)
                nc.scalar.activation(aT[:, b], psA[:, :, 0:GROUP * PARTS], ACT.Copy).then_inc(s["aT_ready"], 1)

            def back(g, b):
                act.wait_ge(s["normed"], 1)
                act.sem_inc(s["normed"], -1)

                def relu(j):
                    nc.scalar.activation(h[:, j % 2], xin[:, b, j], ACT.Relu, bias=shift[:, b, j:j + 1],
                                         scale=rstd[:, b, j:j + 1]).then_inc(s["h_ready"], 1)
                relu(0)
                for j in range(GROUP):
                    if j + 1 < GROUP:
                        relu(j + 1)
                    act.wait_ge(s["psT_ready"], 1)
                    act.sem_inc(s["psT_ready"], -1)
                    if j == GROUP - 1:
                        act.sem_inc(x_free[b], 1)
                    nc.scalar.activation(xT[:, :, ds((g * GROUP + j) * PARTS, PARTS)], psT[j % 2][:], ACT.Copy)\
                        .then_inc(adone, 1)
                    if j > 0:
                        act.wait_ge(adone, 1)
                        act.sem_inc(adone, -1)
                        act.sem_inc(s["psT_free"], 1)
                act.wait_ge(adone, 1)
                act.sem_inc(adone, -1)
                act.sem_inc(s["psT_free"], 1)

            agg_columns(0)
            halves(act, None, 0)[0]()
            agg_columns(1)
            halves(act, None, 1)[0]()
            agg_columns(0)
            with act.Fori(0, GROUPS // 2 - 2) as i:
                for k, b in enumerate((1, 0)):
                    halves(act, None, 1 - b)[0]()
                    agg_columns(b)
                    back(i * 2 + k, 1 - b)
            halves(act, None, 0)[0]()
            agg_columns(1)
            back(GROUPS - 4, 0)
            halves(act, None, 1)[0]()
            back(GROUPS - 3, 1)
            back(GROUPS - 2, 0)
            back(GROUPS - 1, 1)
            act.wait_ge(s["psT_free"], 2)
            act.sem_inc(s["psT_free"], -2)

        @block.gpsimd
        def _(pool):
            with pool.Fori(0, GROUPS // 2):
                for b in range(2):
                    layernorm_scales(chip, pool, T, mv[:, b], rstd[:, b], shift[:, b], var_ready, s["normed"])

        @block.vector
        def _(dve):
            dve.sem_inc(s["psX_free"], 2)
            dve.sem_inc(s["mag_free"], 1)
            dve.sem_inc(s["aT_free"], 2)

            def sum_tables(b):
                dve.wait_ge(agg_in[b], 2 * ROWS_DMA)
                dve.sem_inc(agg_in[b], -(2 * ROWS_DMA))
                nc.vector.tensor_tensor(agg[:, b], agg[:, b], other[:], ALU.add).then_inc(done, 1)
                dve.wait_ge(done, 1)
                dve.sem_inc(done, -1)
                dve.sem_inc(s["asum_ready"], 1)
                dve.sem_inc(s["other_free"], 1)

            def output(b):
                dve.wait_ge(x_in[b], ROWS_DMA)
                dve.sem_inc(x_in[b], -ROWS_DMA)
                for j in range(GROUP):
                    dve.wait_ge(s["psX_ready"], 1)
                    dve.sem_inc(s["psX_ready"], -1)
                    if j == GROUP - 1:
                        dve.sem_inc(s["aT_free"], 1)
                    xs, xv = xin[:, b, j, 0:B], xin[:, b, j, B:D].rearrange("p (b c) -> p b c", c=3)
                    out = psX[j % 2][0:PARTS]
                    nc.vector.tensor_tensor(xs, out[:, 0], xs, ALU.add).then_inc(done, 1)
                    nc.vector.tensor_tensor(xv, out[:, 1:4].rearrange("p c b -> p b c"), xv, ALU.add).then_inc(done, 1)
                    dve.wait_ge(done, 2)
                    dve.sem_inc(done, -2)
                    dve.sem_inc(s["psX_free"], 1)
                dve.sem_inc(x1_ready[b], 1)

            def statistics(b):
                layernorm_stats(chip, dve, lambda j: xin[:, b, j], stats, mv[:, b], var_ready)

            def scalars(b):
                halves(None, dve, b)[1]()

            sum_tables(0)
            sum_tables(1)
            scalars(0)
            with dve.Fori(0, GROUPS // 2 - 1):
                for b in range(2):
                    sum_tables(b)
                    output(b)
                    scalars(1 - b)
                    statistics(b)
            output(0)
            scalars(1)
            statistics(0)
            output(1)
            statistics(1)
            dve.wait_ge(s["psX_free"], 2)
            dve.sem_inc(s["psX_free"], -2)
            dve.wait_ge(s["mag_free"], 1)
            dve.sem_inc(s["mag_free"], -1)
            dve.wait_ge(s["aT_free"], 2)
            dve.sem_inc(s["aT_free"], -2)


def attention_masks(chip, sb, ps, T, dst_tiled):
    nc = chip.nc
    alike = sb("alike", [PARTS, TILES + 1])
    ends_i, ends = sb("ends_i", [HEADS, 2, PARTS], I32), sb("ends", [HEADS, 2, PARTS])
    from_before, base, cont_end, ends_here = (sb(n, [PARTS, TILES if k < 2 else 1]) for k, n in
                                              enumerate(("from_before", "base", "cont_end", "ends_here")))
    whole = sb("whole", [HEADS, PARTS])
    key, first, fix = sb("key", [PARTS, 1]), sb("first", [PARTS, 1]), sb("fix", [PARTS, 1])
    psF = ps("psF", 1, [128, PARTS])[0]
    done, first_ready = chip.sem("dve_done"), chip.sem("first_ready")

    with nc.Block() as block:

        @block.sync
        def _(sp):
            for n, tile in enumerate((0, TILES - 1)):
                sp.dma_start(ends_i[:, n], dst_tiled[tile:tile + 1, :].to_broadcast([HEADS, PARTS])).then_inc(chip.sem("ends_in"), 16)

        @block.tensor
        def _(pe):
            pe.wait_ge(first_ready, 1)
            pe.sem_inc(first_ready, -1)
            nc.tensor.matmul(psF[0:PARTS], first[:].to_broadcast([PARTS, PARTS]), T.ident[0:PARTS, 0:PARTS],
                             start=True, stop=True).then_inc(chip.sem("psF_ready"), 1)

        @block.vector
        def _(dve):
            def do(*steps):
                for step in steps:
                    step.then_inc(done, 1)
                dve.wait_ge(done, len(steps))
                dve.sem_inc(done, -(len(steps)))
            tt, ts, stt = nc.vector.tensor_tensor, nc.vector.tensor_scalar, nc.vector.scalar_tensor_tensor
            d = T.dst_f
            last = TILES - 1
            dve.wait_ge(chip.sem("ends_in"), 32)
            dve.sem_inc(chip.sem("ends_in"), -32)
            do(tt(alike[:], d[:, 0:TILES + 1], d[:, 1:TILES + 2], ALU.is_equal),
               nc.vector.tensor_copy(ends[:], ends_i[:]))
            do(nc.vector.tensor_copy(T.same[:], alike[:, 0:TILES]), nc.vector.tensor_copy(T.same_next[:], alike[:, 1:TILES + 1]),
               nc.vector.tensor_copy(cont_end[:], alike[:, TILES:TILES + 1]))
            do(nc.vector.memset(T.same[:, 0:1], 0.0), nc.vector.memset(T.same_next[:, last:TILES], 0.0))
            do(ts(T.same_neg[:], T.same[:], -NEG, NEG, ALU.mult, ALU.add),
               ts(T.next_neg[:], T.same_next[:], -NEG, NEG, ALU.mult, ALU.add),
               nc.vector.tensor_tensor_scan(from_before[:], alike[:, 0:TILES], alike[:, 0:TILES], 1.0, ALU.mult, ALU.min),
               ts(base[:], d[:, 1:TILES + 1], -1.0, T.spare[:, 0:1], ALU.mult, ALU.add),
               stt(key[:], d[:, TILES:TILES + 1], 1.0, cont_end[:], ALU.add, ALU.mult))
            do(tt(base[:], base[:], from_before[:], ALU.mult), ts(key[:], key[:], -1.0, None, ALU.add),
               tt(ends_here[:], from_before[:, last:TILES], cont_end[:], ALU.mult))
            do(tt(base[:], base[:], d[:, 1:TILES + 1], ALU.add),
               tt(ends_here[:], alike[:, 0:1], ends_here[:], ALU.subtract))
            do(stt(base[:], alike[:, 1:TILES + 1], FAR, base[:], ALU.mult, ALU.add),
               stt(first[:], d[:, 1:2], 2.0, ends_here[:], ALU.add, ALU.mult),
               ts(fix[:], ends_here[:], -FAR, FAR, ALU.mult, ALU.add))
            do(nc.vector.tensor_copy(T.row_i[:], base[:]), ts(first[:], first[:], -2.0, None, ALU.add),
               tt(fix[:], fix[:], d[:, 1:2], ALU.add))
            dve.sem_inc(first_ready, 1)
            do(nc.vector.tensor_copy(T.fix_i[:], fix[:]))
            cont = T.cont
            do(nc.vector.memset(cont[:], 0.0))
            do(tt(cont[:, 1:PARTS], ends[:, 1, 0:PARTS - 1], ends[:, 0, 1:PARTS], ALU.is_equal),
               tt(whole[:], ends[:, 0], ends[:, 1], ALU.is_equal))
            do(tt(T.pass_fwd[:], cont[:, 0:PARTS], whole[:], ALU.mult), tt(T.pass_bwd[:], cont[:, 1:PARTS + 1], whole[:], ALU.mult))
            dve.wait_ge(chip.sem("psF_ready"), 1)
            dve.sem_inc(chip.sem("psF_ready"), -1)
            do(ts(T.carry[:], psF[0:PARTS], key[:, 0:1], None, ALU.is_equal))


def project(chip, sb, ps, T, xT, weight, bias, table, scores):
    nc = chip.nc
    w_high, w_low = sb("w_high", [128, KC, D], F32R), sb("w_low", [128, KC, D], F32R)
    bias_row = None if bias is None else sb("bias_row", [PARTS, D])
    psP = ps("psP", 2, [128, D])
    table_t = tiles_of(table)
    done, adone = chip.sem("dve_done"), chip.sem("act_done")
    names = ("high_done", "split_ready", "split_free", "psP_ready", "psP_free", "w_ready")
    s = {n: chip.sem(n) for n in names}
    row_ready, row_out = chip.sem2("row_ready"), chip.sem2("row_out")

    with ExitStack() as stack:
        raw = stack.enter_context(nc.sbuf_tensor(chip.unique("w_raw"), [128, KC, D], F32))
        with nc.Block() as block:

            @block.sync
            def _(sp):
                sp.dma_start(raw[:], weight.rearrange("(c k) n -> k c n", c=KC)).then_inc(chip.sem("w_in"), 16)
                if bias is not None:
                    sp.dma_start(bias_row[:], bias.unsqueeze(0).to_broadcast([PARTS, D])).then_inc(chip.sem("bias_in"), 16)
                    sp.wait_ge(chip.sem("bias_in"), 16)
                    sp.sem_inc(chip.sem("bias_in"), -16)

            @block.scalar
            def _(act):
                act.wait_ge(chip.sem("w_in"), 16)
                act.sem_inc(chip.sem("w_in"), -16)
                nc.scalar.activation(w_high[:], raw[:], ACT.Copy).then_inc(s["w_ready"], 1)

            @block.vector
            def _(dve):
                dve.wait_ge(s["w_ready"], 1)
                dve.sem_inc(s["w_ready"], -1)
                nc.vector.tensor_tensor(w_low[:], raw[:], w_high[:], ALU.subtract).then_inc(done, 1)
                dve.wait_ge(done, 1)
                dve.sem_inc(done, -1)

    x_high, x_low = sb("x_high", [128, 2, KC, PARTS], F32R), sb("x_low", [128, 2, KC, PARTS], F32R)
    row = sb("row", [PARTS, 2, D])
    if scores is not None:
        on_pool, on_vector_tile, on_vector_end, on_tensor_end, on_scalar_end = scores(chip, sb, ps, T)

    with nc.Block() as block:

        @block.sync
        def _(sp):
            for b in range(2):
                sp.sem_inc(row_out[b], ROWS_DMA)
            with sp.Fori(0, TILES // 2) as i:
                for b in range(2):
                    sp.wait_ge(row_ready[b], 1)
                    sp.sem_inc(row_ready[b], -1)
                    rows_dma(sp, table_t[:, ds(i * 2 + b, 1)].rearrange("p a d -> p (a d)"), row[:, b], row_out[b])
            for b in range(2):
                sp.wait_ge(row_out[b], ROWS_DMA)
                sp.sem_inc(row_out[b], -ROWS_DMA)

        @block.scalar
        def _(act):
            act.sem_inc(s["psP_free"], 2)

            def split(t, b):
                act.wait_ge(s["split_free"], 1)
                act.sem_inc(s["split_free"], -1)
                xs = xT[:, :, ds(t * PARTS, PARTS)]
                nc.scalar.activation(x_high[:, b], xs, ACT.Copy).then_inc(s["high_done"], 1)

            def evacuate(t, b):
                act.wait_ge(s["psP_ready"], 1)
                act.sem_inc(s["psP_ready"], -1)
                act.sem_inc(s["split_free"], 1)
                act.wait_ge(row_out[b], ROWS_DMA)
                act.sem_inc(row_out[b], -ROWS_DMA)
                nc.scalar.activation(row[:, b], psP[b][0:PARTS], ACT.Copy).then_inc(adone, 1)
                act.wait_ge(adone, 1)
                act.sem_inc(adone, -1)
                act.sem_inc(s["psP_free"], 1)
                act.sem_inc(row_ready[b] if bias is None else chip.sem("to_bias"), 1)

            act.sem_inc(s["split_free"], 2)
            split(0, 0)
            split(1, 1)
            with act.Fori(0, TILES // 2 - 1) as i:
                for b in range(2):
                    evacuate(i * 2 + b, b)
                    split(i * 2 + b + 2, b)
            evacuate(TILES - 2, 0)
            evacuate(TILES - 1, 1)
            act.wait_ge(s["psP_free"], 2)
            act.sem_inc(s["psP_free"], -2)
            act.wait_ge(s["split_free"], 2)
            act.sem_inc(s["split_free"], -2)
            if scores is not None:
                on_scalar_end(act)

        @block.gpsimd
        def _(pool):
            if scores is not None:
                on_pool(pool)
            if bias is not None:
                with pool.Fori(0, TILES // 2) as i:
                    for b in range(2):
                        pool.wait_ge(chip.sem("to_bias"), 1)
                        pool.sem_inc(chip.sem("to_bias"), -1)
                        nc.gpsimd.tensor_tensor(row[:, b], row[:, b], bias_row[:], ALU.add).then_inc(row_ready[b], 1)

        @block.vector
        def _(dve):
            def split(t, b):
                dve.wait_ge(s["high_done"], 1)
                dve.sem_inc(s["high_done"], -1)
                xs = xT[:, :, ds(t * PARTS, PARTS)]
                nc.vector.tensor_tensor(x_low[:, b], xs, x_high[:, b], ALU.subtract).then_inc(s["split_ready"], 1)

            if scores is None:
                with dve.Fori(0, TILES // 2) as i:
                    for b in range(2):
                        split(i * 2 + b, b)
            else:
                turn = 2 * SLOTS
                with dve.Fori(0, TILES // turn) as i:
                    for n in range(turn):
                        split(i * turn + n, n % 2)
                        on_vector_tile(dve, i * turn + n, n % SLOTS, i * 2 + n // SLOTS)
                for n in range(TILES % turn):
                    split(TILES // turn * turn + n, n % 2)
                    on_vector_tile(dve, TILES // turn * turn + n, n % SLOTS, TILES // turn * 2 + n // SLOTS)
                on_vector_end(dve)

        @block.tensor
        def _(pe):
            with pe.Fori(0, TILES // 8):
                for b in (0, 1) * 4:
                    pe.wait_ge(s["split_ready"], 1)
                    pe.sem_inc(s["split_ready"], -1)
                    pe.wait_ge(s["psP_free"], 1)
                    pe.sem_inc(s["psP_free"], -1)
                    parts = [(x, w, c) for c in range(KC)
                             for x, w in ((x_high, w_high), (x_high, w_low), (x_low, w_high))]
                    for n, (x, w, c) in enumerate(parts):
                        last = nc.tensor.matmul(psP[b][0:PARTS], x[:, b, c], w[:, c], start=n == 0,
                                                stop=n == len(parts) - 1)
                    last.then_inc(s["psP_ready"], 1)
            if scores is not None:
                on_tensor_end(pe)


def scores_and_softmax(chip, sb, ps, T):
    nc = chip.nc
    q, k = sb("q_rows", [PARTS, SLOTS, D]), sb("k_rows", [PARTS, SLOTS, D])
    index = sb("index", [PARTS, SLOTS, 2], I32)
    score = T.weight
    work = [x[:].rearrange("p b d -> p (b d)")[:, 0:HEADS * TILES].rearrange("p (h t) -> p h t", h=HEADS)
            for x in (q, k)]
    edge_cols = sb("edge_cols", [PARTS, 2, HEADS])
    over = q[0:HEADS].rearrange("p b d -> p (b d)")[:, HEADS * TILES:HEADS * TILES + 6 * PARTS]\
        .rearrange("p (n q) -> p n q", n=6)
    masks = k[0:HEADS].rearrange("p b d -> p (b d)")[:, HEADS * TILES:HEADS * TILES + 3 * PARTS]\
        .rearrange("p (n q) -> p n q", n=3)
    psS = ps("psS", 1, [HEADS, 2, PARTS])[0]
    psC = ps("psC", 1, [128, 2, HEADS])[0]
    done = chip.sem("dve_done")
    came, before = zip(*(chip.counted(f"qk_in_{b}", len(range(b, TILES, SLOTS)) * 32) for b in range(SLOTS)))
    free, seen, pooled = chip.sem("qk_free"), chip.sem("seen"), chip.sem("pool_done")
    cols_ready, psS_ready, rows_ready, psC_ready = (chip.sem(n) for n in ("cols_ready", "psS_ready", "rows_ready", "psC_ready"))

    def on_pool(pool):
        pool.sem_inc(free, SLOTS)

        def gather(t, b):
            pool.wait_ge(free, 1)
            pool.sem_inc(free, -1)
            nc.gpsimd.tensor_copy(index[:, b, 0:1], T.dst_ext[:, ds(t + 1, 1)]).then_inc(pooled, 1)
            nc.gpsimd.tensor_copy(index[:, b, 1:2], T.src_i[:, ds(t, 1)]).then_inc(pooled, 1)
            pool.wait_ge(pooled, 2)
            pool.sem_inc(pooled, -2)
            for n, (rows, table) in enumerate(((q, T.q), (k, T.k))):
                nc.gpsimd.indirect_dma_start(out=rows[:, b], out_offset=None, in_=table[:, :],
                                             in_offset=bass.IndirectOffsetOnAxis(ap=index[:, b, n:n + 1], axis=0),
                                             bounds_check=N - 1).then_inc(came[b], 16)

        with pool.Fori(0, TILES // SLOTS) as i:
            for b in range(SLOTS):
                gather(i * SLOTS + b, b)
        for b in range(TILES % SLOTS):
            gather(TILES // SLOTS * SLOTS + b, b)
        pool.wait_ge(free, SLOTS)
        pool.sem_inc(free, -SLOTS)

    def on_vector_tile(dve, t, b, earlier):
        dve.wait_ge(came[b], earlier * 32 + (before[b] + 32))
        dve.sem_inc(seen, 1)
        nc.vector.tensor_tensor(q[:, b], q[:, b], k[:, b], ALU.mult).then_inc(done, 1)
        dve.wait_ge(done, 1)
        dve.sem_inc(done, -1)
        nc.vector.tensor_reduce(score[:, :, ds(t, 1)].rearrange("p h a -> p (h a)"),
                                q[:, b].rearrange("p (h d) -> p h d", h=HEADS), AXIS.X, ALU.add).then_inc(done, 1)
        dve.wait_ge(done, 1)
        dve.sem_inc(done, -1)
        dve.sem_inc(free, 1)

    def scan(out, mask, data, op0, op1, backward=False):
        way = slice(None, None, -1) if backward else slice(None)
        return [nc.vector.tensor_tensor_scan(out[:, h, way], mask[:, way], data[:, h, way], 0.0, op0, op1)
                for h in range(HEADS)]

    def on_vector_end(dve):
        def do(*steps):
            for step in steps:
                step.then_inc(done, 1)
            dve.wait_ge(done, len(steps))
            dve.sem_inc(done, -(len(steps)))
        tt, ts, copy = nc.vector.tensor_tensor, nc.vector.tensor_scalar, nc.vector.tensor_copy
        last = TILES - 1
        a, m = work
        do(ts(score[:], score[:], float(HD) ** -0.5, None, ALU.mult))

        def across(first, last_col, maximum):
            do(copy(edge_cols[:, 0], last_col), copy(edge_cols[:, 1], first))
            dve.sem_inc(cols_ready, 1)
            dve.wait_ge(psS_ready, 1)
            dve.sem_inc(psS_ready, -1)
            do(copy(over[:, 0:2], psS[:]))
            fwd, bwd, cont = T.pass_fwd[:], T.pass_bwd[:], T.cont[:, 1:PARTS]
            if maximum:
                do(ts(masks[:, 0], fwd, -NEG, NEG, ALU.mult, ALU.add), ts(masks[:, 1], bwd, -NEG, NEG, ALU.mult, ALU.add),
                   ts(masks[:, 2, 0:PARTS - 1], cont, -NEG, NEG, ALU.mult, ALU.add))
                fwd, bwd, cont = masks[:, 0], masks[:, 1], masks[:, 2, 0:PARTS - 1]
            op, use = ((ALU.add, ALU.max), ALU.add) if maximum else ((ALU.mult, ALU.add), ALU.mult)
            back = op if maximum else (ALU.mult, ALU.max)
            do(nc.vector.tensor_tensor_scan(over[:, 2], fwd, over[:, 0], 0.0, *op),
               nc.vector.tensor_tensor_scan(over[:, 3, ::-1], bwd[:, ::-1], over[:, 1, ::-1], 0.0, *back),
               nc.vector.memset(over[:, 4:6], NEG if maximum else 0.0))
            do(tt(over[:, 4, 1:PARTS], over[:, 2, 0:PARTS - 1], cont, use),
               tt(over[:, 5, 0:PARTS - 1], over[:, 3, 1:PARTS], cont, use))
            dve.sem_inc(rows_ready, 1)
            dve.wait_ge(psC_ready, 1)
            dve.sem_inc(psC_ready, -1)

        do(*scan(a, T.same_neg, score, ALU.add, ALU.max), *scan(m, T.next_neg, score, ALU.add, ALU.max, True))
        across(m[:, :, 0], a[:, :, last], True)
        do(copy(a, score[:]))
        do(tt(a[:, :, 0], psC[0:PARTS, 0], a[:, :, 0], ALU.max))
        do(tt(a[:, :, last], psC[0:PARTS, 1], a[:, :, last], ALU.max))
        do(*scan(m, T.same_neg, a, ALU.add, ALU.max))
        do(*scan(a, T.next_neg, m, ALU.add, ALU.max, True))
        do(tt(score[:], score[:], a, ALU.subtract))
        dve.sem_inc(chip.sem("shifted"), 1)
        dve.wait_ge(chip.sem("exp_ready"), 1)
        dve.sem_inc(chip.sem("exp_ready"), -1)
        do(*scan(a, T.same, score, ALU.mult, ALU.add))
        across(a[:, :, 0], a[:, :, last], False)
        do(copy(m, score[:]))
        do(tt(m[:, :, 0], psC[0:PARTS, 0], m[:, :, 0], ALU.add))
        do(*scan(a, T.same, m, ALU.mult, ALU.add))
        do(*scan(m, T.same_next, a, ALU.mult, ALU.max, True))
        across(m[:, :, 0], a[:, :, last], False)
        do(tt(a[:, :, last], psC[0:PARTS, 1], a[:, :, last], ALU.max))
        do(*scan(m, T.same_next, a, ALU.mult, ALU.max, True))
        do(ts(m, m, 1e-16, None, ALU.add))
        do(nc.vector.reciprocal(m, m))
        do(tt(score[:], score[:], m, ALU.mult))

    def on_tensor_end(pe):
        for _ in range(3):
            pe.wait_ge(cols_ready, 1)
            pe.sem_inc(cols_ready, -1)
            for n in range(2):
                t = nc.tensor.transpose(psS[:, n], edge_cols[:, n], T.ident[0:PARTS, 0:PARTS])
            t.then_inc(psS_ready, 1)
            pe.wait_ge(rows_ready, 1)
            pe.sem_inc(rows_ready, -1)
            for n in range(2):
                t = nc.tensor.transpose(psC[0:PARTS, n], over[:, 4 + n], T.ident[0:HEADS, 0:HEADS])
            t.then_inc(psC_ready, 1)

    def on_scalar_end(act):
        act.wait_ge(chip.sem("shifted"), 1)
        act.sem_inc(chip.sem("shifted"), -1)
        nc.scalar.activation(score[:], score[:], ACT.Exp).then_inc(chip.sem("exp_ready"), 1)

    return on_pool, on_vector_tile, on_vector_end, on_tensor_end, on_scalar_end


def aggregate(chip, sb, ps, T):
    nc = chip.nc
    v, weighted, acc = sb("v_rows", [PARTS, GROUP, D]), sb("weighted", [PARTS, D]), sb("acc", [PARTS, GROUP, D])
    v_index, row_index = sb("v_index", [PARTS, 2, GROUP], I32), sb("row_index", [PARTS, 2, GROUP], I32)
    psF = ps("psFix", 1, [128, D])[0]
    done, pooled, seen = chip.sem("dve_done"), chip.sem("pool_done"), chip.sem("seen")
    v_in, v_before = zip(*(chip.counted(f"v_in_{n}", GROUPS * 16) for n in range(GROUP)))
    out, out_before = zip(*(chip.counted(f"acc_out_{n}", GROUPS * 16) for n in range(GROUP)))
    fixed, fixed_before = chip.counted("fixed", 16)
    v_free, acc_ready, acc_free = chip.sem("v_free"), chip.sem("acc_ready"), chip.sem("acc_free")

    with nc.Block() as block:

        @block.gpsimd
        def _(pool):
            pool.sem_inc(acc_free, GROUP)

            def gather(b, n):
                pool.wait_ge(v_free, 1)
                pool.sem_inc(v_free, -1)
                nc.gpsimd.indirect_dma_start(out=v[:, n], out_offset=None, in_=T.v[:, :],
                                             in_offset=bass.IndirectOffsetOnAxis(ap=v_index[:, b, n:n + 1], axis=0),
                                             bounds_check=N - 1).then_inc(v_in[n], 16)

            def scatter(b, n, groups_before):
                pool.wait_ge(acc_ready, 1)
                pool.sem_inc(acc_ready, -1)
                nc.gpsimd.indirect_dma_start(out=T.agg[:, :], out_offset=bass.IndirectOffsetOnAxis(ap=row_index[:, b, n:n + 1], axis=0),
                                             in_=acc[:, n], in_offset=None, bounds_check=N + PARTS - 1,
                                             oob_is_err=False).then_inc(out[n], 16)
                if n >= 2:
                    pool.wait_ge(out[n - 2], (0 if groups_before is None else groups_before * 16) + (out_before[n - 2] + 16))
                    pool.sem_inc(acc_free, 1)
                elif groups_before is not None:
                    pool.wait_ge(out[n + 2], groups_before * 16 + out_before[n + 2])
                    pool.sem_inc(acc_free, 1)

            def indices(to, table, g):
                nc.gpsimd.tensor_copy(to, table[:, ds(g * GROUP, GROUP)]).then_inc(pooled, 1)
                pool.wait_ge(pooled, 1)
                pool.sem_inc(pooled, -1)

            def step(g, b, first=False, last=False):
                if not last:
                    indices(v_index[:, 1 - b], T.src_i, g + 1)
                indices(row_index[:, b], T.row_i, g)
                for n in range(GROUP):
                    if not last:
                        gather(1 - b, n)
                    scatter(b, n, None if first else g)

            indices(v_index[:, 0], T.src_i, 0)
            for n in range(GROUP):
                gather(0, n)
            step(0, 0, first=True)
            with pool.Fori(0, GROUPS // 2 - 1) as i:
                for k, b in enumerate((1, 0)):
                    step(i * 2 + k + 1, b)
            step(GROUPS - 1, 1, last=True)
            for n in (GROUP - 2, GROUP - 1):
                pool.wait_ge(out[n], out_before[n] + GROUPS * 16)
                pool.sem_inc(acc_free, 1)
            pool.wait_ge(v_free, GROUP)
            pool.sem_inc(v_free, -GROUP)
            pool.sem_inc(chip.sem("rows_out"), 1)
            pool.wait_ge(chip.sem("fix_ready"), 1)
            pool.sem_inc(chip.sem("fix_ready"), -1)
            nc.gpsimd.indirect_dma_start(out=T.agg[:, :], out_offset=bass.IndirectOffsetOnAxis(ap=T.fix_i[:, 0:1], axis=0),
                                         in_=weighted[:], in_offset=None, bounds_check=N - 1,
                                         oob_is_err=False).then_inc(fixed, 16)
            pool.wait_ge(fixed, fixed_before + 16)
            pool.sem_inc(seen, 1)

        @block.vector
        def _(dve):
            nc.vector.memset(acc[:, GROUP - 1], 0.0).then_inc(done, 1)
            dve.wait_ge(done, 1)
            dve.sem_inc(done, -1)
            dve.sem_inc(v_free, GROUP)
            with dve.Fori(0, GROUPS) as g:
                for n in range(GROUP):
                    t = ds(g * GROUP + n, 1)
                    dve.wait_ge(v_in[n], g * 16 + (v_before[n] + 16))
                    dve.sem_inc(seen, 1)
                    w = T.weight[:, :, t].to_broadcast([PARTS, HEADS, HD])
                    nc.vector.tensor_tensor(weighted[:].rearrange("p (h d) -> p h d", h=HEADS),
                                            v[:, n].rearrange("p (h d) -> p h d", h=HEADS), w, ALU.mult).then_inc(done, 1)
                    dve.wait_ge(done, 1)
                    dve.sem_inc(done, -1)
                    dve.sem_inc(v_free, 1)
                    dve.wait_ge(acc_free, 1)
                    dve.sem_inc(acc_free, -1)
                    nc.vector.scalar_tensor_tensor(acc[:, n], acc[:, (n - 1) % GROUP], T.same[:, t], weighted[:], ALU.mult,
                                                   ALU.add).then_inc(done, 1)
                    dve.wait_ge(done, 1)
                    dve.sem_inc(done, -1)
                    dve.sem_inc(acc_ready, 1)
            dve.wait_ge(acc_free, GROUP)
            dve.sem_inc(acc_free, -GROUP)
            dve.sem_inc(chip.sem("last_acc"), 1)
            dve.wait_ge(chip.sem("side_in"), ROWS_DMA)
            dve.sem_inc(chip.sem("side_in"), -ROWS_DMA)
            dve.wait_ge(chip.sem("psFix_ready"), 1)
            dve.sem_inc(chip.sem("psFix_ready"), -1)
            nc.vector.tensor_tensor(weighted[:], psF[0:PARTS], v[:, 0], ALU.add).then_inc(chip.sem("fix_ready"), 1)

        @block.sync
        def _(sp):
            sp.wait_ge(chip.sem("rows_out"), 1)
            sp.sem_inc(chip.sem("rows_out"), -1)
            rows_dma(sp, v[:, 0], T.agg[N:N + PARTS, :], chip.sem("side_in"))

        @block.tensor
        def _(pe):
            pe.wait_ge(chip.sem("last_acc"), 1)
            pe.sem_inc(chip.sem("last_acc"), -1)
            nc.tensor.matmul(psF[0:PARTS], T.carry[:], acc[:, GROUP - 1], start=True, stop=True).then_inc(chip.sem("psFix_ready"), 1)


HALF = 2
HCOLS = HALF * PARTS
HSTEPS = TILES // HALF


def output_projection(chip, sb, ps, T, xT, weight, bias):
    nc = chip.nc
    w_high, w_low = sb("wo_high", [128, KC, D], F32R), sb("wo_low", [128, KC, D], F32R)
    bias_col = sb("bo_col", [128, KC])
    psT, psY = ps("psT_o", 4, [128, 2, HCOLS]), ps("psY", 4, [128, 2, HCOLS])
    agg_t = tiles_of(T.agg[0:N, :])
    done, adone = chip.sem("dve_done"), chip.sem("act_done")
    rows_in, rows_free = chip.sem2("rows_in"), chip.sem2("rows_free")
    names = ("psT_ready", "psT_free", "high_done", "split_ready", "split_free", "psY_ready", "psY_free", "w_ready")
    s = {n: chip.sem(n) for n in names}

    with ExitStack() as stack:
        raw = stack.enter_context(nc.sbuf_tensor(chip.unique("wo_raw"), [128, KC, D], F32))
        with nc.Block() as block:

            @block.sync
            def _(sp):
                sp.dma_start(raw[:], weight.rearrange("(c k) n -> k c n", c=KC)).then_inc(chip.sem("w_in"), 16)
                sp.dma_start(bias_col[:], bias).then_inc(chip.sem("bias_in"), 16)
                sp.wait_ge(chip.sem("bias_in"), 16)
                sp.sem_inc(chip.sem("bias_in"), -16)

            @block.scalar
            def _(act):
                act.wait_ge(chip.sem("w_in"), 16)
                act.sem_inc(chip.sem("w_in"), -16)
                nc.scalar.activation(w_high[:], raw[:], ACT.Copy).then_inc(s["w_ready"], 1)

            @block.vector
            def _(dve):
                dve.wait_ge(s["w_ready"], 1)
                dve.sem_inc(s["w_ready"], -1)
                nc.vector.tensor_tensor(w_low[:], raw[:], w_high[:], ALU.subtract).then_inc(done, 1)
                dve.wait_ge(done, 1)
                dve.sem_inc(done, -1)

    rows = sb("agg_rows", [PARTS, HALF, D])
    a_high, a_low = sb("a_high", [128, 2, KC, HCOLS], F32R), sb("a_low", [128, 2, KC, HCOLS], F32R)
    with nc.Block() as block:

        @block.sync
        def _(sp):
            for b in range(2):
                sp.sem_inc(rows_free[b], 1)
            with sp.Fori(0, HSTEPS) as i:
                for j in range(HALF):
                    sp.wait_ge(rows_free[j], 1)
                    sp.sem_inc(rows_free[j], -1)
                    rows_dma(sp, rows[:, j], agg_t[:, ds(i * HALF + j, 1)].rearrange("p a d -> p (a d)"), rows_in[j])
            for b in range(2):
                sp.wait_ge(rows_free[b], 1)
                sp.sem_inc(rows_free[b], -1)

        @block.tensor
        def _(pe):
            def transposes(b):
                pe.wait_ge(s["psT_free"], 1)
                pe.sem_inc(s["psT_free"], -1)
                for j in range(HALF):
                    pe.wait_ge(rows_in[j], ROWS_DMA)
                    pe.sem_inc(rows_in[j], -ROWS_DMA)
                    for c in range(KC):
                        last = nc.tensor.transpose(psT[2 * b + c // 2][:, c % 2, j * PARTS:(j + 1) * PARTS],
                                                   rows[:, j, c * 128:(c + 1) * 128], T.ident[0:PARTS, 0:PARTS])
                    last.then_inc(s["psT_ready"], 1)

            def products(b):
                pe.wait_ge(s["split_ready"], 1)
                pe.sem_inc(s["split_ready"], -1)
                pe.wait_ge(s["psY_free"], 1)
                pe.sem_inc(s["psY_free"], -1)
                for m in range(KC):
                    parts = [(w, a, c) for c in range(KC) for w, a in ((w_high, a_high), (w_low, a_high), (w_high, a_low))]
                    for n, (w, a, c) in enumerate(parts):
                        last = nc.tensor.matmul(psY[2 * b + m // 2][:, m % 2], w[:, c, m * 128:(m + 1) * 128], a[:, b, c],
                                                start=n == 0, stop=n == len(parts) - 1)
                last.then_inc(s["psY_ready"], 1)

            transposes(0)
            with pe.Fori(0, HSTEPS // 2 - 1) as i:
                transposes(1)
                products(0)
                transposes(0)
                products(1)
            transposes(1)
            products(0)
            products(1)

        @block.scalar
        def _(act):
            act.sem_inc(s["split_free"], 2)
            with act.Fori(0, HSTEPS // 2) as i:
                for b in range(2):
                    for j in range(HALF):
                        act.wait_ge(s["psT_ready"], 1)
                        act.sem_inc(s["psT_ready"], -1)
                        act.sem_inc(rows_free[j], 1)
                    act.wait_ge(s["split_free"], 1)
                    act.sem_inc(s["split_free"], -1)
                    for k in range(2):
                        nc.scalar.activation(a_high[:, b, 2 * k:2 * k + 2], psT[2 * b + k][:], ACT.Copy).then_inc(adone, 1)
                    act.wait_ge(adone, 2)
                    act.sem_inc(adone, -2)
                    act.sem_inc(s["high_done"], 1)
            act.wait_ge(s["split_free"], 2)
            act.sem_inc(s["split_free"], -2)

        @block.vector
        def _(dve):
            dve.sem_inc(s["psT_free"], 2)
            dve.sem_inc(s["psY_free"], 2)

            def split(b):
                dve.wait_ge(s["high_done"], 1)
                dve.sem_inc(s["high_done"], -1)
                for k in range(2):
                    nc.vector.tensor_tensor(a_low[:, b, 2 * k:2 * k + 2], psT[2 * b + k][:], a_high[:, b, 2 * k:2 * k + 2],
                                            ALU.subtract).then_inc(done, 1)
                dve.wait_ge(done, 2)
                dve.sem_inc(done, -2)
                dve.sem_inc(s["psT_free"], 1)
                dve.sem_inc(s["split_ready"], 1)

            def add(step, b):
                dve.wait_ge(s["psY_ready"], 1)
                dve.sem_inc(s["psY_ready"], -1)
                dve.sem_inc(s["split_free"], 1)
                cols = ds(step * HCOLS, HCOLS)
                for m in range(KC):
                    nc.vector.scalar_tensor_tensor(xT[:, m, cols], psY[2 * b + m // 2][:, m % 2], bias_col[:, m:m + 1],
                                                   xT[:, m, cols], ALU.add, ALU.add).then_inc(done, 1)
                dve.wait_ge(done, KC)
                dve.sem_inc(done, -KC)
                dve.sem_inc(s["psY_free"], 1)
                for m in range(KC):
                    nc.vector.bn_stats(out=T.bn_stats[:, m, ds(step, 1)].rearrange("p a s -> p (a s)"),
                                       in_=xT[:, m, cols]).then_inc(done, 1)
                dve.wait_ge(done, KC)
                dve.sem_inc(done, -KC)

            split(0)
            with dve.Fori(0, HSTEPS // 2 - 1) as i:
                split(1)
                add(i * 2, 0)
                split(0)
                add(i * 2 + 1, 1)
            split(1)
            add(HSTEPS - 2, 0)
            add(HSTEPS - 1, 1)
            dve.wait_ge(s["psT_free"], 2)
            dve.sem_inc(s["psT_free"], -2)
            dve.wait_ge(s["psY_free"], 2)
            dve.sem_inc(s["psY_free"], -2)


def batchnorm(chip, sb, T, xT, gain, shift, steps):
    nc = chip.nc
    g, b_ = sb("bn_gain", [128, KC]), sb("bn_shift", [128, KC])
    mv, scale, off = sb("bn_mv", [128, KC, 2]), sb("bn_scale", [128, KC]), sb("bn_off", [128, KC])
    done, adone, pooled = chip.sem("dve_done"), chip.sem("act_done"), chip.sem("pool_done")
    with nc.Block() as block:

        @block.sync
        def _(sp):
            for out, in_ in ((g, gain), (b_, shift)):
                sp.dma_start(out[:], in_).then_inc(chip.sem("bn_in"), 16)

        @block.gpsimd
        def _(pool):
            pool.wait_ge(chip.sem("bn_aggregated"), 1)
            pool.sem_inc(chip.sem("bn_aggregated"), -1)
            pool.wait_ge(chip.sem("bn_in"), 32)
            pool.sem_inc(chip.sem("bn_in"), -32)

            def do(step):
                step.then_inc(pooled, 1)
                pool.wait_ge(pooled, 1)
                pool.sem_inc(pooled, -1)
            do(nc.gpsimd.tensor_scalar(scale[:], mv[:, :, 1], BN_EPS, None, ALU.add))
            do(nc.gpsimd.tensor_tensor(scale[:], scale[:], T.minus_half[:].to_broadcast([128, KC]), ALU.pow))
            do(nc.gpsimd.tensor_tensor(scale[:], scale[:], g[:], ALU.mult))
            do(nc.gpsimd.tensor_tensor(off[:], mv[:, :, 0], scale[:], ALU.mult))
            do(nc.gpsimd.tensor_tensor(off[:], b_[:], off[:], ALU.subtract))
            pool.sem_inc(chip.sem("bn_scales_v"), 1)
            pool.sem_inc(chip.sem("bn_scales_a"), 1)

        @block.vector
        def _(dve):
            for m in range(KC):
                nc.vector.bn_aggr(out=mv[:, m], in_=T.bn_stats[:, m, 0:steps]).then_inc(done, 1)
            dve.wait_ge(done, KC)
            dve.sem_inc(done, -KC)
            dve.sem_inc(chip.sem("bn_aggregated"), 1)
            dve.wait_ge(chip.sem("bn_scales_v"), 1)
            dve.sem_inc(chip.sem("bn_scales_v"), -1)
            for m in range(3):
                width = N if m < 2 else N // 2
                nc.vector.tensor_scalar(xT[:, m, 0:width], xT[:, m, 0:width], scale[:, m:m + 1], off[:, m:m + 1], ALU.mult,
                                        ALU.add).then_inc(done, 1)
            dve.wait_ge(done, 3)
            dve.sem_inc(done, -3)

        @block.scalar
        def _(act):
            act.wait_ge(chip.sem("bn_scales_a"), 1)
            act.sem_inc(chip.sem("bn_scales_a"), -1)
            for m, start in ((3, 0), (2, N // 2)):
                nc.scalar.activation(xT[:, m, start:N], xT[:, m, start:N], ACT.Identity, bias=off[:, m:m + 1],
                                     scale=scale[:, m:m + 1]).then_inc(adone, 1)
            act.wait_ge(adone, 2)
            act.sem_inc(adone, -2)


def feed_forward(chip, sb, ps, T, xT, w1, b1, w2, b2):
    nc = chip.nc
    cols_n = GROUP * PARTS
    w1_high, w1_low = sb("w1_high", [128, KC, 2 * FF], F32R), sb("w1_low", [128, KC, 2 * FF], F32R)
    w2_high, w2_low = sb("w2_high", [2 * FF, D], F32R), sb("w2_low", [2 * FF, D], F32R)
    b1_col, b2_col = sb("b1_col", [2 * FF, 1]), sb("b2_col", [128, KC])
    psH, psY = ps("psH_f", 2, [128, cols_n]), ps("psY_f", 4, [128, cols_n])
    done, adone = chip.sem("dve_done"), chip.sem("act_done")
    names = ("high_done", "split_ready", "split_free", "psH_ready", "psH_free", "hid_ready", "hid_free", "hid_low_ready",
             "parts_free", "psY_ready", "psY_free")
    s = {n: chip.sem(n) for n in names}

    with ExitStack() as stack:
        w1_raw = stack.enter_context(nc.sbuf_tensor(chip.unique("w1_raw"), [128, KC, 2 * FF], F32))
        w2_raw = stack.enter_context(nc.sbuf_tensor(chip.unique("w2_raw"), [2 * FF, D], F32))
        with nc.Block() as block:

            @block.sync
            def _(sp):
                w1v = w1.rearrange("(c k) n -> k c n", c=KC)
                moves = ((w1_raw[:, :, 0:FF], w1v), (w1_raw[:, :, FF:2 * FF], w1v), (w2_raw[0:FF], w2),
                         (w2_raw[FF:2 * FF], w2), (b1_col[0:FF], b1.unsqueeze(1)), (b1_col[FF:2 * FF], b1.unsqueeze(1)),
                         (b2_col[:], b2))
                for out, in_ in moves:
                    sp.dma_start(out, in_).then_inc(chip.sem("w_in"), 16)
                sp.wait_ge(chip.sem("w_in"), 16 * len(moves))
                sp.sem_inc(chip.sem("w_in"), -(16 * len(moves)))
                sp.sem_inc(chip.sem("w_here"), 1)

            @block.scalar
            def _(act):
                act.wait_ge(chip.sem("w_here"), 1)
                act.sem_inc(chip.sem("w_here"), -1)
                nc.scalar.activation(w1_high[:], w1_raw[:], ACT.Copy).then_inc(adone, 1)
                nc.scalar.activation(w2_high[:], w2_raw[:], ACT.Copy).then_inc(adone, 1)
                act.wait_ge(adone, 2)
                act.sem_inc(adone, -2)
                act.sem_inc(chip.sem("w_high"), 1)

            @block.vector
            def _(dve):
                dve.wait_ge(chip.sem("w_high"), 1)
                dve.sem_inc(chip.sem("w_high"), -1)
                nc.vector.tensor_tensor(w1_low[:], w1_raw[:], w1_high[:], ALU.subtract).then_inc(done, 1)
                nc.vector.tensor_tensor(w2_low[:], w2_raw[:], w2_high[:], ALU.subtract).then_inc(done, 1)
                dve.wait_ge(done, 2)
                dve.sem_inc(done, -2)

    x_high, x_low = sb("ff_x_high", [128, KC, cols_n], F32R), sb("ff_x_low", [128, KC, cols_n], F32R)
    hid, parts_ = sb("hid", [2 * FF, cols_n]), sb("hid_parts", [2 * FF, 2, cols_n], F32R)
    PAIRS = (slice(0, 2), slice(2, 4))
    with nc.Block() as block:

        @block.scalar
        def _(act):
            def split(g, pair):
                act.wait_ge(s["split_free"], 1)
                act.sem_inc(s["split_free"], -1)
                nc.scalar.activation(x_high[:, PAIRS[pair]], xT[:, PAIRS[pair], ds(g * cols_n, cols_n)], ACT.Copy)\
                    .then_inc(s["high_done"], 1)

            def hidden(b):
                act.wait_ge(s["psH_ready"], 1)
                act.sem_inc(s["psH_ready"], -1)
                act.wait_ge(s["hid_free"], 1)
                act.sem_inc(s["hid_free"], -1)
                nc.scalar.activation(hid[:], psH[b][:], ACT.Relu, bias=b1_col[:, 0:1]).then_inc(adone, 1)
                act.wait_ge(s["parts_free"], 1)
                act.sem_inc(s["parts_free"], -1)
                act.wait_ge(adone, 1)
                act.sem_inc(adone, -1)
                act.sem_inc(s["psH_free"], 1)
                nc.scalar.activation(parts_[:, b], hid[:], ACT.Copy).then_inc(s["hid_ready"], 1)

            act.sem_inc(s["split_free"], 2)
            act.sem_inc(s["psH_free"], 2)
            split(0, 0)
            split(0, 1)
            with act.Fori(0, GROUPS // 2 - 1) as i:
                for b in range(2):
                    split(i * 2 + b + 1, 0)
                    hidden(b)
                    split(i * 2 + b + 1, 1)
            split(GROUPS - 1, 0)
            hidden(0)
            split(GROUPS - 1, 1)
            hidden(1)
            act.wait_ge(s["psH_free"], 2)
            act.sem_inc(s["psH_free"], -2)
            act.wait_ge(s["split_free"], 2)
            act.sem_inc(s["split_free"], -2)

        @block.gpsimd
        def _(pool):
            with pool.Fori(0, GROUPS) as g:
                for pair in range(2):
                    pool.wait_ge(s["high_done"], 1)
                    pool.sem_inc(s["high_done"], -1)
                    nc.gpsimd.tensor_tensor(x_low[:, PAIRS[pair]], xT[:, PAIRS[pair], ds(g * cols_n, cols_n)],
                                            x_high[:, PAIRS[pair]], ALU.subtract).then_inc(s["split_ready"], 1)

        @block.tensor
        def _(pe):
            def hidden(b):
                pe.wait_ge(s["psH_free"], 1)
                pe.sem_inc(s["psH_free"], -1)
                for pair in range(2):
                    pe.wait_ge(s["split_ready"], 1)
                    pe.sem_inc(s["split_ready"], -1)
                    parts = [(w, a, c) for c in (2 * pair, 2 * pair + 1)
                             for w, a in ((w1_high, x_high), (w1_low, x_high), (w1_high, x_low))]
                    for n, (w, a, c) in enumerate(parts):
                        last = nc.tensor.matmul(psH[b][:], w[:, c], a[:, c], start=pair == 0 and n == 0,
                                                stop=pair == 1 and n == len(parts) - 1)
                    last.then_inc(s["split_free"] if pair == 0 else chip.sem("pe_done"), 1)
                pe.wait_ge(chip.sem("pe_done"), 1)
                pe.sem_inc(chip.sem("pe_done"), -1)
                pe.sem_inc(s["split_free"], 1)
                pe.sem_inc(s["psH_ready"], 1)

            def outputs(b):
                pe.wait_ge(s["hid_low_ready"], 1)
                pe.sem_inc(s["hid_low_ready"], -1)
                for m in range(KC):
                    pe.wait_ge(s["psY_free"], 1)
                    pe.sem_inc(s["psY_free"], -1)
                    out = slice(m * 128, (m + 1) * 128)
                    nc.tensor.matmul(psY[m][:], w2_high[:, out], parts_[:, b], start=True, stop=False)
                    nc.tensor.matmul(psY[m][:], w2_low[0:FF, out], parts_[0:FF, b], start=False, stop=True)\
                        .then_inc(s["psY_ready"], 1)

            hidden(0)
            with pe.Fori(0, GROUPS // 2 - 1) as i:
                for b in range(2):
                    hidden(1 - b)
                    outputs(b)
            hidden(1)
            outputs(0)
            outputs(1)

        @block.vector
        def _(dve):
            dve.sem_inc(s["psY_free"], 4)
            dve.sem_inc(s["hid_free"], 1)
            dve.sem_inc(s["parts_free"], 2)

            def low(b):
                dve.wait_ge(s["hid_ready"], 1)
                dve.sem_inc(s["hid_ready"], -1)
                nc.vector.tensor_tensor(parts_[FF:2 * FF, b], hid[FF:2 * FF], parts_[FF:2 * FF, b], ALU.subtract)\
                    .then_inc(done, 1)

            def add(g, m):
                cols = ds(g * cols_n, cols_n)
                dve.wait_ge(s["psY_ready"], 1)
                dve.sem_inc(s["psY_ready"], -1)
                nc.vector.scalar_tensor_tensor(xT[:, m, cols], psY[m][:], b2_col[:, m:m + 1], xT[:, m, cols], ALU.add,
                                               ALU.add).then_inc(done, 1)

            def statistics(g, m):
                nc.vector.bn_stats(out=T.bn_stats[:, m, ds(g, 1)].rearrange("p a s -> p (a s)"),
                                   in_=xT[:, m, ds(g * cols_n, cols_n)]).then_inc(done, 1)

            def step(g, b, more):
                add(g, 0)
                add(g, 1)
                dve.wait_ge(done, 1)
                dve.sem_inc(done, -1)
                dve.sem_inc(s["psY_free"], 1)
                statistics(g, 0)
                if more:
                    low(1 - b)
                dve.wait_ge(done, 1)
                dve.sem_inc(done, -1)
                dve.sem_inc(s["psY_free"], 1)
                statistics(g, 1)
                add(g, 2)
                dve.wait_ge(done, 1)
                dve.sem_inc(done, -1)
                if more:
                    dve.wait_ge(done, 1)
                    dve.sem_inc(done, -1)
                    dve.sem_inc(s["hid_free"], 1)
                    dve.sem_inc(s["hid_low_ready"], 1)
                add(g, 3)
                dve.wait_ge(done, 2)
                dve.sem_inc(done, -2)
                dve.sem_inc(s["psY_free"], 1)
                statistics(g, 2)
                dve.wait_ge(done, 1)
                dve.sem_inc(done, -1)
                dve.sem_inc(s["psY_free"], 1)
                dve.sem_inc(s["parts_free"], 1)
                statistics(g, 3)
                dve.wait_ge(done, 2)
                dve.sem_inc(done, -2)

            low(0)
            dve.wait_ge(done, 1)
            dve.sem_inc(done, -1)
            dve.sem_inc(s["hid_free"], 1)
            dve.sem_inc(s["hid_low_ready"], 1)
            with dve.Fori(0, GROUPS // 2 - 1) as i:
                for b in range(2):
                    step(i * 2 + b, b, True)
            step(GROUPS - 2, 0, True)
            step(GROUPS - 1, 1, False)
            dve.wait_ge(s["psY_free"], 4)
            dve.sem_inc(s["psY_free"], -4)
            dve.wait_ge(s["hid_free"], 1)
            dve.sem_inc(s["hid_free"], -1)
            dve.wait_ge(s["parts_free"], 2)
            dve.sem_inc(s["parts_free"], -2)


def finish(chip, sb, ps, T, xT, gain, shift, out):
    nc = chip.nc
    x1 = sb("x1", [PARTS, 2, GROUP, D])
    column = sb("column", [128, 2, KC, PARTS])
    gain_row, shift_row = sb("gain_row", [PARTS, D]), sb("shift_row", [PARTS, D])
    z = sb("z", [PARTS, 2, D])
    stats, mv = sb("stats_z", [PARTS, 2, 6]), sb("mv_z", [PARTS, 2, 2])
    rstd, off = sb("rstd_z", [PARTS, 2]), sb("off_z", [PARTS, 2])
    psZ = ps("psZ", 2, [128, D])
    done, adone, pooled = chip.sem("dve_done"), chip.sem("act_done"), chip.sem("pool_done")
    names = ("column_ready", "column_free", "psZ_ready", "psZ_free", "var_ready", "normed", "z_ready", "z_free",
             "sum_ready", "z_first")
    s = {n: chip.sem(n) for n in names}
    x_in, sum_done, stored = (chip.sem2(n) for n in ("x_loaded", "sum_done", "stored"))
    t_in, t_out = tiles_of(T.x1), tiles_of(out)

    with nc.Block() as block:

        @block.sync
        def _(sp):
            for o, i_ in ((gain_row, gain), (shift_row, shift)):
                sp.dma_start(o[:], i_.unsqueeze(0).to_broadcast([PARTS, D])).then_inc(chip.sem("bias_in"), 16)
            sp.wait_ge(chip.sem("bias_in"), 32)
            sp.sem_inc(chip.sem("bias_in"), -32)
            sp.sem_inc(chip.sem("gains_here"), 1)
            sp.sem_inc(chip.sem("shifts_here"), 1)

            def load(g, b):
                sp.wait_ge(stored[b], ROWS_DMA)
                sp.sem_inc(stored[b], -ROWS_DMA)
                rows_dma(sp, x1[:, b], t_in[:, ds(g * GROUP, GROUP)], x_in[b])

            def store(g, b):
                sp.wait_ge(sum_done[b], GROUP)
                sp.sem_inc(sum_done[b], -GROUP)
                rows_dma(sp, t_out[:, ds(g * GROUP, GROUP)], x1[:, b], stored[b])

            for b in range(2):
                sp.sem_inc(stored[b], ROWS_DMA)
                load(b, b)
            with sp.Fori(0, GROUPS // 2 - 1) as i:
                for b in range(2):
                    store(i * 2 + b, b)
                    load(i * 2 + b + 2, b)
            for b in range(2):
                store(GROUPS - 2 + b, b)
            for b in range(2):
                sp.wait_ge(stored[b], ROWS_DMA)
                sp.sem_inc(stored[b], -ROWS_DMA)

        @block.gpsimd
        def _(pool):
            pool.wait_ge(chip.sem("shifts_here"), 1)
            pool.sem_inc(chip.sem("shifts_here"), -1)
            pool.sem_inc(s["column_free"], 2)
            with pool.Fori(0, GROUPS // 2) as i:
                for b in range(2):
                    pool.wait_ge(x_in[b], ROWS_DMA)
                    pool.sem_inc(x_in[b], -ROWS_DMA)
                    for j in range(GROUP):
                        k = j % 2
                        pool.wait_ge(s["var_ready"], 1)
                        pool.sem_inc(s["var_ready"], -1)
                        nc.gpsimd.tensor_scalar(rstd[:, k:k + 1], mv[:, k, 1:2], LN_EPS, None, ALU.add).then_inc(pooled, 1)
                        nc.gpsimd.tensor_scalar(off[:, k:k + 1], mv[:, k, 0:1], -1.0, None, ALU.mult).then_inc(pooled, 1)
                        pool.wait_ge(pooled, 2)
                        pool.sem_inc(pooled, -2)
                        nc.gpsimd.tensor_tensor(rstd[:, k:k + 1], rstd[:, k:k + 1], T.minus_half[0:PARTS], ALU.pow)\
                            .then_inc(pooled, 1)
                        pool.wait_ge(pooled, 1)
                        pool.sem_inc(pooled, -1)
                        nc.gpsimd.tensor_tensor(off[:, k:k + 1], off[:, k:k + 1], rstd[:, k:k + 1], ALU.mult)\
                            .then_inc(s["normed"], 1)
                        nc.gpsimd.tensor_tensor(x1[:, b, j], x1[:, b, j], shift_row[:], ALU.add).then_inc(s["sum_ready"], 1)

        @block.scalar
        def _(act):
            act.sem_inc(s["psZ_free"], 2)

            def column_of(t, k):
                act.wait_ge(s["column_free"], 1)
                act.sem_inc(s["column_free"], -1)
                nc.scalar.activation(column[:, k], xT[:, :, ds(t * PARTS, PARTS)], ACT.Copy).then_inc(s["column_ready"], 1)

            def norm(k):
                act.wait_ge(s["normed"], 1)
                act.sem_inc(s["normed"], -1)
                act.wait_ge(s["z_free"], 1)
                act.sem_inc(s["z_free"], -1)
                nc.scalar.activation(z[:, k], psZ[k][0:PARTS], ACT.Identity, bias=off[:, k:k + 1], scale=rstd[:, k:k + 1])\
                    .then_inc(adone, 1)
                act.wait_ge(adone, 1)
                act.sem_inc(adone, -1)
                act.sem_inc(s["psZ_free"], 1)
                act.sem_inc(s["z_ready"], 1)

            column_of(0, 0)
            column_of(1, 1)
            with act.Fori(0, TILES // 2 - 1) as i:
                for k in range(2):
                    norm(k)
                    column_of(i * 2 + k + 2, k)
            norm(0)
            norm(1)
            act.wait_ge(s["psZ_free"], 2)
            act.sem_inc(s["psZ_free"], -2)
            act.wait_ge(s["column_free"], 2)
            act.sem_inc(s["column_free"], -2)
            act.wait_ge(s["z_free"], 2)
            act.sem_inc(s["z_free"], -2)

        @block.tensor
        def _(pe):
            with pe.Fori(0, TILES // 2) as i:
                for k in range(2):
                    pe.wait_ge(s["column_ready"], 1)
                    pe.sem_inc(s["column_ready"], -1)
                    pe.wait_ge(s["psZ_free"], 1)
                    pe.sem_inc(s["psZ_free"], -1)
                    for c in range(KC):
                        last = nc.tensor.transpose(psZ[k][0:PARTS, c * 128:(c + 1) * 128], column[:, k, c], T.ident[:])
                    last.then_inc(s["psZ_ready"], 1)

        @block.vector
        def _(dve):
            dve.wait_ge(chip.sem("gains_here"), 1)
            dve.sem_inc(chip.sem("gains_here"), -1)
            dve.sem_inc(s["z_free"], 2)

            def statistics(k):
                dve.wait_ge(s["psZ_ready"], 1)
                dve.sem_inc(s["psZ_ready"], -1)
                dve.sem_inc(s["column_free"], 1)
                nc.vector.bn_stats(out=stats[:, k], in_=psZ[k][0:PARTS]).then_inc(done, 1)
                dve.wait_ge(done, 1)
                dve.sem_inc(done, -1)
                nc.vector.bn_aggr(out=mv[:, k], in_=stats[:, k]).then_inc(s["var_ready"], 1)

            def add(b, j):
                k = j % 2
                dve.wait_ge(s["z_ready"], 1)
                dve.sem_inc(s["z_ready"], -1)
                nc.vector.tensor_tensor(z[:, k], z[:, k], gain_row[:], ALU.mult).then_inc(done, 1)
                dve.wait_ge(done, 1)
                dve.sem_inc(done, -1)
                dve.wait_ge(s["sum_ready"], 1)
                dve.sem_inc(s["sum_ready"], -1)
                nc.vector.tensor_tensor(x1[:, b, j], x1[:, b, j], z[:, k], ALU.add).then_inc(done, 1)
                dve.wait_ge(done, 1)
                dve.sem_inc(done, -1)
                dve.sem_inc(sum_done[b], 1)
                dve.sem_inc(s["z_free"], 1)

            statistics(0)
            with dve.Fori(0, GROUPS // 2 - 1) as i:
                for b in range(2):
                    for j in range(GROUP):
                        statistics((j + 1) % 2)
                        add(b, j)
            for b in range(2):
                for j in range(GROUP):
                    if (b, j) != (1, GROUP - 1):
                        statistics((j + 1) % 2)
                    add(b, j)


class Names:
    pass


def program(nc, A, out, scratch):
    ctx = ExitStack()
    with ctx:
        chip = Chip(nc, ctx)

        def allocator(stack):
            def sb(name, shape, dtype=F32):
                return stack.enter_context(nc.sbuf_tensor(chip.unique(name), shape, dtype))

            def ps(name, n, shape):
                size = math.prod(shape[1:])
                banks = -(-size // 512)
                whole = [stack.enter_context(nc.psum_tensor(chip.unique(name), [128, banks * 512], F32)) for k in range(n)]
                pieces = [w[0:shape[0], 0:size] for w in whole]
                return pieces if len(shape) == 2 else [x.rearrange("p (a b) -> p a b", a=shape[1]) for x in pieces]
            return sb, ps

        keep, _ = allocator(ctx)
        T, W = Names(), Names()
        T.messages, T.agg_l0, T.agg, T.x1 = scratch("messages", [N, MSG]), \
            [scratch(f"agg_l0_{k}", [N + PARTS, AGG]) for k in range(2)], scratch("agg", [N + PARTS, D]), scratch("x1_rows", [N, D])
        xT = keep("xT", [128, KC, N])
        rooms = [xT[0:PARTS, c].rearrange("p (t q) -> p t q", t=TILES) for c in range(KC)]
        T.same_src, T.earlier, T.srcq_i, T.zeros = rooms[0], rooms[1], rooms[2].bitcast(I32), xT[0:PARTS, 3]
        T.ident = keep("ident", [128, 128])
        T.minus_half = keep("minus_half", [128, 1])
        T.dst_ext = keep("dst_ext", [PARTS, TILES + 2], I32)
        T.dst_f = keep("dst_f", [PARTS, TILES + 2])
        T.src_i = keep("src_i", [PARTS, TILES], I32)
        T.spare_i, T.spare = keep("spare_i", [PARTS, 1], I32), keep("spare", [PARTS, 1])
        interaction = ExitStack()
        keep_l0, _ = allocator(interaction)
        W.f2o1_s, W.f2o2_s, W.vec = keep_l0("w_f2o1_s", [128, B]), keep_l0("w_f2o2_s", [B, B]), keep_l0("w_vec", [128, 2, B])
        with ExitStack() as edges:
            sb, _ = allocator(edges)
            W.in2f, W.w1, W.b1, W.w2 = sb("w_in2f", [B, 2, F]), sb("w1", [R, F]), sb("b1", [F, 1]), sb("w2", [F + 1, 6 * F])
            T.src_f = sb("src_f", [PARTS, TILES])
            T.rcut, T.y = sb("rcut", [PARTS, TILES]), sb("y", [PARTS, TILES, 4])
            T.dup, T.tmp80, T.scat_i = sb("dup", [PARTS, TILES]), sb("tmp80", [PARTS, TILES]), sb("scat_i", [PARTS, TILES], I32)
            T.lower = sb("lower", [PARTS, PARTS])
            with ExitStack() as stage:
                setup(chip, *allocator(stage), T, W, A)
            with ExitStack() as stage:
                l0_node_messages(chip, *allocator(stage), A.x, T, W)
            with ExitStack() as stage:
                l0_edges(chip, *allocator(stage), T, W, A.radial)
        with ExitStack() as stage:
            l0_nodes(chip, *allocator(stage), A.x, T, W, xT)
        interaction.close()

        T.q, T.k, T.v = (scratch(n, [N, D]) for n in ("q", "k", "v"))
        T.same, T.same_next, T.same_neg, T.next_neg = (keep(n, [PARTS, TILES]) for n in ("same", "same_next", "same_neg", "next_neg"))
        T.row_i, T.fix_i, T.carry = keep("row_i", [PARTS, TILES], I32), keep("fix_i", [PARTS, 1], I32), keep("carry", [PARTS, PARTS])
        T.pass_fwd, T.pass_bwd, T.cont = keep("pass_fwd", [HEADS, PARTS]), keep("pass_bwd", [HEADS, PARTS]), \
            keep("cont", [HEADS, PARTS + 1])
        T.weight = keep("weight", [PARTS, HEADS, TILES])
        with ExitStack() as stage:
            attention_masks(chip, *allocator(stage), T, A.dst_tiled)
        for layer in range(LAYERS):
            for weight, bias, table, scores in ((A.wk, None, T.k, None), (A.wq, A.bq, T.q, None),
                                                (A.wv, None, T.v, scores_and_softmax)):
                with ExitStack() as stage:
                    project(chip, *allocator(stage), T, xT, weight[layer], None if bias is None else bias[layer], table, scores)
            with ExitStack() as stage:
                aggregate(chip, *allocator(stage), T)
            with ExitStack() as norms:
                T.bn_stats = allocator(norms)[0]("bn_stats", [128, KC, HSTEPS, 6])
                with ExitStack() as stage:
                    output_projection(chip, *allocator(stage), T, xT, A.wo[layer], A.bo[layer])
                with ExitStack() as stage:
                    batchnorm(chip, allocator(stage)[0], T, xT, A.g1[layer], A.beta1[layer], HSTEPS)
                with ExitStack() as stage:
                    feed_forward(chip, *allocator(stage), T, xT, A.ff1[layer], A.ffb1[layer], A.ff2[layer], A.ffb2[layer])
                with ExitStack() as stage:
                    batchnorm(chip, allocator(stage)[0], T, xT, A.g2[layer], A.beta2[layer], GROUPS)
        with ExitStack() as stage:
            finish(chip, *allocator(stage), T, xT, A.ln_g, A.ln_b, out)


def kernel(**inputs):
    import numpy as np
    import concourse.bacc as bacc
    from concourse.bass_utils import run_bass_kernel_spmd

    nc = bacc.Bacc("TRN2", target_bir_lowering=False, num_devices=1)
    g = {k: np.asarray(v) for k, v in inputs.items()}
    laid = {
        "x": g["x"],
        "src": g["src"], "dst": g["dst"],
        "src_tiled": g["src"].reshape(PARTS, TILES).T.reshape(-1),
        "dst_tiled": g["dst"].reshape(PARTS, TILES).T,
        "radial": g["edge_attr_20"].reshape(PARTS, TILES, R).transpose(2, 1, 0).reshape(R, E),
        "y": g["edge_attr_4"], "rcut": g["edge_weight"],
        "in2f_s": g["L0_gnn_w_in2f_s"], "in2f_v": g["L0_gnn_w_in2f_v"],
        "w1": g["L0_gnn_W1"], "b1": g["L0_gnn_b1"],
        "w2": g["L0_gnn_W2"].reshape(F, F, 6).transpose(0, 2, 1).reshape(F, 6 * F),
        "b2": g["L0_gnn_b2"].reshape(F, 6).T.reshape(6 * F),
        "f2o1_s": g["L0_gnn_w_f2o1_s"], "f2o1_vT": g["L0_gnn_w_f2o1_v"].T,
        "f2o2_s": g["L0_gnn_w_f2o2_s"], "f2o2_v": g["L0_gnn_w_f2o2_v"],
        "ln_g": g["L1_gnn_ln_g"], "ln_b": g["L1_gnn_ln_b"], "bq": g["L1_gnn_bq"], "ffb1": g["L1_gnn_b1"],
    }
    for to, name in (("wq", "Wq"), ("wk", "Wk"), ("wv", "Wv"), ("wo", "Wo"), ("ff1", "W1"), ("ff2", "W2")):
        laid[to] = g["L1_gnn_" + name].transpose(0, 2, 1)
    for to, name in (("bo", "bo"), ("ffb2", "b2"), ("g1", "g1"), ("beta1", "beta1"), ("g2", "g2"), ("beta2", "beta2")):
        laid[to] = g["L1_gnn_" + name].reshape(LAYERS, KC, 128).transpose(0, 2, 1)
    arrays, A = {}, Names()
    for name, a in laid.items():
        arrays[f"in_{name}"] = np.ascontiguousarray(a)
        A.__dict__[name] = nc.dram_tensor(f"in_{name}", list(a.shape), mybir.dt.from_np(a.dtype), kind="ExternalInput").ap()
    out = nc.dram_tensor("out", [N, D], F32, kind="ExternalOutput").ap()

    def scratch(name, shape):
        return nc.dram_tensor(name, shape, F32).ap()

    program(nc, A, out, scratch)
    return run_bass_kernel_spmd(nc, [arrays], core_ids=[0]).results[0]["out"]
```

```python
import math
from contextlib import ExitStack, contextmanager

import concourse.bass as bass
from concourse import mybir

F32 = mybir.dt.float32
F32R = mybir.dt.float32r
I32 = mybir.dt.int32
ALU = mybir.AluOpType
ACT = mybir.ActivationFunctionType
AXIS = mybir.AxisListType

N = 10000
E = 10000
D = 512
PARTS = 125
TILES = N // PARTS
GROUP = 4
GROUPS = TILES // GROUP
KC = D // 128
WIDE = 112
ROWS_DMA = 32
B = 128
F = 32
R = 20
MSG = 4 * F
AGG = 8 * F
HEADS = 8
HD = D // HEADS
LAYERS = 2
SLOTS = 3
FF = 64
LN_EPS = 1e-5
BN_EPS = 1e-5
LOG2 = 0.6931471805599453
FAR = 16384.0
NEG = -1e30
ds = bass.ds


def rows_dma(engine, out, in_, sem):
    engine.dma_start(out[0:WIDE], in_[0:WIDE]).then_inc(sem, 16)
    engine.dma_start(out[WIDE:PARTS], in_[WIDE:PARTS]).then_inc(sem, 16)


class Chip:

    def __init__(self, nc, ctx):
        self.nc, self.ctx, self.stage_ctx, self.tensors = nc, ctx, None, 0
        self.sems, self.kept, self.counts = {}, {}, {}

    def sem(self, name):
        if name not in self.sems:
            self.sems[name] = self.stage_ctx.enter_context(self.nc.semaphore(name))
        return self.sems[name]

    def kept_sem(self, name):
        if name not in self.kept:
            self.kept[name] = self.ctx.enter_context(self.nc.semaphore(name))
        return self.kept[name]

    @contextmanager
    def stage(self):
        with ExitStack() as stack:
            self.stage_ctx = stack
            yield stack
        self.sems = {}

    def sem2(self, name):
        return [self.sem(f"{name}_0"), self.sem(f"{name}_1")]

    def unique(self, name):
        self.tensors += 1
        return f"{name}_{self.tensors}"

    def counted(self, name, n):
        before = self.counts.get(name, 0)
        self.counts[name] = before + n
        return self.kept_sem(name), before


def tiles_of(dram):
    return dram.rearrange("(p t) d -> p t d", t=TILES)


def bcast(ap, n):
    a = ap.unsqueeze(len(ap.shape))
    return a.to_broadcast([*ap.shape, n])


def zero_rows(engine, T, table, cols, g, zeroed):
    n = TILES * cols // GROUPS
    rows_dma(engine, table[0:N, :].rearrange("(p t) d -> p (t d)", t=TILES)[:, ds(g * n, n)], T.zeros[:, 0:n], zeroed)


def setup(chip, sb, ps, T, W, A):
    nc = chip.nc
    raw_vT = sb("raw_vT", [B, 2, 2 * F])
    raw_o2v = sb("raw_o2v", [B, B])
    psV = ps("psV", 1, [128, B])[0]
    made, loads, weights_in = chip.sem("const_made"), chip.sem("edges_in"), chip.kept_sem("weights_in")
    done, cleared = chip.sem("dve_done"), chip.sem("cleared")
    with nc.Block() as block:

        @block.gpsimd
        def _(pool):
            nc.gpsimd.memset(T.dst_ext[:], -1).then_inc(made, 1)
            pool.wait_ge(made, 1)
            pool.sem_inc(made, -1)
            pool.sem_inc(cleared, 1)
            nc.gpsimd.memset(T.ident[:], 0.0).then_inc(made, 1)
            nc.gpsimd.memset(T.lower[:], 1.0).then_inc(made, 1)
            nc.gpsimd.memset(T.zeros[:, 0:TILES * D // GROUPS], 0.0).then_inc(made, 1)
            nc.gpsimd.memset(T.minus_half[:], -0.5).then_inc(made, 1)
            pool.wait_ge(made, 4)
            pool.sem_inc(made, -4)
            nc.gpsimd.affine_select(out=T.ident[:], in_=T.ident[:], compare_op=ALU.not_equal, fill=1.0,
                                    base=0, pattern=[[-1, 128]], channel_multiplier=1).then_inc(made, 1)
            nc.gpsimd.affine_select(out=T.lower[:], in_=T.lower[:], compare_op=ALU.is_gt, fill=0.0,
                                    base=0, pattern=[[-1, PARTS]], channel_multiplier=1).then_inc(made, 1)
            nc.gpsimd.iota(T.spare_i[:], pattern=[[0, 1]], base=N, channel_multiplier=1).then_inc(made, 1)
            pool.wait_ge(made, 3)
            pool.sem_inc(made, -3)
            nc.gpsimd.tensor_copy(T.spare[:], T.spare_i[:]).then_inc(made, 1)
            pool.wait_ge(made, 1)
            pool.sem_inc(made, -1)

        @block.sync
        def _(sp):
            moves = ((raw_vT[:, 0], A.f2o1_vT), (raw_vT[:, 1], A.f2o1_vT), (raw_o2v[:], A.f2o2_v),
                     (W.in2f[:, 0], A.in2f_s), (W.in2f[:, 1], A.in2f_v), (W.f2o1_s[0:2 * F], A.f2o1_s),
                     (W.f2o2_s[:], A.f2o2_s), (W.w1[:], A.w1), (W.b1[:], A.b1.rearrange("(f a) -> f a", a=1)),
                     (W.w2[0:F], A.w2), (W.w2[F:F + 1], A.b2.unsqueeze(0)))
            for out, in_ in moves:
                sp.dma_start(out, in_).then_inc(weights_in, 16)
            sp.wait_ge(cleared, 1)
            sp.sem_inc(cleared, -1)
            moves2 = ((T.src_i[:], A.src.rearrange("(p t) -> p t", t=TILES)),
                      (T.dst_ext[:, 1:TILES + 1], A.dst.rearrange("(p t) -> p t", t=TILES)),
                      (T.rcut[:], A.rcut.rearrange("(p t) -> p t", t=TILES)),
                      (T.y[:], A.y.rearrange("(p t) c -> p t c", t=TILES)),
                      (T.srcq_i[:].rearrange("p t q -> p (t q)"), A.src_tiled.unsqueeze(0).to_broadcast([PARTS, E])))
            for out, in_ in moves2:
                sp.dma_start(out, in_).then_inc(loads, 16)
            sp.wait_ge(loads, 16 * len(moves2))
            sp.sem_inc(loads, -(16 * len(moves2)))

        @block.tensor
        def _(pe):
            pe.wait_ge(weights_in, 16 * 11)
            nc.tensor.matmul(psV[:], raw_vT[:].rearrange("k a m -> k (a m)"), raw_o2v[:], start=True, stop=True)\
                .then_inc(chip.sem("psV_ready"), 1)

        @block.vector
        def _(dve):
            nc.vector.memset(W.vec[:], 0.0).then_inc(done, 1)
            nc.vector.memset(W.f2o1_s[2 * F:128], 0.0).then_inc(done, 1)
            dve.wait_ge(done, 2)
            dve.sem_inc(done, -2)
            dve.wait_ge(weights_in, 16 * 11)
            root = 1.0 / math.sqrt(B)
            nc.vector.tensor_scalar(W.in2f[:], W.in2f[:], root, None, ALU.mult).then_inc(done, 1)
            nc.vector.tensor_scalar(W.f2o2_s[:], W.f2o2_s[:], root, None, ALU.mult).then_inc(done, 1)
            nc.vector.tensor_scalar(W.f2o1_s[0:2 * F], W.f2o1_s[0:2 * F], 1.0 / math.sqrt(2 * F), None, ALU.mult)\
                .then_inc(done, 1)
            dve.wait_ge(chip.sem("psV_ready"), 1)
            dve.sem_inc(chip.sem("psV_ready"), -1)
            for half in range(2):
                rows = slice(64 * half, 64 * half + 64)
                nc.vector.tensor_scalar(W.vec[rows, half], psV[rows], root / math.sqrt(2 * F), None, ALU.mult)\
                    .then_inc(done, 1)
            dve.wait_ge(done, 5)
            dve.sem_inc(done, -5)


def layernorm_stats(chip, dve, tile_of, stats, mv, var_ready):
    nc, done = chip.nc, chip.sem("dve_done")
    for j in range(GROUP):
        nc.vector.bn_stats(out=stats[:, j], in_=tile_of(j)).then_inc(done, 1)
    dve.wait_ge(done, GROUP)
    dve.sem_inc(done, -GROUP)
    for j in range(GROUP):
        nc.vector.bn_aggr(out=mv[:, j], in_=stats[:, j]).then_inc(done, 1)
    dve.wait_ge(done, GROUP)
    dve.sem_inc(done, -GROUP)
    dve.sem_inc(var_ready, 1)


def layernorm_scales(chip, pool, T, mv, rstd, shift, var_ready, normed):
    nc, done = chip.nc, chip.sem("pool_done")
    pool.wait_ge(var_ready, 1)
    pool.sem_inc(var_ready, -1)
    nc.gpsimd.tensor_scalar(rstd, mv[:, :, 1], LN_EPS, None, ALU.add).then_inc(done, 1)
    nc.gpsimd.tensor_scalar(shift, mv[:, :, 0], -1.0, None, ALU.mult).then_inc(done, 1)
    pool.wait_ge(done, 2)
    pool.sem_inc(done, -2)
    nc.gpsimd.tensor_tensor(rstd, rstd, T.minus_half[0:PARTS, 0:1].to_broadcast([PARTS, GROUP]), ALU.pow).then_inc(done, 1)
    pool.wait_ge(done, 1)
    pool.sem_inc(done, -1)
    nc.gpsimd.tensor_tensor(shift, shift, rstd, ALU.mult).then_inc(normed, 1)


def l0_node_messages(chip, sb, ps, x, T, W):
    nc = chip.nc
    zero_cols = TILES * D // GROUPS
    xin = [T.zeros[:, zero_cols + n * GROUP * D:zero_cols + (n + 1) * GROUP * D].rearrange("p (j d) -> p j d", j=GROUP)
           for n in range(3)] + [sb("xin", [PARTS, GROUP, D])[:]]
    stats = sb("stats", [PARTS, GROUP, 6])
    mv = sb("mv", [PARTS, 2, GROUP, 2])
    rstd, shift = sb("rstd", [PARTS, 2, GROUP]), sb("shift", [PARTS, 2, GROUP])
    h = sb("h", [PARTS, 2, D])
    hT = sb("hT", [128, 2, KC, PARTS])
    stage = sb("stage", [PARTS, 2, GROUP, MSG])
    psT = ps("psT", 2, [128, KC, PARTS])
    psM = ps("psM", 2, [128, 4, F])
    loaded, x_free = ([chip.sem(f"{name}_{n}") for n in range(4)] for name in ("x_loaded", "x_free"))
    stored = chip.sem2("stored")
    stage_ready = chip.sem2("stage_ready")
    normed, h_ready, psT_ready = chip.sem("normed"), chip.sem("h_ready"), chip.sem("psT_ready")
    hT_ready, hT_free, psM_ready, psM_free = (chip.sem(n) for n in ("hT_ready", "hT_free", "psM_ready", "psM_free"))
    done, var_ready = chip.sem("dve_done"), chip.sem("var_ready")
    xt, table = tiles_of(x), tiles_of(T.messages)

    with nc.Block() as block:

        @block.sync
        def _(sp):
            def load(g, n):
                sp.wait_ge(x_free[n], 1)
                sp.sem_inc(x_free[n], -1)
                rows_dma(sp, xin[n], xt[:, ds(g * GROUP, GROUP)], loaded[n])

            def store(g, b):
                sp.wait_ge(stage_ready[b], 1)
                sp.sem_inc(stage_ready[b], -1)
                rows_dma(sp, table[:, ds(g * GROUP, GROUP)], stage[:, b], stored[b])

            zeroed = chip.sem("zeroed")
            def zero(g):
                for table_l0 in T.agg_l0:
                    zero_rows(sp, T, table_l0, AGG, g, zeroed)

            for b in range(2):
                sp.sem_inc(stored[b], ROWS_DMA)
            for n in range(4):
                sp.sem_inc(x_free[n], 1)
                load(n, n)
            with sp.Fori(0, GROUPS // 4 - 1) as i:
                for n in range(4):
                    load(i * 4 + n + 4, n)
                    zero(i * 4 + n)
                    store(i * 4 + n, n % 2)
            for n in range(4):
                zero(GROUPS - 4 + n)
                store(GROUPS - 4 + n, n % 2)
            for table_l0 in T.agg_l0:
                rows_dma(sp, table_l0[N:N + PARTS, :], T.zeros[:, 0:AGG], zeroed)
            sp.wait_ge(zeroed, (GROUPS + 1) * 2 * ROWS_DMA)
            sp.sem_inc(zeroed, -((GROUPS + 1) * 2 * ROWS_DMA))
            for n in range(4):
                sp.wait_ge(x_free[n], 1)
                sp.sem_inc(x_free[n], -1)
            for b in range(2):
                sp.wait_ge(stored[b], ROWS_DMA)
                sp.sem_inc(stored[b], -ROWS_DMA)

        @block.vector
        def _(dve):
            dve.sem_inc(hT_free, 2)
            dve.sem_inc(psM_free, 2)

            def statistics(n):
                dve.wait_ge(loaded[n], ROWS_DMA)
                dve.sem_inc(loaded[n], -ROWS_DMA)
                layernorm_stats(chip, dve, lambda j: xin[n][:, j], stats, mv[:, n % 2], var_ready)

            def messages(g, b):
                tiles = ds(g * GROUP, GROUP)
                nc.vector.tensor_tensor(T.same_src[:, tiles], T.srcq_i[:, tiles], bcast(T.src_i[:, tiles], PARTS),
                                        ALU.is_equal).then_inc(chip.sem("same_src_made"), 1)
                dve.wait_ge(stored[b], ROWS_DMA)
                dve.sem_inc(stored[b], -ROWS_DMA)
                for j in range(GROUP):
                    dve.wait_ge(psM_ready, 1)
                    dve.sem_inc(psM_ready, -1)
                    dve.sem_inc(hT_free, 1)
                    nc.vector.tensor_copy(stage[:, b, j], psM[j % 2][0:PARTS].rearrange("p a f -> p (a f)")).then_inc(done, 1)
                    dve.wait_ge(done, 1)
                    dve.sem_inc(done, -1)
                    dve.sem_inc(psM_free, 1)
                dve.sem_inc(stage_ready[b], 1)
                dve.wait_ge(chip.sem("dups_marked"), 1)
                dve.sem_inc(chip.sem("dups_marked"), -1)
                nc.vector.tensor_reduce(T.dup[:, tiles], T.earlier[:, tiles], AXIS.X, ALU.add).then_inc(done, 1)
                dve.wait_ge(done, 1)
                dve.sem_inc(done, -1)

            statistics(0)
            with dve.Fori(0, GROUPS // 4 - 1) as i:
                for n in range(4):
                    statistics((n + 1) % 4)
                    messages(i * 4 + n, n % 2)
            for n in range(4):
                if n < 3:
                    statistics(n + 1)
                messages(GROUPS - 4 + n, n % 2)
            dve.wait_ge(hT_free, 2)
            dve.sem_inc(hT_free, -2)
            dve.wait_ge(psM_free, 2)
            dve.sem_inc(psM_free, -2)

        @block.scalar
        def _(act):
            with act.Fori(0, GROUPS // 4):
                for n in range(4):
                    b = n % 2
                    act.wait_ge(normed, 1)
                    act.sem_inc(normed, -1)

                    def relu(j):
                        nc.scalar.activation(h[:, j % 2], xin[n][:, j], ACT.Relu, bias=shift[:, b, j:j + 1],
                                             scale=rstd[:, b, j:j + 1]).then_inc(h_ready, 1)
                    relu(0)
                    for j in range(GROUP):
                        if j + 1 < GROUP:
                            relu(j + 1)
                        act.wait_ge(psT_ready, 1)
                        act.sem_inc(psT_ready, -1)
                        act.wait_ge(hT_free, 1)
                        act.sem_inc(hT_free, -1)
                        nc.scalar.activation(hT[:, j % 2], psT[j % 2][:], ACT.Copy).then_inc(hT_ready, 1)

        @block.tensor
        def _(pe):
            with pe.Fori(0, GROUPS // 4):
                for n in range(4):
                    def transpose(j):
                        pe.wait_ge(h_ready, 1)
                        pe.sem_inc(h_ready, -1)
                        if j == GROUP - 1:
                            pe.sem_inc(x_free[n], 1)
                        vectors = h[:, j % 2, B:D].rearrange("p (b c) -> p c b", c=3)
                        for c in range(4):
                            last = nc.tensor.transpose(psT[j % 2][:, c], h[:, j % 2, 0:B] if c == 0 else vectors[:, c - 1],
                                                       T.ident[0:PARTS, 0:PARTS])
                        last.then_inc(psT_ready, 1)

                    transpose(0)
                    for j in range(GROUP):
                        if j + 1 < GROUP:
                            transpose(j + 1)
                        pe.wait_ge(hT_ready, 1)
                        pe.sem_inc(hT_ready, -1)
                        pe.wait_ge(psM_free, 1)
                        pe.sem_inc(psM_free, -1)
                        for c in range(4):
                            last = nc.tensor.matmul(psM[j % 2][0:PARTS, c], hT[:, j % 2, c], W.in2f[:, min(c, 1)],
                                                    start=True, stop=True)
                        last.then_inc(psM_ready, 1)

        @block.gpsimd
        def _(pool):
            pooled = chip.sem("pool_done")
            for to, from_ in ((T.src_f, T.src_i), (T.dst_f, T.dst_ext)):
                nc.gpsimd.tensor_copy(to[:], from_[:]).then_inc(pooled, 1)
            pool.wait_ge(pooled, 2)
            pool.sem_inc(pooled, -2)

            def earlier(g):
                pool.wait_ge(chip.sem("same_src_made"), 1)
                pool.sem_inc(chip.sem("same_src_made"), -1)
                tiles = ds(g * GROUP, GROUP)
                nc.gpsimd.tensor_tensor(T.earlier[:, tiles], T.same_src[:, tiles],
                                        T.lower[:].unsqueeze(1).to_broadcast([PARTS, GROUP, PARTS]), ALU.mult)\
                    .then_inc(chip.sem("dups_marked"), 1)

            def scales(b):
                layernorm_scales(chip, pool, T, mv[:, b], rstd[:, b], shift[:, b], var_ready, normed)

            scales(0)
            with pool.Fori(0, GROUPS // 2 - 1) as i:
                for b in range(2):
                    scales(1 - b)
                    earlier(i * 2 + b)
            scales(1)
            earlier(GROUPS - 2)
            earlier(GROUPS - 1)

    with nc.Block() as block:

        @block.vector
        def _(dve):
            nc.vector.tensor_scalar(T.dup[:], T.dup[:], 1.0, None, ALU.min).then_inc(done, 1)
            nc.vector.tensor_scalar(T.tmp80[:], T.src_f[:], -1.0, T.spare[:, 0:1], ALU.mult, ALU.add).then_inc(done, 1)
            dve.wait_ge(done, 2)
            dve.sem_inc(done, -2)
            nc.vector.tensor_tensor(T.tmp80[:], T.tmp80[:], T.dup[:], ALU.mult).then_inc(done, 1)
            dve.wait_ge(done, 1)
            dve.sem_inc(done, -1)
            nc.vector.tensor_tensor(T.tmp80[:], T.tmp80[:], T.src_f[:], ALU.add).then_inc(done, 1)
            dve.wait_ge(done, 1)
            dve.sem_inc(done, -1)
            nc.vector.tensor_copy(T.scat_i[:], T.tmp80[:]).then_inc(done, 1)
            dve.wait_ge(done, 1)
            dve.sem_inc(done, -1)


def softplus_minus_log2(chip, act, dve, z_in, bias, mag, out, z_ready, mag_free, mag_ready, out_ready, freed):
    nc = chip.nc

    def scalar_half():
        done = chip.sem("act_done")
        act.wait_ge(z_ready, 1)
        act.sem_inc(z_ready, -1)
        act.wait_ge(mag_free, 1)
        act.sem_inc(mag_free, -1)
        nc.scalar.activation(mag, z_in, ACT.Abs, **({} if bias is None else {"bias": bias})).then_inc(done, 1)
        act.wait_ge(done, 1)
        act.sem_inc(done, -1)
        nc.scalar.activation(mag, mag, ACT.Exp, scale=-1.0).then_inc(done, 1)
        act.wait_ge(done, 1)
        act.sem_inc(done, -1)
        nc.scalar.activation(mag, mag, ACT.Ln, bias=1.0).then_inc(mag_ready, 1)

    def vector_half():
        done = chip.sem("dve_done")
        dve.wait_ge(mag_ready, 1)
        dve.sem_inc(mag_ready, -1)
        nc.vector.tensor_scalar(out, z_in, 0.0 if bias is None else bias, 0.0, ALU.add, ALU.max).then_inc(done, 1)
        dve.wait_ge(done, 1)
        dve.sem_inc(done, -1)
        nc.vector.scalar_tensor_tensor(out, mag, -LOG2, out, ALU.add, ALU.add).then_inc(done, 1)
        dve.wait_ge(done, 1)
        dve.sem_inc(done, -1)
        for s in (out_ready, mag_free, *freed):
            dve.sem_inc(s, 1)

    return scalar_half, vector_half


def l0_edges(chip, sb, ps, T, W, edge_radial, dst_tiled):
    nc = chip.nc
    msg = sb("msg", [PARTS, 2, GROUP, MSG])
    gather_i = sb("gather_i", [PARTS, 2, GROUP], I32)
    scatter_i = sb("scatter_i", [PARTS, 2, GROUP], I32)
    radial = sb("radial", [R, 2, GROUP * PARTS])
    mag = sb("mag", [F, 2, GROUP * PARTS])
    hidden = sb("hidden", [F + 1, 2, GROUP * PARTS])
    filt = sb("filt", [PARTS, GROUP, 4, F])
    s_filt = sb("s_filt", [PARTS, GROUP, 2, F])
    v_filt = sb("v_filt", [PARTS, GROUP, 3, F])
    v_y = sb("v_y", [PARTS, GROUP, 3, F])
    dot = sb("dot", [PARTS, GROUP, F])
    edge = sb("edge", [PARTS, 2, GROUP, 8, F])
    summed = sb("summed", [PARTS, 2, GROUP, AGG])
    same = sb("same", [PARTS, 2, GROUP, PARTS])
    psH = ps("psH", 2, [F, GROUP * PARTS])
    psW = ps("psW", 2, [128, GROUP, 4 * F])
    psR = ps("psR", 4, [128, 2, AGG])
    done = chip.sem("dve_done")
    names = ("psH_free", "mag_free", "mag_ready", "hidden_ready", "psW_ready", "psW_free", "edge_ready", "edge_free",
             "psR_ready", "psR_free", "msg_free", "summed_ready", "summed_free", "psH_ready", "same_ready")
    s = {n: chip.sem(n) for n in names}
    radial_in, radial_free = chip.sem2("radial_in"), chip.sem2("radial_free")
    msg_in = [chip.counted(f"msg_in_{b}", 0)[0] for b in range(2)]
    added = [chip.counted(f"added_{b}", 0)[0] for b in range(2)]
    seen = chip.kept_sem("seen")
    ones_ready = chip.sem("ones_ready")

    with nc.Block() as block:

        @block.sync
        def _(sp):
            def load(g, b):
                sp.wait_ge(radial_free[b], 1)
                sp.sem_inc(radial_free[b], -1)
                sp.dma_start(radial[:, b], edge_radial[:, ds(g * (GROUP * PARTS), GROUP * PARTS)]).then_inc(radial_in[b], 16)
            for b in range(2):
                sp.sem_inc(radial_free[b], 1)
            zeroed = chip.sem("zeroed")
            with sp.Fori(0, GROUPS // 2) as i:
                for b in range(2):
                    load(i * 2 + b, b)
                    zero_rows(sp, T, T.agg, D, i * 2 + b, zeroed)
            sp.dma_start(T.srcq_i.rearrange("p t q -> p (t q)"),
                         dst_tiled.rearrange("t p -> (t p)").unsqueeze(0).to_broadcast([PARTS, E])).then_inc(chip.sem("dsts_in"), 16)
            rows_dma(sp, T.agg[N:N + PARTS, :], T.zeros[:, 0:D], zeroed)
            sp.wait_ge(zeroed, (GROUPS + 1) * ROWS_DMA)
            sp.sem_inc(zeroed, -((GROUPS + 1) * ROWS_DMA))
            sp.wait_ge(chip.sem("dsts_in"), 16)
            sp.sem_inc(chip.sem("dsts_in"), -16)
            for b in range(2):
                sp.wait_ge(radial_free[b], 1)
                sp.sem_inc(radial_free[b], -1)

        @block.tensor
        def _(pe):
            def hidden_of(g, b):
                pe.wait_ge(radial_in[b], 16)
                pe.sem_inc(radial_in[b], -16)
                pe.wait_ge(s["psH_free"], 1)
                pe.sem_inc(s["psH_free"], -1)
                nc.tensor.matmul(psH[b][:], W.w1[:], radial[:, b], start=True, stop=True).then_inc(s["psH_ready"], 1)

            def filters(g, b):
                pe.wait_ge(s["hidden_ready"], 1)
                pe.sem_inc(s["hidden_ready"], -1)
                pe.wait_ge(s["psW_free"], 1)
                pe.sem_inc(s["psW_free"], -1)
                for j in range(GROUP):
                    last = nc.tensor.matmul(psW[b][0:PARTS, j], hidden[:, b, j * PARTS:(j + 1) * PARTS], W.w2[:, 0:4 * F],
                                            start=True, stop=True)
                last.then_inc(s["psW_ready"], 1)

            def sums(g, b):
                pe.wait_ge(s["edge_ready"], 1)
                pe.sem_inc(s["edge_ready"], -1)
                pe.wait_ge(s["same_ready"], 1)
                pe.sem_inc(s["same_ready"], -1)
                pe.wait_ge(s["psR_free"], 1)
                pe.sem_inc(s["psR_free"], -1)
                for j in range(GROUP):
                    last = nc.tensor.matmul(psR[2 * b + j // 2][0:PARTS, j % 2], same[:, b, j],
                                            edge[:, b, j].rearrange("p a f -> p (a f)"), start=True, stop=True)
                last.then_inc(s["psR_ready"], 1)

            pe.wait_ge(ones_ready, 1)
            pe.sem_inc(ones_ready, -1)
            hidden_of(0, 0)
            hidden_of(1, 1)
            filters(0, 0)
            with pe.Fori(0, GROUPS // 2 - 1) as i:
                for b in range(2):
                    hidden_of(i * 2 + b + 2, b)
                    filters(i * 2 + b + 1, 1 - b)
                    sums(i * 2 + b, b)
            filters(GROUPS - 1, 1)
            sums(GROUPS - 2, 0)
            sums(GROUPS - 1, 1)

        def halves(act, dve, b):
            return softplus_minus_log2(chip, act, dve, psH[b][:], W.b1[:, 0:1], mag[:, b], hidden[0:F, b],
                                       s["psH_ready"], s["mag_free"], s["mag_ready"], s["hidden_ready"], [s["psH_free"]])

        @block.scalar
        def _(act):
            act.sem_inc(s["psR_free"], 2)
            act.sem_inc(s["edge_free"], 2)

            def softplus(g, b):
                halves(act, None, b)[0]()
                act.sem_inc(radial_free[b], 1)

            def equal_sources(g, b):
                nc.scalar.activation(same[:, b], T.same_src[:, ds(g * GROUP, GROUP)], ACT.Copy).then_inc(s["same_ready"], 1)

            def evacuate(g, b):
                act.wait_ge(s["psR_ready"], 1)
                act.sem_inc(s["psR_ready"], -1)
                act.sem_inc(s["edge_free"], 1)
                act.wait_ge(s["summed_free"], 1)
                act.sem_inc(s["summed_free"], -1)
                adone = chip.sem("act_done")
                for k in range(2):
                    nc.scalar.activation(summed[:, b, 2 * k:2 * k + 2], psR[2 * b + k][0:PARTS], ACT.Copy).then_inc(adone, 1)
                act.wait_ge(adone, 2)
                act.sem_inc(adone, -2)
                act.sem_inc(s["psR_free"], 1)
                act.sem_inc(s["summed_ready"], 1)

            for b in range(2):
                softplus(b, b)
                equal_sources(b, b)
            with act.Fori(0, GROUPS // 2 - 1) as i:
                for b in range(2):
                    softplus(i * 2 + b + 2, b)
                    evacuate(i * 2 + b, b)
                    equal_sources(i * 2 + b + 2, b)
            evacuate(GROUPS - 2, 0)
            evacuate(GROUPS - 1, 1)
            act.wait_ge(s["psR_free"], 2)
            act.sem_inc(s["psR_free"], -2)
            act.wait_ge(s["summed_free"], 2)
            act.sem_inc(s["summed_free"], -2)

        @block.vector
        def _(dve):
            nc.vector.memset(hidden[F:F + 1], 1.0).then_inc(done, 1)
            dve.wait_ge(done, 1)
            dve.sem_inc(done, -1)
            dve.sem_inc(s["psH_free"], 2)
            dve.sem_inc(s["mag_free"], 2)
            dve.sem_inc(s["psW_free"], 2)
            dve.sem_inc(s["msg_free"], 2)
            dve.sem_inc(ones_ready, 1)

            def half(g, b):
                halves(None, dve, b)[1]()

            def products(g, b, i):
                tiles = ds(g * GROUP, GROUP)
                ys = T.y[:, tiles, 0]
                ys3 = bcast(bcast(ys, 3), F)
                yv = bcast(T.y[:, tiles, 1:4], F)
                rcut = T.rcut[:, tiles]
                dve.wait_ge(s["psW_ready"], 1)
                dve.sem_inc(s["psW_ready"], -1)
                nc.vector.tensor_tensor(filt[:].rearrange("p j k f -> p j (k f)"), psW[b][0:PARTS], bcast(rcut, 4 * F),
                                        ALU.mult).then_inc(done, 1)
                dve.wait_ge(done, 1)
                dve.sem_inc(done, -1)
                dve.sem_inc(s["psW_free"], 1)
                dve.wait_ge(msg_in[b], i * (16 * GROUP) + 16 * GROUP)
                dve.sem_inc(seen, 1)
                m = msg[:, b].rearrange("p j (k f) -> p j k f", k=4)
                scalars = m[:, :, 0:1].to_broadcast([PARTS, GROUP, 2, F])
                nc.vector.tensor_tensor(s_filt[:], scalars, filt[:, :, 0:3:2], ALU.mult).then_inc(done, 1)
                nc.vector.tensor_tensor(v_filt[:], m[:, :, 1:4], filt[:, :, 3:4].to_broadcast([PARTS, GROUP, 3, F]),
                                        ALU.mult).then_inc(done, 1)
                nc.vector.tensor_tensor(v_y[:], m[:, :, 1:4], yv, ALU.mult).then_inc(done, 1)
                dve.wait_ge(done, 3)
                dve.sem_inc(done, -3)
                dve.sem_inc(s["msg_free"], 1)
                dve.wait_ge(s["edge_free"], 1)
                dve.sem_inc(s["edge_free"], -1)
                out = edge[:, b]
                nc.vector.tensor_tensor(out[:, :, 0], s_filt[:, :, 0], bcast(ys, F), ALU.mult).then_inc(done, 1)
                nc.vector.tensor_tensor(out[:, :, 2:8:2], s_filt[:, :, 1:2].to_broadcast([PARTS, GROUP, 3, F]), yv,
                                        ALU.mult).then_inc(done, 1)
                nc.vector.tensor_tensor(out[:, :, 3:8:2], v_filt[:], ys3, ALU.mult).then_inc(done, 1)
                nc.vector.tensor_reduce(dot[:], v_y[:].rearrange("p j c f -> p j f c"), AXIS.X, ALU.add).then_inc(done, 1)
                dve.wait_ge(done, 4)
                dve.sem_inc(done, -4)
                nc.vector.scalar_tensor_tensor(out[:, :, 1], dot[:], 1.0 / math.sqrt(3.0), filt[:, :, 1], ALU.mult,
                                               ALU.mult).then_inc(done, 1)
                dve.wait_ge(done, 1)
                dve.sem_inc(done, -1)
                dve.sem_inc(s["edge_ready"], 1)

            half(0, 0)
            half(1, 1)
            with dve.Fori(0, GROUPS // 2 - 1) as i:
                for b in range(2):
                    products(i * 2 + b, b, i)
                    half(i * 2 + b + 2, b)
            for b in range(2):
                products(GROUPS - 2 + b, b, GROUPS // 2 - 1)
            dve.wait_ge(s["psH_free"], 2)
            dve.sem_inc(s["psH_free"], -2)
            dve.wait_ge(s["mag_free"], 2)
            dve.sem_inc(s["mag_free"], -2)
            dve.wait_ge(s["psW_free"], 2)
            dve.sem_inc(s["psW_free"], -2)
            dve.wait_ge(s["edge_free"], 2)
            dve.sem_inc(s["edge_free"], -2)
            dve.wait_ge(s["msg_free"], 2)
            dve.sem_inc(s["msg_free"], -2)

        @block.gpsimd
        def _(pool):
            pooled = chip.sem("pool_done")
            pool.sem_inc(s["summed_free"], 2)

            def gather(g, b):
                pool.wait_ge(s["msg_free"], 1)
                pool.sem_inc(s["msg_free"], -1)
                nc.gpsimd.tensor_copy(gather_i[:, b], T.dst_ext[:, ds(g * GROUP + 1, GROUP)]).then_inc(pooled, 1)
                pool.wait_ge(pooled, 1)
                pool.sem_inc(pooled, -1)
                for j in range(GROUP):
                    nc.gpsimd.indirect_dma_start(out=msg[:, b, j], out_offset=None, in_=T.messages[:, :],
                                                 in_offset=bass.IndirectOffsetOnAxis(ap=gather_i[:, b, j:j + 1], axis=0),
                                                 bounds_check=N - 1).then_inc(msg_in[b], 16)

            def scatter(g, b, first):
                nc.gpsimd.tensor_copy(scatter_i[:, b], T.scat_i[:, ds(g * GROUP, GROUP)]).then_inc(pooled, 1)
                pool.wait_ge(pooled, 1)
                pool.sem_inc(pooled, -1)
                pool.wait_ge(s["summed_ready"], 1)
                pool.sem_inc(s["summed_ready"], -1)
                for j in range(GROUP):
                    if not (first and j < 2):
                        pool.wait_ge(added[j % 2], g * 32 + 16 * (j // 2))
                        pool.sem_inc(seen, 1)
                    if j == 1 and not first:
                        pool.sem_inc(s["summed_free"], 1)
                    nc.gpsimd.indirect_dma_start(out=T.agg_l0[j % 2][:, :],
                                                 out_offset=bass.IndirectOffsetOnAxis(ap=scatter_i[:, b, j:j + 1], axis=0),
                                                 in_=summed[:, b, j], in_offset=None, bounds_check=N + PARTS - 1,
                                                 compute_op=ALU.add).then_inc(added[j % 2], 16)

            gather(0, 0)
            gather(1, 1)
            scatter(0, 0, True)
            with pool.Fori(0, GROUPS // 2 - 1) as i:
                for k, b in enumerate((1, 0)):
                    gather(i * 2 + k + 2, 1 - b)
                    scatter(i * 2 + k + 1, b, False)
            scatter(GROUPS - 1, 1, False)
            for b in range(2):
                pool.wait_ge(added[b], GROUPS * 32)
            pool.sem_inc(s["summed_free"], 1)


def sort_edges(chip, sb, ps, T):
    nc = chip.nc
    COLS, ROWS = PARTS, N // PARTS
    ROUND = 12582912.0
    row, column, before = sb("row", [PARTS, TILES]), sb("column", [PARTS, TILES]), sb("before", [PARTS, TILES])
    iota_i, iota = sb("iota_i", [PARTS, COLS], I32), sb("iota", [PARTS, COLS])
    upper, ones = sb("upper", [ROWS, ROWS]), sb("ones", [ROWS, COLS])
    count, running, start = (sb(n, [ROWS, COLS]) for n in ("count", "running", "start"))
    offset = sb("offset", [ROWS, 1])
    in_row = sb("in_row", [PARTS, 2, GROUP, ROWS])
    in_column = T.same_src
    row_T = sb("row_T", [ROWS, 2, GROUP * PARTS])
    tables = sb("tables", [ROWS, 2, GROUP, COLS])
    equal = sb("equal", [PARTS, 2, GROUP, PARTS])
    product, rank = sb("product", [PARTS, GROUP, COLS]), sb("rank", [PARTS, GROUP])
    pairs = sb("pairs", [PARTS, TILES, 2], I32)
    position, pair = sb("position", [PARTS, 2, GROUP], I32), sb("pair", [PARTS, 2, GROUP, 2], I32)
    rows, row_before, row_after = sb("rows", [PARTS, TILES, 2], I32), sb("row_before", [PARTS, 2], I32), sb("row_after", [PARTS, 2], I32)
    psN, psOff = ps("psN", 1, [128, COLS])[0], ps("psOff", 1, [128, 1])[0]
    psT = ps("psT_s", 2, [128, GROUP * PARTS])
    psG, psU = ps("psG", 2, [128, GROUP, COLS]), ps("psU", 2, [128, GROUP, COLS])
    done, pooled = chip.sem("dve_done"), chip.sem("pool_done")
    names = ("iota_ready", "in_row_ready", "in_row_free", "equal_ready", "earlier_ready", "counted_all", "running_ready",
             "offset_ready", "psT_ready", "row_T_ready", "tables_ready", "psU_ready", "psG_ready", "psG_free",
             "position_ready", "position_free")
    s = {n: chip.sem(n) for n in names}
    placed = [chip.counted(f"placed_{b}", 0)[0] for b in range(2)]
    seen = chip.kept_sem("seen")
    tt, ts, stt, copy = nc.vector.tensor_tensor, nc.vector.tensor_scalar, nc.vector.scalar_tensor_tensor, nc.vector.tensor_copy

    def rows_of_group(dve, g, b):
        dve.wait_ge(s["in_row_free"], 1)
        dve.sem_inc(s["in_row_free"], -1)
        tiles = ds(g * GROUP, GROUP)
        tt(in_row[:, b], iota[:, 0:ROWS].unsqueeze(1).to_broadcast([PARTS, GROUP, ROWS]), bcast(row[:, tiles], ROWS),
           ALU.is_equal).then_inc(done, 1)

    with nc.Block() as block:

        @block.gpsimd
        def _(pool):
            nc.gpsimd.iota(iota_i[:], pattern=[[1, COLS]], base=0, channel_multiplier=0).then_inc(pooled, 1)
            nc.gpsimd.memset(upper[:], 1.0).then_inc(pooled, 1)
            pool.wait_ge(pooled, 2)
            pool.sem_inc(pooled, -2)
            nc.gpsimd.tensor_copy(iota[:], iota_i[:]).then_inc(s["iota_ready"], 1)
            nc.gpsimd.affine_select(out=upper[:], in_=upper[:], compare_op=ALU.is_gt, fill=0.0, base=0,
                                    pattern=[[1, ROWS]], channel_multiplier=-1).then_inc(pooled, 1)
            pool.wait_ge(pooled, 1)
            pool.sem_inc(pooled, -1)
            with pool.Fori(0, GROUPS // 2):
                for b in range(2):
                    pool.wait_ge(s["equal_ready"], 1)
                    pool.sem_inc(s["equal_ready"], -1)
                    nc.gpsimd.tensor_tensor(equal[:, b], equal[:, b], T.lower[:].unsqueeze(1).to_broadcast([PARTS, GROUP, PARTS]),
                                            ALU.mult).then_inc(s["earlier_ready"], 1)

        @block.vector
        def _(dve):
            dst = T.dst_f[:, 1:TILES + 1]
            nc.vector.memset(ones[:], 1.0).then_inc(done, 1)
            ts(row[:], dst, 1.0 / COLS, 0.5 / COLS - 0.5, ALU.mult, ALU.add).then_inc(done, 1)
            dve.wait_ge(done, 2)
            dve.sem_inc(done, -2)
            ts(row[:], row[:], ROUND, None, ALU.add).then_inc(done, 1)
            dve.wait_ge(done, 1)
            dve.sem_inc(done, -1)
            ts(row[:], row[:], -ROUND, None, ALU.add).then_inc(done, 1)
            dve.wait_ge(done, 1)
            dve.sem_inc(done, -1)
            stt(column[:], row[:], -float(COLS), dst, ALU.mult, ALU.add).then_inc(done, 1)
            dve.wait_ge(done, 1)
            dve.sem_inc(done, -1)
            dve.wait_ge(s["iota_ready"], 1)
            dve.sem_inc(s["iota_ready"], -1)
            dve.sem_inc(s["in_row_free"], 2)

            def build(g, b):
                tiles = ds(g * GROUP, GROUP)
                tt(in_column[:, tiles], iota[:].unsqueeze(1).to_broadcast([PARTS, GROUP, COLS]), bcast(column[:, tiles], COLS),
                   ALU.is_equal).then_inc(done, 1)
                tt(equal[:, b], T.srcq_i[:, tiles], bcast(T.dst_ext[:, ds(g * GROUP + 1, GROUP)], PARTS), ALU.is_equal)\
                    .then_inc(s["equal_ready"], 1)
                rows_of_group(dve, g, b)
                dve.wait_ge(done, 2)
                dve.sem_inc(done, -2)
                dve.sem_inc(s["in_row_ready"], 1)

            def count_earlier(g, b):
                dve.wait_ge(s["earlier_ready"], 1)
                dve.sem_inc(s["earlier_ready"], -1)
                nc.vector.tensor_reduce(before[:, ds(g * GROUP, GROUP)], equal[:, b], AXIS.X, ALU.add).then_inc(done, 1)
                dve.wait_ge(done, 1)
                dve.sem_inc(done, -1)

            copy(pairs[:, :, 0], T.src_i[:]).then_inc(done, 1)
            copy(pairs[:, :, 1], T.dst_ext[:, 1:TILES + 1]).then_inc(done, 1)
            dve.wait_ge(done, 2)
            dve.sem_inc(done, -2)
            build(0, 0)
            with dve.Fori(0, GROUPS // 2 - 1) as i:
                for k, b in enumerate((1, 0)):
                    build(i * 2 + k + 1, b)
                    count_earlier(i * 2 + k, 1 - b)
            build(GROUPS - 1, 1)
            count_earlier(GROUPS - 2, 0)
            count_earlier(GROUPS - 1, 1)
            dve.wait_ge(s["in_row_free"], 2)
            dve.sem_inc(s["in_row_free"], -2)
            dve.wait_ge(s["counted_all"], 1)
            dve.sem_inc(s["counted_all"], -1)
            copy(count[:], psN[0:ROWS]).then_inc(done, 1)
            dve.wait_ge(done, 1)
            dve.sem_inc(done, -1)
            nc.vector.tensor_tensor_scan(running[:], ones[:], count[:], 0.0, ALU.mult, ALU.add).then_inc(done, 1)
            dve.wait_ge(done, 1)
            dve.sem_inc(done, -1)
            dve.sem_inc(s["running_ready"], 1)
            tt(start[:], running[:], count[:], ALU.subtract).then_inc(done, 1)
            dve.wait_ge(s["offset_ready"], 1)
            dve.sem_inc(s["offset_ready"], -1)
            copy(offset[:], psOff[0:ROWS]).then_inc(done, 1)
            dve.wait_ge(done, 2)
            dve.sem_inc(done, -2)
            ts(tables[:, 0, 0], start[:], offset[:, 0:1], None, ALU.add).then_inc(done, 1)
            dve.wait_ge(done, 1)
            dve.sem_inc(done, -1)

        @block.tensor
        def _(pe):
            def count_group(g, b, first=False, last=False):
                pe.wait_ge(s["in_row_ready"], 1)
                pe.sem_inc(s["in_row_ready"], -1)
                for j in range(GROUP):
                    add = nc.tensor.matmul(psN[0:ROWS], in_row[:, b, j],
                                           in_column[:, ds(g * GROUP + j, 1)].rearrange("p a c -> p (a c)"),
                                           start=first and j == 0, stop=last and j == GROUP - 1)
                add.then_inc(s["in_row_free"], 1)

            count_group(0, 0, first=True)
            with pe.Fori(0, GROUPS // 2 - 1) as i:
                for k, b in enumerate((1, 0)):
                    count_group(i * 2 + k + 1, b)
            count_group(GROUPS - 1, 1, last=True)
            pe.sem_inc(s["counted_all"], 1)
            pe.wait_ge(s["running_ready"], 1)
            pe.sem_inc(s["running_ready"], -1)
            nc.tensor.matmul(psOff[0:ROWS], upper[:], running[:, COLS - 1:COLS], start=True, stop=True)\
                .then_inc(s["offset_ready"], 1)

    with nc.Block() as block:

        @block.tensor
        def _(pe):
            def additions(g, b):
                pe.wait_ge(s["in_row_ready"], 1)
                pe.sem_inc(s["in_row_ready"], -1)
                for j in range(GROUP):
                    last = nc.tensor.transpose(psT[b][0:ROWS, j * PARTS:(j + 1) * PARTS], in_row[:, b, j],
                                               T.ident[0:PARTS, 0:PARTS])
                last.then_inc(s["psT_ready"], 1)
                for j in range(GROUP):
                    last = nc.tensor.matmul(psU[b][0:ROWS, j], in_row[:, b, j],
                                            in_column[:, ds(g * GROUP + j, 1)].rearrange("p a c -> p (a c)"),
                                            start=True, stop=True)
                last.then_inc(s["psU_ready"], 1)

            def look_up(b):
                pe.wait_ge(s["row_T_ready"], 1)
                pe.sem_inc(s["row_T_ready"], -1)
                pe.wait_ge(s["psG_free"], 1)
                pe.sem_inc(s["psG_free"], -1)
                pe.wait_ge(s["tables_ready"], 1)
                pe.sem_inc(s["tables_ready"], -1)
                for j in range(GROUP):
                    look = nc.tensor.matmul(psG[b][0:PARTS, j], row_T[:, b, j * PARTS:(j + 1) * PARTS], tables[:, b, j],
                                            start=True, stop=True)
                look.then_inc(s["psG_ready"], 1)

            additions(0, 0)
            with pe.Fori(0, GROUPS // 2 - 1) as i:
                for b in range(2):
                    additions(i * 2 + b + 1, 1 - b)
                    look_up(b)
            additions(GROUPS - 1, 1)
            look_up(0)
            look_up(1)

        @block.scalar
        def _(act):
            with act.Fori(0, GROUPS // 2):
                for b in range(2):
                    act.wait_ge(s["psT_ready"], 1)
                    act.sem_inc(s["psT_ready"], -1)
                    nc.scalar.activation(row_T[:, b], psT[b][0:ROWS], ACT.Copy).then_inc(s["row_T_ready"], 1)

        @block.vector
        def _(dve):
            dve.sem_inc(s["in_row_free"], 2)
            dve.sem_inc(s["psG_free"], 2)
            dve.sem_inc(s["position_free"], 2)

            def additions(g, b, more=True):
                dve.wait_ge(s["psU_ready"], 1)
                dve.sem_inc(s["psU_ready"], -1)
                dve.sem_inc(s["in_row_free"], 1)
                for j in range(GROUP):
                    to = tables[:, b, j + 1] if j + 1 < GROUP else tables[:, 1 - b, 0]
                    tt(to, tables[:, b, j], psU[b][0:ROWS, j], ALU.add).then_inc(done, 1)
                    dve.wait_ge(done, 1)
                    dve.sem_inc(done, -1)
                dve.sem_inc(s["tables_ready"], 1)
                if more:
                    rows_of_group(dve, g + 2, b)
                    dve.wait_ge(done, 1)
                    dve.sem_inc(done, -1)
                    dve.sem_inc(s["in_row_ready"], 1)

            def positions(g, b):
                tiles = ds(g * GROUP, GROUP)
                tt(product[:], psG[b][0:PARTS], in_column[:, tiles], ALU.mult).then_inc(done, 1)
                dve.wait_ge(s["position_free"], 1)
                dve.sem_inc(s["position_free"], -1)
                copy(pair[:, b], pairs[:, tiles]).then_inc(done, 1)
                dve.wait_ge(done, 1)
                dve.sem_inc(done, -1)
                dve.sem_inc(s["psG_free"], 1)
                nc.vector.tensor_reduce(rank[:], product[:], AXIS.X, ALU.add).then_inc(done, 1)
                dve.wait_ge(done, 2)
                dve.sem_inc(done, -2)
                tt(rank[:], rank[:], before[:, tiles], ALU.add).then_inc(done, 1)
                dve.wait_ge(done, 1)
                dve.sem_inc(done, -1)
                copy(position[:, b], rank[:]).then_inc(done, 1)
                dve.wait_ge(done, 1)
                dve.sem_inc(done, -1)
                dve.sem_inc(s["position_ready"], 1)

            for b in range(2):
                rows_of_group(dve, b, b)
                dve.wait_ge(done, 1)
                dve.sem_inc(done, -1)
                dve.sem_inc(s["in_row_ready"], 1)
            additions(0, 0)
            with dve.Fori(0, GROUPS // 2 - 2) as i:
                for k, b in enumerate((1, 0)):
                    dve.wait_ge(s["psG_ready"], 1)
                    dve.sem_inc(s["psG_ready"], -1)
                    additions(i * 2 + k + 1, b)
                    positions(i * 2 + k, 1 - b)
            for g in range(GROUPS - 3, GROUPS):
                dve.wait_ge(s["psG_ready"], 1)
                dve.sem_inc(s["psG_ready"], -1)
                additions(g, g % 2, more=g < GROUPS - 2)
                positions(g - 1, (g - 1) % 2)
            dve.wait_ge(s["psG_ready"], 1)
            dve.sem_inc(s["psG_ready"], -1)
            positions(GROUPS - 1, 1)
            dve.wait_ge(s["in_row_free"], 2)
            dve.sem_inc(s["in_row_free"], -2)
            dve.wait_ge(s["psG_free"], 2)
            dve.sem_inc(s["psG_free"], -2)
            dve.wait_ge(s["position_free"], 2)
            dve.sem_inc(s["position_free"], -2)

        @block.gpsimd
        def _(pool):
            def scatter(b):
                pool.wait_ge(s["position_ready"], 1)
                pool.sem_inc(s["position_ready"], -1)
                for j in range(GROUP):
                    nc.gpsimd.indirect_dma_start(out=T.pairs[:, :],
                                                 out_offset=bass.IndirectOffsetOnAxis(ap=position[:, b, j:j + 1], axis=0),
                                                 in_=pair[:, b, j], in_offset=None, bounds_check=N - 1).then_inc(placed[b], 16)

            scatter(0)
            with pool.Fori(0, GROUPS // 2 - 1) as i:
                for b in (1, 0):
                    scatter(b)
                    pool.wait_ge(placed[1 - b], i * (16 * GROUP) + 16 * GROUP)
                    pool.sem_inc(s["position_free"], 1)
            scatter(1)
            for b in range(2):
                pool.wait_ge(placed[b], GROUPS // 2 * 16 * GROUP)
                pool.sem_inc(s["position_free"], 1)

    with nc.Block() as block:

        @block.vector
        def _(dve):
            for neighbour in (row_before, row_after):
                nc.vector.memset(neighbour[:], -1).then_inc(done, 1)
            dve.wait_ge(done, 2)
            dve.sem_inc(done, -2)
            dve.sem_inc(chip.sem("cleared"), 1)
            dve.wait_ge(chip.sem("sorted_in"), 16 * 3)
            dve.sem_inc(chip.sem("sorted_in"), -(16 * 3))
            for to, from_ in ((T.src_i[:], rows[:, :, 0]), (T.dst_ext[:, 1:TILES + 1], rows[:, :, 1]),
                              (T.dst_ext[:, 0:1], row_before[:, 1:2]), (T.dst_ext[:, TILES + 1:TILES + 2], row_after[:, 1:2])):
                copy(to, from_).then_inc(done, 1)
            dve.wait_ge(done, 4)
            dve.sem_inc(done, -4)
            copy(T.dst_f[:], T.dst_ext[:]).then_inc(done, 1)
            dve.wait_ge(done, 1)
            dve.sem_inc(done, -1)

        @block.sync
        def _(sp):
            sorted_rows = T.pairs.rearrange("(p t) c -> p t c", t=TILES)
            sp.dma_start(rows[:], sorted_rows).then_inc(chip.sem("sorted_in"), 16)
            sp.wait_ge(chip.sem("cleared"), 1)
            sp.sem_inc(chip.sem("cleared"), -1)
            sp.dma_start(row_before[1:PARTS], sorted_rows[0:PARTS - 1, TILES - 1]).then_inc(chip.sem("sorted_in"), 16)
            sp.dma_start(row_after[0:PARTS - 1], sorted_rows[1:PARTS, 0]).then_inc(chip.sem("sorted_in"), 16)


def l0_nodes(chip, sb, ps, x, T, W, xT):
    nc = chip.nc
    agg, other = sb("agg_rows", [PARTS, 2, GROUP, AGG]), sb("other_rows", [PARTS, GROUP, AGG])
    xin = sb("xin_d", [PARTS, 2, GROUP, D])
    aT = sb("aT", [128, 2, 2, GROUP * PARTS])
    mag = sb("mag_d", [128, GROUP * PARTS])
    os1 = sb("os1", [128, 2, GROUP * PARTS])
    stats, mv = sb("stats_d", [PARTS, GROUP, 6]), sb("mv_d", [PARTS, 2, GROUP, 2])
    rstd, shift = sb("rstd_d", [PARTS, 2, GROUP]), sb("shift_d", [PARTS, 2, GROUP])
    h = sb("h_d", [PARTS, 2, D])
    psA = ps("psA", 1, [128, 2, 512])[0]
    psO = ps("psO", 1, [128, GROUP * PARTS])[0]
    psX = ps("psX", 2, [128, 4, B])
    psT = ps("psT_d", 2, [128, KC, PARTS])
    done = chip.sem("dve_done")
    names = ("asum_ready", "psA_ready", "aT_ready", "aT_free", "psO_ready", "mag_free", "mag_ready", "os1_ready",
             "psX_ready", "psX_free", "normed", "h_ready", "psT_ready", "psT_free", "other_free")
    s = {n: chip.sem(n) for n in names}
    agg_in, agg_free = chip.sem2("agg_in"), chip.sem2("agg_free")
    var_ready = chip.sem("var_ready")
    x_in, x_free = ([chip.sem2(f"{n}_{b}") for b in range(2)] for n in ("x_half_in", "x_half_free"))
    x1_ready, x1_out = chip.sem2("x1_ready"), chip.sem2("stored")
    pair = GROUP // 2
    tA, tB, tx, tx1 = (tiles_of(a) for a in (T.agg_l0[0][0:N, :], T.agg_l0[1][0:N, :], x, T.x1))

    with nc.Block() as block:

        @block.sync
        def _(sp):
            def load_agg(g, b):
                sp.wait_ge(agg_free[b], 1)
                sp.sem_inc(agg_free[b], -1)
                rows_dma(sp, agg[:, b], tA[:, ds(g * GROUP, GROUP)], agg_in[b])
                sp.wait_ge(s["other_free"], 1)
                sp.sem_inc(s["other_free"], -1)
                rows_dma(sp, other[:], tB[:, ds(g * GROUP, GROUP)], agg_in[b])

            def load_x(g, b):
                sp.wait_ge(x1_out[b], ROWS_DMA)
                sp.sem_inc(x1_out[b], -ROWS_DMA)
                for half in range(2):
                    sp.wait_ge(x_free[b][half], 1)
                    sp.sem_inc(x_free[b][half], -1)
                    rows_dma(sp, xin[:, b, half * pair:half * pair + pair], tx[:, ds(g * GROUP + half * pair, pair)], x_in[b][half])

            def store(g, b):
                sp.wait_ge(x1_ready[b], 1)
                sp.sem_inc(x1_ready[b], -1)
                rows_dma(sp, tx1[:, ds(g * GROUP, GROUP)], xin[:, b], x1_out[b])

            sp.sem_inc(s["other_free"], 1)
            for b in range(2):
                sp.sem_inc(agg_free[b], 1)
                for half in range(2):
                    sp.sem_inc(x_free[b][half], 1)
                sp.sem_inc(x1_out[b], ROWS_DMA)
                load_agg(b, b)
                load_x(b, b)
            load_agg(2, 0)
            load_agg(3, 1)
            store(0, 0)
            with sp.Fori(0, GROUPS // 2 - 2) as i:
                for k, b in enumerate((1, 0)):
                    load_agg(i * 2 + k + 4, 1 - b)
                    store(i * 2 + k + 1, b)
                    load_x(i * 2 + k + 2, 1 - b)
            store(GROUPS - 3, 1)
            load_x(GROUPS - 2, 0)
            store(GROUPS - 2, 0)
            load_x(GROUPS - 1, 1)
            store(GROUPS - 1, 1)
            sp.wait_ge(s["other_free"], 1)
            sp.sem_inc(s["other_free"], -1)
            for b in range(2):
                sp.wait_ge(agg_free[b], 1)
                sp.sem_inc(agg_free[b], -1)
                for half in range(2):
                    sp.wait_ge(x_free[b][half], 1)
                    sp.sem_inc(x_free[b][half], -1)
                sp.wait_ge(x1_out[b], ROWS_DMA)
                sp.sem_inc(x1_out[b], -ROWS_DMA)

        @block.tensor
        def _(pe):
            def out_product(b, j):
                cols = slice(j * PARTS, (j + 1) * PARTS)
                pe.wait_ge(s["psX_free"], 1)
                pe.sem_inc(s["psX_free"], -1)
                nc.tensor.matmul(psX[j % 2][0:PARTS, 0], os1[:, b, cols], W.f2o2_s[:], start=True, stop=True)
                for c, (half, blk) in enumerate(((1, 0), (0, 1), (1, 1))):
                    last = nc.tensor.matmul(psX[j % 2][0:PARTS, 1 + c], aT[:, b, blk, cols], W.vec[:, half],
                                            start=True, stop=True)
                last.then_inc(s["psX_ready"], 1)

            def agg_transposes(b):
                pe.wait_ge(s["asum_ready"], 1)
                pe.sem_inc(s["asum_ready"], -1)
                for blk in range(2):
                    for j in range(GROUP):
                        last = nc.tensor.transpose(psA[:, blk, j * PARTS:(j + 1) * PARTS],
                                                   agg[:, b, j, blk * 128:(blk + 1) * 128], T.ident[0:PARTS, 0:PARTS])
                last.then_inc(s["psA_ready"], 1)

            def scalars(b):
                pe.wait_ge(s["aT_ready"], 1)
                pe.sem_inc(s["aT_ready"], -1)
                pe.sem_inc(agg_free[b], 1)
                nc.tensor.matmul(psO[:], W.f2o1_s[:], aT[:, b, 0], start=True, stop=True).then_inc(s["psO_ready"], 1)

            def h_transpose(j):
                pe.wait_ge(s["h_ready"], 1)
                pe.sem_inc(s["h_ready"], -1)
                pe.wait_ge(s["psT_free"], 1)
                pe.sem_inc(s["psT_free"], -1)
                for c in range(KC):
                    last = nc.tensor.transpose(psT[j % 2][:, c], h[:, j % 2, c * 128:(c + 1) * 128],
                                               T.ident[0:PARTS, 0:PARTS])
                last.then_inc(s["psT_ready"], 1)

            def step(b, first=False, left=2):
                if left > 1:
                    agg_transposes(b)
                for j in range(GROUP):
                    out_product(b, j)
                for j in range(GROUP):
                    if j == GROUP - 1 and left > 0:
                        pe.wait_ge(s["os1_ready"], 1)
                        pe.sem_inc(s["os1_ready"], -1)
                        if left > 1:
                            scalars(b)
                    if not first:
                        h_transpose(j)

            agg_transposes(0)
            scalars(0)
            agg_transposes(1)
            pe.wait_ge(s["os1_ready"], 1)
            pe.sem_inc(s["os1_ready"], -1)
            scalars(1)
            step(0, first=True)
            with pe.Fori(0, GROUPS // 2 - 2):
                step(1)
                step(0)
            step(1)
            step(0, left=1)
            step(1, left=0)
            for j in range(GROUP):
                h_transpose(j)

        def halves(act, dve, b):
            return softplus_minus_log2(chip, act, dve, psO[:], None, mag[:], os1[:, b], s["psO_ready"], s["mag_free"],
                                       s["mag_ready"], s["os1_ready"], [])

        @block.scalar
        def _(act):
            act.sem_inc(s["psT_free"], 2)
            adone = chip.sem("act_done")

            def agg_columns(b):
                act.wait_ge(s["psA_ready"], 1)
                act.sem_inc(s["psA_ready"], -1)
                act.wait_ge(s["aT_free"], 1)
                act.sem_inc(s["aT_free"], -1)
                nc.scalar.activation(aT[:, b], psA[:, :, 0:GROUP * PARTS], ACT.Copy).then_inc(s["aT_ready"], 1)

            def back(g, b):
                act.wait_ge(s["normed"], 1)
                act.sem_inc(s["normed"], -1)

                def relu(j):
                    nc.scalar.activation(h[:, j % 2], xin[:, b, j], ACT.Relu, bias=shift[:, b, j:j + 1],
                                         scale=rstd[:, b, j:j + 1]).then_inc(s["h_ready"], 1)
                relu(0)
                for j in range(GROUP):
                    if j + 1 < GROUP:
                        relu(j + 1)
                    act.wait_ge(s["psT_ready"], 1)
                    act.sem_inc(s["psT_ready"], -1)
                    if j % pair == pair - 1:
                        act.sem_inc(x_free[b][j // pair], 1)
                    nc.scalar.activation(xT[:, :, ds((g * GROUP + j) * PARTS, PARTS)], psT[j % 2][:], ACT.Copy)\
                        .then_inc(adone, 1)
                    if j > 0:
                        act.wait_ge(adone, 1)
                        act.sem_inc(adone, -1)
                        act.sem_inc(s["psT_free"], 1)
                act.wait_ge(adone, 1)
                act.sem_inc(adone, -1)
                act.sem_inc(s["psT_free"], 1)

            agg_columns(0)
            halves(act, None, 0)[0]()
            agg_columns(1)
            halves(act, None, 1)[0]()
            agg_columns(0)
            with act.Fori(0, GROUPS // 2 - 2) as i:
                for k, b in enumerate((1, 0)):
                    halves(act, None, 1 - b)[0]()
                    agg_columns(b)
                    back(i * 2 + k, 1 - b)
            halves(act, None, 0)[0]()
            agg_columns(1)
            back(GROUPS - 4, 0)
            halves(act, None, 1)[0]()
            back(GROUPS - 3, 1)
            back(GROUPS - 2, 0)
            back(GROUPS - 1, 1)
            act.wait_ge(s["psT_free"], 2)
            act.sem_inc(s["psT_free"], -2)

        @block.gpsimd
        def _(pool):
            with pool.Fori(0, GROUPS // 2):
                for b in range(2):
                    layernorm_scales(chip, pool, T, mv[:, b], rstd[:, b], shift[:, b], var_ready, s["normed"])

        @block.vector
        def _(dve):
            dve.sem_inc(s["psX_free"], 2)
            dve.sem_inc(s["mag_free"], 1)
            dve.sem_inc(s["aT_free"], 2)

            def sum_tables(b):
                dve.wait_ge(agg_in[b], 2 * ROWS_DMA)
                dve.sem_inc(agg_in[b], -(2 * ROWS_DMA))
                nc.vector.tensor_tensor(agg[:, b], agg[:, b], other[:], ALU.add).then_inc(done, 1)
                dve.wait_ge(done, 1)
                dve.sem_inc(done, -1)
                dve.sem_inc(s["asum_ready"], 1)
                dve.sem_inc(s["other_free"], 1)

            def output(b):
                for j in range(GROUP):
                    if j % pair == 0:
                        dve.wait_ge(x_in[b][j // pair], ROWS_DMA)
                        dve.sem_inc(x_in[b][j // pair], -ROWS_DMA)
                    dve.wait_ge(s["psX_ready"], 1)
                    dve.sem_inc(s["psX_ready"], -1)
                    if j == GROUP - 1:
                        dve.sem_inc(s["aT_free"], 1)
                    xs, xv = xin[:, b, j, 0:B], xin[:, b, j, B:D].rearrange("p (b c) -> p b c", c=3)
                    out = psX[j % 2][0:PARTS]
                    nc.vector.tensor_tensor(xs, out[:, 0], xs, ALU.add).then_inc(done, 1)
                    nc.vector.tensor_tensor(xv, out[:, 1:4].rearrange("p c b -> p b c"), xv, ALU.add).then_inc(done, 1)
                    dve.wait_ge(done, 2)
                    dve.sem_inc(done, -2)
                    dve.sem_inc(s["psX_free"], 1)
                dve.sem_inc(x1_ready[b], 1)

            def statistics(b):
                layernorm_stats(chip, dve, lambda j: xin[:, b, j], stats, mv[:, b], var_ready)

            def scalars(b):
                halves(None, dve, b)[1]()

            sum_tables(0)
            sum_tables(1)
            scalars(0)
            with dve.Fori(0, GROUPS // 2 - 1):
                for b in range(2):
                    sum_tables(b)
                    output(b)
                    scalars(1 - b)
                    statistics(b)
            output(0)
            scalars(1)
            statistics(0)
            output(1)
            statistics(1)
            dve.wait_ge(s["psX_free"], 2)
            dve.sem_inc(s["psX_free"], -2)
            dve.wait_ge(s["mag_free"], 1)
            dve.sem_inc(s["mag_free"], -1)
            dve.wait_ge(s["aT_free"], 2)
            dve.sem_inc(s["aT_free"], -2)


def attention_masks(chip, sb, ps, T):
    nc = chip.nc
    alike = sb("alike", [PARTS, TILES + 1])
    ends_i, ends = sb("ends_i", [HEADS, 2, PARTS, 2], I32), sb("ends", [HEADS, 2, PARTS])
    from_before, base, cont_end, ends_here = (sb(n, [PARTS, TILES if k < 2 else 1]) for k, n in
                                              enumerate(("from_before", "base", "cont_end", "ends_here")))
    whole = sb("whole", [HEADS, PARTS])
    key, first, fix = sb("key", [PARTS, 1]), sb("first", [PARTS, 1]), sb("fix", [PARTS, 1])
    psF = ps("psF", 1, [128, PARTS])[0]
    done, first_ready = chip.sem("dve_done"), chip.sem("first_ready")

    with nc.Block() as block:

        @block.sync
        def _(sp):
            for n, tile in enumerate((0, TILES - 1)):
                edges = T.pairs.rearrange("(p t) c -> p t c", t=TILES)[:, tile]
                sp.dma_start(ends_i[:, n], edges.unsqueeze(0).to_broadcast([HEADS, PARTS, 2])).then_inc(chip.sem("ends_in"), 16)

        @block.tensor
        def _(pe):
            pe.wait_ge(first_ready, 1)
            pe.sem_inc(first_ready, -1)
            nc.tensor.matmul(psF[0:PARTS], first[:].to_broadcast([PARTS, PARTS]), T.ident[0:PARTS, 0:PARTS],
                             start=True, stop=True).then_inc(chip.sem("psF_ready"), 1)

        @block.vector
        def _(dve):
            def do(*steps):
                for step in steps:
                    step.then_inc(done, 1)
                dve.wait_ge(done, len(steps))
                dve.sem_inc(done, -(len(steps)))
            tt, ts, stt = nc.vector.tensor_tensor, nc.vector.tensor_scalar, nc.vector.scalar_tensor_tensor
            d = T.dst_f
            last = TILES - 1
            dve.wait_ge(chip.sem("ends_in"), 32)
            dve.sem_inc(chip.sem("ends_in"), -32)
            do(tt(alike[:], d[:, 0:TILES + 1], d[:, 1:TILES + 2], ALU.is_equal),
               nc.vector.tensor_copy(ends[:], ends_i[:, :, :, 1]))
            do(nc.vector.tensor_copy(T.same[:], alike[:, 0:TILES]), nc.vector.tensor_copy(T.same_next[:], alike[:, 1:TILES + 1]),
               nc.vector.tensor_copy(cont_end[:], alike[:, TILES:TILES + 1]))
            do(nc.vector.memset(T.same[:, 0:1], 0.0), nc.vector.memset(T.same_next[:, last:TILES], 0.0))
            do(ts(T.same_neg[:], T.same[:], -NEG, NEG, ALU.mult, ALU.add),
               ts(T.next_neg[:], T.same_next[:], -NEG, NEG, ALU.mult, ALU.add),
               nc.vector.tensor_tensor_scan(from_before[:], alike[:, 0:TILES], alike[:, 0:TILES], 1.0, ALU.mult, ALU.min),
               ts(base[:], d[:, 1:TILES + 1], -1.0, T.spare[:, 0:1], ALU.mult, ALU.add),
               stt(key[:], d[:, TILES:TILES + 1], 1.0, cont_end[:], ALU.add, ALU.mult))
            do(tt(base[:], base[:], from_before[:], ALU.mult), ts(key[:], key[:], -1.0, None, ALU.add),
               tt(ends_here[:], from_before[:, last:TILES], cont_end[:], ALU.mult))
            do(tt(base[:], base[:], d[:, 1:TILES + 1], ALU.add),
               tt(ends_here[:], alike[:, 0:1], ends_here[:], ALU.subtract))
            do(stt(base[:], alike[:, 1:TILES + 1], FAR, base[:], ALU.mult, ALU.add),
               stt(first[:], d[:, 1:2], 2.0, ends_here[:], ALU.add, ALU.mult),
               ts(fix[:], ends_here[:], -FAR, FAR, ALU.mult, ALU.add))
            do(nc.vector.tensor_copy(T.row_i[:], base[:]), ts(first[:], first[:], -2.0, None, ALU.add),
               tt(fix[:], fix[:], d[:, 1:2], ALU.add))
            dve.sem_inc(first_ready, 1)
            do(nc.vector.tensor_copy(T.fix_i[:], fix[:]))
            cont = T.cont
            do(nc.vector.memset(cont[:], 0.0))
            do(tt(cont[:, 1:PARTS], ends[:, 1, 0:PARTS - 1], ends[:, 0, 1:PARTS], ALU.is_equal),
               tt(whole[:], ends[:, 0], ends[:, 1], ALU.is_equal))
            do(tt(T.pass_fwd[:], cont[:, 0:PARTS], whole[:], ALU.mult), tt(T.pass_bwd[:], cont[:, 1:PARTS + 1], whole[:], ALU.mult))
            dve.wait_ge(chip.sem("psF_ready"), 1)
            dve.sem_inc(chip.sem("psF_ready"), -1)
            do(ts(T.carry[:], psF[0:PARTS], key[:, 0:1], None, ALU.is_equal))


def project(chip, sb, ps, T, xT, weight, bias, table, scores, normalise):
    nc = chip.nc
    w_high, w_low = sb("w_high", [128, KC, D], F32R), sb("w_low", [128, KC, D], F32R)
    bias_row = None if bias is None else sb("bias_row", [PARTS, D])
    psP = ps("psP", 4, [128, D])
    table_t = tiles_of(table)
    done, adone = chip.sem("dve_done"), chip.sem("act_done")
    names = ("high_done", "split_ready", "split_free", "psP_ready", "psP_free", "w_ready")
    s = {n: chip.sem(n) for n in names}
    row_ready, row_out = chip.sem2("row_ready"), chip.sem2("row_out")

    with ExitStack() as stack:
        raw = stack.enter_context(nc.sbuf_tensor(chip.unique("w_raw"), [128, KC, D], F32))
        with nc.Block() as block:

            @block.sync
            def _(sp):
                sp.dma_start(raw[:], weight.rearrange("(c k) n -> k c n", c=KC)).then_inc(chip.sem("w_in"), 16)
                if bias is not None:
                    sp.dma_start(bias_row[:], bias.unsqueeze(0).to_broadcast([PARTS, D])).then_inc(chip.sem("bias_in"), 16)
                    sp.wait_ge(chip.sem("bias_in"), 16)
                    sp.sem_inc(chip.sem("bias_in"), -16)

            @block.scalar
            def _(act):
                act.wait_ge(chip.sem("w_in"), 16)
                act.sem_inc(chip.sem("w_in"), -16)
                nc.scalar.activation(w_high[:], raw[:], ACT.Copy).then_inc(s["w_ready"], 1)

            @block.vector
            def _(dve):
                dve.wait_ge(s["w_ready"], 1)
                dve.sem_inc(s["w_ready"], -1)
                nc.vector.tensor_tensor(w_low[:], raw[:], w_high[:], ALU.subtract).then_inc(done, 1)
                dve.wait_ge(done, 1)
                dve.sem_inc(done, -1)

    STEP = 2 if scores is None else 1
    x_high, x_low = (sb(n, [128, 2, KC, STEP * PARTS], F32R) for n in ("x_high", "x_low"))
    row = sb("row", [PARTS, 2, D])
    if scores is not None:
        on_pool, on_vector_tile, on_vector_end, on_tensor_end, on_scalar_end = scores(chip, sb, ps, T)

    with nc.Block() as block:

        @block.sync
        def _(sp):
            for b in range(2):
                sp.sem_inc(row_out[b], ROWS_DMA)
            with sp.Fori(0, TILES // 2) as i:
                for b in range(2):
                    sp.wait_ge(row_ready[b], 1)
                    sp.sem_inc(row_ready[b], -1)
                    rows_dma(sp, table_t[:, ds(i * 2 + b, 1)].rearrange("p a d -> p (a d)"), row[:, b], row_out[b])
            for b in range(2):
                sp.wait_ge(row_out[b], ROWS_DMA)
                sp.sem_inc(row_out[b], -ROWS_DMA)

        @block.scalar
        def _(act):
            act.sem_inc(s["psP_free"], 4)

            def split(step, b):
                act.wait_ge(s["split_free"], 1)
                act.sem_inc(s["split_free"], -1)
                if normalise:
                    act.wait_ge(chip.sem("x_normed"), 1)
                    act.sem_inc(chip.sem("x_normed"), -1)
                xs = xT[:, :, ds(step * (STEP * PARTS), STEP * PARTS)]
                nc.scalar.activation(x_high[:, b], xs, ACT.Copy).then_inc(s["high_done"], 1)

            def evacuate(t, n):
                b = n % 2
                act.wait_ge(s["psP_ready"], 1)
                act.sem_inc(s["psP_ready"], -1)
                if n % STEP == STEP - 1:
                    act.sem_inc(s["split_free"], 1)
                act.wait_ge(row_out[b], ROWS_DMA)
                act.sem_inc(row_out[b], -ROWS_DMA)
                nc.scalar.activation(row[:, b], psP[n][0:PARTS], ACT.Copy).then_inc(adone, 1)
                act.wait_ge(adone, 1)
                act.sem_inc(adone, -1)
                act.sem_inc(s["psP_free"], 1)
                act.sem_inc(row_ready[b] if bias is None else chip.sem("to_bias"), 1)

            act.sem_inc(s["split_free"], 2)
            split(0, 0)
            split(1, 1)
            with act.Fori(0, TILES // 4 - 1) as i:
                for n in range(4):
                    evacuate(i * 4 + n, n)
                    if n % STEP == STEP - 1:
                        split(i * (4 // STEP) + n // STEP + 2, n // STEP % 2)
            for n in range(4):
                evacuate(TILES - 4 + n, n)
                if STEP == 1 and n < 2:
                    split(TILES - 2 + n, n)
            act.wait_ge(s["psP_free"], 4)
            act.sem_inc(s["psP_free"], -4)
            act.wait_ge(s["split_free"], 2)
            act.sem_inc(s["split_free"], -2)
            if scores is not None:
                on_scalar_end(act)

        @block.gpsimd
        def _(pool):
            if scores is not None:
                on_pool(pool)
            if bias is not None:
                with pool.Fori(0, TILES // 2) as i:
                    for b in range(2):
                        pool.wait_ge(chip.sem("to_bias"), 1)
                        pool.sem_inc(chip.sem("to_bias"), -1)
                        nc.gpsimd.tensor_tensor(row[:, b], row[:, b], bias_row[:], ALU.add).then_inc(row_ready[b], 1)

        @block.vector
        def _(dve):
            def split(step, b):
                dve.wait_ge(s["high_done"], 1)
                dve.sem_inc(s["high_done"], -1)
                xs = xT[:, :, ds(step * (STEP * PARTS), STEP * PARTS)]
                nc.vector.tensor_tensor(x_low[:, b], xs, x_high[:, b], ALU.subtract).then_inc(s["split_ready"], 1)

            def norm(step):
                cols = ds(step * (STEP * PARTS), STEP * PARTS)
                for m in range(KC):
                    nc.vector.tensor_scalar(xT[:, m, cols], xT[:, m, cols], T.bn_scale[:, m:m + 1], T.bn_off[:, m:m + 1],
                                            ALU.mult, ALU.add).then_inc(done, 1)
                dve.wait_ge(done, KC)
                dve.sem_inc(done, -KC)
                dve.sem_inc(chip.sem("x_normed"), 1)

            if scores is None:
                if normalise:
                    norm(0)
                    norm(1)
                with dve.Fori(0, TILES // STEP // 2 - 1) as i:
                    for b in range(2):
                        split(i * 2 + b, b)
                        if normalise:
                            norm(i * 2 + b + 2)
                for b in range(2):
                    split(TILES // STEP - 2 + b, b)
            else:
                turn = 2 * SLOTS
                with dve.Fori(0, TILES // turn) as i:
                    for n in range(turn):
                        split(i * turn + n, n % 2)
                        on_vector_tile(dve, i * turn + n, n % SLOTS, i * 2 + n // SLOTS)
                for n in range(TILES % turn):
                    split(TILES // turn * turn + n, n % 2)
                    on_vector_tile(dve, TILES // turn * turn + n, n % SLOTS, TILES // turn * 2 + n // SLOTS)
                on_vector_end(dve)

        @block.tensor
        def _(pe):
            with pe.Fori(0, TILES // 8):
                for k in range(8):
                    b, j = k // STEP % 2, k % STEP
                    if k % 2 == 0:
                        pe.wait_ge(s["psP_free"], 2)
                        pe.sem_inc(s["psP_free"], -2)
                    if j == 0:
                        pe.wait_ge(s["split_ready"], 1)
                        pe.sem_inc(s["split_ready"], -1)
                    parts = [(x, w, c) for c in range(KC)
                             for x, w in ((x_high, w_high), (x_high, w_low), (x_low, w_high))]
                    for n, (x, w, c) in enumerate(parts):
                        last = nc.tensor.matmul(psP[k % 4][0:PARTS], x[:, b, c, j * PARTS:(j + 1) * PARTS], w[:, c], start=n == 0,
                                                stop=n == len(parts) - 1)
                    last.then_inc(s["psP_ready"], 1)
            if scores is not None:
                on_tensor_end(pe)


def scores_and_softmax(chip, sb, ps, T):
    nc = chip.nc
    q, k = sb("q_rows", [PARTS, SLOTS, D]), sb("k_rows", [PARTS, SLOTS, D])
    index = sb("index", [PARTS, SLOTS, 2], I32)
    score = T.weight
    work = [x[:].rearrange("p b d -> p (b d)")[:, 0:HEADS * TILES].rearrange("p (h t) -> p h t", h=HEADS)
            for x in (q, k)]
    edge_cols = sb("edge_cols", [PARTS, 2, HEADS])
    over = q[0:HEADS].rearrange("p b d -> p (b d)")[:, HEADS * TILES:HEADS * TILES + 6 * PARTS]\
        .rearrange("p (n q) -> p n q", n=6)
    masks = k[0:HEADS].rearrange("p b d -> p (b d)")[:, HEADS * TILES:HEADS * TILES + 3 * PARTS]\
        .rearrange("p (n q) -> p n q", n=3)
    psS = ps("psS", 1, [HEADS, 2, PARTS])[0]
    psC = ps("psC", 1, [128, 2, HEADS])[0]
    done = chip.sem("dve_done")
    came, before = zip(*(chip.counted(f"qk_in_{b}", len(range(b, TILES, SLOTS)) * 32) for b in range(SLOTS)))
    free, seen, pooled = chip.sem("qk_free"), chip.kept_sem("seen"), chip.sem("pool_done")
    cols_ready, psS_ready, rows_ready, psC_ready = (chip.sem(n) for n in ("cols_ready", "psS_ready", "rows_ready", "psC_ready"))

    def on_pool(pool):
        pool.sem_inc(free, SLOTS)

        def gather(t, b):
            pool.wait_ge(free, 1)
            pool.sem_inc(free, -1)
            nc.gpsimd.tensor_copy(index[:, b, 0:1], T.dst_ext[:, ds(t + 1, 1)]).then_inc(pooled, 1)
            nc.gpsimd.tensor_copy(index[:, b, 1:2], T.src_i[:, ds(t, 1)]).then_inc(pooled, 1)
            pool.wait_ge(pooled, 2)
            pool.sem_inc(pooled, -2)
            for n, (rows, table) in enumerate(((q, T.q), (k, T.k))):
                nc.gpsimd.indirect_dma_start(out=rows[:, b], out_offset=None, in_=table[:, :],
                                             in_offset=bass.IndirectOffsetOnAxis(ap=index[:, b, n:n + 1], axis=0),
                                             bounds_check=N - 1).then_inc(came[b], 16)

        with pool.Fori(0, TILES // SLOTS) as i:
            for b in range(SLOTS):
                gather(i * SLOTS + b, b)
        for b in range(TILES % SLOTS):
            gather(TILES // SLOTS * SLOTS + b, b)
        pool.wait_ge(free, SLOTS)
        pool.sem_inc(free, -SLOTS)

    def on_vector_tile(dve, t, b, earlier):
        dve.wait_ge(came[b], earlier * 32 + (before[b] + 32))
        dve.sem_inc(seen, 1)
        nc.vector.tensor_tensor(q[:, b], q[:, b], k[:, b], ALU.mult).then_inc(done, 1)
        dve.wait_ge(done, 1)
        dve.sem_inc(done, -1)
        nc.vector.tensor_reduce(score[:, :, ds(t, 1)].rearrange("p h a -> p (h a)"),
                                q[:, b].rearrange("p (h d) -> p h d", h=HEADS), AXIS.X, ALU.add).then_inc(done, 1)
        dve.wait_ge(done, 1)
        dve.sem_inc(done, -1)
        dve.sem_inc(free, 1)

    def scan(out, mask, data, op0, op1, backward=False):
        way = slice(None, None, -1) if backward else slice(None)
        return [nc.vector.tensor_tensor_scan(out[:, h, way], mask[:, way], data[:, h, way], 0.0, op0, op1)
                for h in range(HEADS)]

    def on_vector_end(dve):
        def do(*steps):
            for step in steps:
                step.then_inc(done, 1)
            dve.wait_ge(done, len(steps))
            dve.sem_inc(done, -(len(steps)))
        tt, ts, copy = nc.vector.tensor_tensor, nc.vector.tensor_scalar, nc.vector.tensor_copy
        last = TILES - 1
        a, m = work
        do(ts(score[:], score[:], float(HD) ** -0.5, None, ALU.mult))

        def across(first, last_col, maximum):
            do(copy(edge_cols[:, 0], last_col), copy(edge_cols[:, 1], first))
            dve.sem_inc(cols_ready, 1)
            dve.wait_ge(psS_ready, 1)
            dve.sem_inc(psS_ready, -1)
            do(copy(over[:, 0:2], psS[:]))
            fwd, bwd, cont = T.pass_fwd[:], T.pass_bwd[:], T.cont[:, 1:PARTS]
            if maximum:
                do(ts(masks[:, 0], fwd, -NEG, NEG, ALU.mult, ALU.add), ts(masks[:, 1], bwd, -NEG, NEG, ALU.mult, ALU.add),
                   ts(masks[:, 2, 0:PARTS - 1], cont, -NEG, NEG, ALU.mult, ALU.add))
                fwd, bwd, cont = masks[:, 0], masks[:, 1], masks[:, 2, 0:PARTS - 1]
            op, use = ((ALU.add, ALU.max), ALU.add) if maximum else ((ALU.mult, ALU.add), ALU.mult)
            back = op if maximum else (ALU.mult, ALU.max)
            do(nc.vector.tensor_tensor_scan(over[:, 2], fwd, over[:, 0], 0.0, *op),
               nc.vector.tensor_tensor_scan(over[:, 3, ::-1], bwd[:, ::-1], over[:, 1, ::-1], 0.0, *back),
               nc.vector.memset(over[:, 4:6], NEG if maximum else 0.0))
            do(tt(over[:, 4, 1:PARTS], over[:, 2, 0:PARTS - 1], cont, use),
               tt(over[:, 5, 0:PARTS - 1], over[:, 3, 1:PARTS], cont, use))
            dve.sem_inc(rows_ready, 1)
            dve.wait_ge(psC_ready, 1)
            dve.sem_inc(psC_ready, -1)

        do(*scan(a, T.same_neg, score, ALU.add, ALU.max), *scan(m, T.next_neg, score, ALU.add, ALU.max, True))
        across(m[:, :, 0], a[:, :, last], True)
        do(copy(a, score[:]))
        do(tt(a[:, :, 0], psC[0:PARTS, 0], a[:, :, 0], ALU.max))
        do(tt(a[:, :, last], psC[0:PARTS, 1], a[:, :, last], ALU.max))
        do(*scan(m, T.same_neg, a, ALU.add, ALU.max))
        do(*scan(a, T.next_neg, m, ALU.add, ALU.max, True))
        do(tt(score[:], score[:], a, ALU.subtract))
        dve.sem_inc(chip.sem("shifted"), 1)
        dve.wait_ge(chip.sem("exp_ready"), 1)
        dve.sem_inc(chip.sem("exp_ready"), -1)
        do(*scan(a, T.same, score, ALU.mult, ALU.add))
        across(a[:, :, 0], a[:, :, last], False)
        do(copy(m, score[:]))
        do(tt(m[:, :, 0], psC[0:PARTS, 0], m[:, :, 0], ALU.add))
        do(*scan(a, T.same, m, ALU.mult, ALU.add))
        do(*scan(m, T.same_next, a, ALU.mult, ALU.max, True))
        across(m[:, :, 0], a[:, :, last], False)
        do(tt(a[:, :, last], psC[0:PARTS, 1], a[:, :, last], ALU.max))
        do(*scan(m, T.same_next, a, ALU.mult, ALU.max, True))
        do(ts(m, m, 1e-16, None, ALU.add))
        do(nc.vector.reciprocal(m, m))
        do(tt(score[:], score[:], m, ALU.mult))

    def on_tensor_end(pe):
        for _ in range(3):
            pe.wait_ge(cols_ready, 1)
            pe.sem_inc(cols_ready, -1)
            for n in range(2):
                t = nc.tensor.transpose(psS[:, n], edge_cols[:, n], T.ident[0:PARTS, 0:PARTS])
            t.then_inc(psS_ready, 1)
            pe.wait_ge(rows_ready, 1)
            pe.sem_inc(rows_ready, -1)
            for n in range(2):
                t = nc.tensor.transpose(psC[0:PARTS, n], over[:, 4 + n], T.ident[0:HEADS, 0:HEADS])
            t.then_inc(psC_ready, 1)

    def on_scalar_end(act):
        act.wait_ge(chip.sem("shifted"), 1)
        act.sem_inc(chip.sem("shifted"), -1)
        nc.scalar.activation(score[:], score[:], ACT.Exp).then_inc(chip.sem("exp_ready"), 1)

    return on_pool, on_vector_tile, on_vector_end, on_tensor_end, on_scalar_end


def aggregate(chip, sb, ps, T):
    nc = chip.nc
    v, weighted, acc = sb("v_rows", [PARTS, GROUP, D]), sb("weighted", [PARTS, D]), sb("acc", [PARTS, GROUP, D])
    v_index, row_index = sb("v_index", [PARTS, 2, GROUP], I32), sb("row_index", [PARTS, 2, GROUP], I32)
    psF = ps("psFix", 1, [128, D])[0]
    done, pooled, seen = chip.sem("dve_done"), chip.sem("pool_done"), chip.kept_sem("seen")
    v_in, v_before = zip(*(chip.counted(f"v_in_{n}", GROUPS * 16) for n in range(GROUP)))
    out, out_before = zip(*(chip.counted(f"acc_out_{n}", GROUPS * 16) for n in range(GROUP)))
    fixed, fixed_before = chip.counted("fixed", 16)
    v_free, acc_ready, acc_free = chip.sem("v_free"), chip.sem("acc_ready"), chip.sem("acc_free")

    with nc.Block() as block:

        @block.gpsimd
        def _(pool):
            pool.sem_inc(acc_free, GROUP)

            def gather(b, n):
                pool.wait_ge(v_free, 1)
                pool.sem_inc(v_free, -1)
                nc.gpsimd.indirect_dma_start(out=v[:, n], out_offset=None, in_=T.v[:, :],
                                             in_offset=bass.IndirectOffsetOnAxis(ap=v_index[:, b, n:n + 1], axis=0),
                                             bounds_check=N - 1).then_inc(v_in[n], 16)

            def scatter(b, n, groups_before):
                pool.wait_ge(acc_ready, 1)
                pool.sem_inc(acc_ready, -1)
                nc.gpsimd.indirect_dma_start(out=T.agg[:, :], out_offset=bass.IndirectOffsetOnAxis(ap=row_index[:, b, n:n + 1], axis=0),
                                             in_=acc[:, n], in_offset=None, bounds_check=N + PARTS - 1,
                                             oob_is_err=False).then_inc(out[n], 16)
                if n >= 2:
                    pool.wait_ge(out[n - 2], (0 if groups_before is None else groups_before * 16) + (out_before[n - 2] + 16))
                    pool.sem_inc(acc_free, 1)
                elif groups_before is not None:
                    pool.wait_ge(out[n + 2], groups_before * 16 + out_before[n + 2])
                    pool.sem_inc(acc_free, 1)

            def indices(to, table, g):
                nc.gpsimd.tensor_copy(to, table[:, ds(g * GROUP, GROUP)]).then_inc(pooled, 1)
                pool.wait_ge(pooled, 1)
                pool.sem_inc(pooled, -1)

            def step(g, b, first=False, last=False):
                if not last:
                    indices(v_index[:, 1 - b], T.src_i, g + 1)
                indices(row_index[:, b], T.row_i, g)
                for n in range(GROUP):
                    if not last:
                        gather(1 - b, n)
                    scatter(b, n, None if first else g)

            indices(v_index[:, 0], T.src_i, 0)
            for n in range(GROUP):
                gather(0, n)
            step(0, 0, first=True)
            with pool.Fori(0, GROUPS // 2 - 1) as i:
                for k, b in enumerate((1, 0)):
                    step(i * 2 + k + 1, b)
            step(GROUPS - 1, 1, last=True)
            for n in (GROUP - 2, GROUP - 1):
                pool.wait_ge(out[n], out_before[n] + GROUPS * 16)
                pool.sem_inc(acc_free, 1)
            pool.wait_ge(v_free, GROUP)
            pool.sem_inc(v_free, -GROUP)
            pool.sem_inc(chip.sem("rows_out"), 1)
            pool.wait_ge(chip.sem("fix_ready"), 1)
            pool.sem_inc(chip.sem("fix_ready"), -1)
            nc.gpsimd.indirect_dma_start(out=T.agg[:, :], out_offset=bass.IndirectOffsetOnAxis(ap=T.fix_i[:, 0:1], axis=0),
                                         in_=weighted[:], in_offset=None, bounds_check=N - 1,
                                         oob_is_err=False).then_inc(fixed, 16)
            pool.wait_ge(fixed, fixed_before + 16)
            pool.sem_inc(seen, 1)

        @block.vector
        def _(dve):
            nc.vector.memset(acc[:, GROUP - 1], 0.0).then_inc(done, 1)
            dve.wait_ge(done, 1)
            dve.sem_inc(done, -1)
            dve.sem_inc(v_free, GROUP)
            with dve.Fori(0, GROUPS) as g:
                for n in range(GROUP):
                    t = ds(g * GROUP + n, 1)
                    dve.wait_ge(v_in[n], g * 16 + (v_before[n] + 16))
                    dve.sem_inc(seen, 1)
                    w = T.weight[:, :, t].to_broadcast([PARTS, HEADS, HD])
                    nc.vector.tensor_tensor(weighted[:].rearrange("p (h d) -> p h d", h=HEADS),
                                            v[:, n].rearrange("p (h d) -> p h d", h=HEADS), w, ALU.mult).then_inc(done, 1)
                    dve.wait_ge(done, 1)
                    dve.sem_inc(done, -1)
                    dve.sem_inc(v_free, 1)
                    dve.wait_ge(acc_free, 1)
                    dve.sem_inc(acc_free, -1)
                    nc.vector.scalar_tensor_tensor(acc[:, n], acc[:, (n - 1) % GROUP], T.same[:, t], weighted[:], ALU.mult,
                                                   ALU.add).then_inc(done, 1)
                    dve.wait_ge(done, 1)
                    dve.sem_inc(done, -1)
                    dve.sem_inc(acc_ready, 1)
            dve.wait_ge(acc_free, GROUP)
            dve.sem_inc(acc_free, -GROUP)
            dve.sem_inc(chip.sem("last_acc"), 1)
            dve.wait_ge(chip.sem("side_in"), ROWS_DMA)
            dve.sem_inc(chip.sem("side_in"), -ROWS_DMA)
            dve.wait_ge(chip.sem("psFix_ready"), 1)
            dve.sem_inc(chip.sem("psFix_ready"), -1)
            nc.vector.tensor_tensor(weighted[:], psF[0:PARTS], v[:, 0], ALU.add).then_inc(chip.sem("fix_ready"), 1)

        @block.sync
        def _(sp):
            sp.wait_ge(chip.sem("rows_out"), 1)
            sp.sem_inc(chip.sem("rows_out"), -1)
            rows_dma(sp, v[:, 0], T.agg[N:N + PARTS, :], chip.sem("side_in"))

        @block.tensor
        def _(pe):
            pe.wait_ge(chip.sem("last_acc"), 1)
            pe.sem_inc(chip.sem("last_acc"), -1)
            nc.tensor.matmul(psF[0:PARTS], T.carry[:], acc[:, GROUP - 1], start=True, stop=True).then_inc(chip.sem("psFix_ready"), 1)


HALF = 2
HCOLS = HALF * PARTS
HSTEPS = TILES // HALF


def output_projection(chip, sb, ps, T, xT, weight, bias):
    nc = chip.nc
    w_high, w_low = sb("wo_high", [128, KC, D], F32R), sb("wo_low", [128, KC, D], F32R)
    bias_col = sb("bo_col", [128, KC])
    psT, psY = ps("psT_o", 4, [128, 2, HCOLS]), ps("psY", 4, [128, 2, HCOLS])
    agg_t = tiles_of(T.agg[0:N, :])
    done, adone = chip.sem("dve_done"), chip.sem("act_done")
    rows_in, rows_free = chip.sem2("rows_in"), chip.sem2("rows_free")
    names = ("psT_ready", "psT_free", "high_done", "split_ready", "split_free", "psY_ready", "psY_free", "w_ready")
    s = {n: chip.sem(n) for n in names}

    with ExitStack() as stack:
        raw = stack.enter_context(nc.sbuf_tensor(chip.unique("wo_raw"), [128, KC, D], F32))
        with nc.Block() as block:

            @block.sync
            def _(sp):
                sp.dma_start(raw[:], weight.rearrange("(c k) n -> k c n", c=KC)).then_inc(chip.sem("w_in"), 16)
                sp.dma_start(bias_col[:], bias).then_inc(chip.sem("bias_in"), 16)
                sp.wait_ge(chip.sem("bias_in"), 16)
                sp.sem_inc(chip.sem("bias_in"), -16)

            @block.scalar
            def _(act):
                act.wait_ge(chip.sem("w_in"), 16)
                act.sem_inc(chip.sem("w_in"), -16)
                nc.scalar.activation(w_high[:], raw[:], ACT.Copy).then_inc(s["w_ready"], 1)

            @block.vector
            def _(dve):
                dve.wait_ge(s["w_ready"], 1)
                dve.sem_inc(s["w_ready"], -1)
                nc.vector.tensor_tensor(w_low[:], raw[:], w_high[:], ALU.subtract).then_inc(done, 1)
                dve.wait_ge(done, 1)
                dve.sem_inc(done, -1)

    rows = sb("agg_rows", [PARTS, HALF, D])
    a_high, a_low = sb("a_high", [128, 2, KC, HCOLS], F32R), sb("a_low", [128, 2, KC, HCOLS], F32R)
    with nc.Block() as block:

        @block.sync
        def _(sp):
            for b in range(2):
                sp.sem_inc(rows_free[b], 1)
            with sp.Fori(0, HSTEPS) as i:
                for j in range(HALF):
                    sp.wait_ge(rows_free[j], 1)
                    sp.sem_inc(rows_free[j], -1)
                    rows_dma(sp, rows[:, j], agg_t[:, ds(i * HALF + j, 1)].rearrange("p a d -> p (a d)"), rows_in[j])
            for b in range(2):
                sp.wait_ge(rows_free[b], 1)
                sp.sem_inc(rows_free[b], -1)

        @block.tensor
        def _(pe):
            def transposes(b):
                pe.wait_ge(s["psT_free"], 1)
                pe.sem_inc(s["psT_free"], -1)
                for j in range(HALF):
                    pe.wait_ge(rows_in[j], ROWS_DMA)
                    pe.sem_inc(rows_in[j], -ROWS_DMA)
                    for c in range(KC):
                        last = nc.tensor.transpose(psT[2 * b + c // 2][:, c % 2, j * PARTS:(j + 1) * PARTS],
                                                   rows[:, j, c * 128:(c + 1) * 128], T.ident[0:PARTS, 0:PARTS])
                    last.then_inc(s["psT_ready"], 1)

            def products(b):
                pe.wait_ge(s["split_ready"], 1)
                pe.sem_inc(s["split_ready"], -1)
                pe.wait_ge(s["psY_free"], 1)
                pe.sem_inc(s["psY_free"], -1)
                for m in range(KC):
                    parts = [(w, a, c) for c in range(KC) for w, a in ((w_high, a_high), (w_low, a_high), (w_high, a_low))]
                    for n, (w, a, c) in enumerate(parts):
                        last = nc.tensor.matmul(psY[2 * b + m // 2][:, m % 2], w[:, c, m * 128:(m + 1) * 128], a[:, b, c],
                                                start=n == 0, stop=n == len(parts) - 1)
                last.then_inc(s["psY_ready"], 1)

            transposes(0)
            with pe.Fori(0, HSTEPS // 2 - 1) as i:
                transposes(1)
                products(0)
                transposes(0)
                products(1)
            transposes(1)
            products(0)
            products(1)

        @block.scalar
        def _(act):
            act.sem_inc(s["split_free"], 2)
            with act.Fori(0, HSTEPS // 2) as i:
                for b in range(2):
                    for j in range(HALF):
                        act.wait_ge(s["psT_ready"], 1)
                        act.sem_inc(s["psT_ready"], -1)
                        act.sem_inc(rows_free[j], 1)
                    act.wait_ge(s["split_free"], 1)
                    act.sem_inc(s["split_free"], -1)
                    for k in range(2):
                        nc.scalar.activation(a_high[:, b, 2 * k:2 * k + 2], psT[2 * b + k][:], ACT.Copy).then_inc(adone, 1)
                    act.wait_ge(adone, 2)
                    act.sem_inc(adone, -2)
                    act.sem_inc(s["high_done"], 1)
            act.wait_ge(s["split_free"], 2)
            act.sem_inc(s["split_free"], -2)

        @block.vector
        def _(dve):
            dve.sem_inc(s["psT_free"], 2)
            dve.sem_inc(s["psY_free"], 2)

            def split(b):
                dve.wait_ge(s["high_done"], 1)
                dve.sem_inc(s["high_done"], -1)
                for k in range(2):
                    nc.vector.tensor_tensor(a_low[:, b, 2 * k:2 * k + 2], psT[2 * b + k][:], a_high[:, b, 2 * k:2 * k + 2],
                                            ALU.subtract).then_inc(done, 1)
                dve.wait_ge(done, 2)
                dve.sem_inc(done, -2)
                dve.sem_inc(s["psT_free"], 1)
                dve.sem_inc(s["split_ready"], 1)

            def add(step, b):
                dve.wait_ge(s["psY_ready"], 1)
                dve.sem_inc(s["psY_ready"], -1)
                dve.sem_inc(s["split_free"], 1)
                cols = ds(step * HCOLS, HCOLS)
                for m in range(KC):
                    nc.vector.scalar_tensor_tensor(xT[:, m, cols], psY[2 * b + m // 2][:, m % 2], bias_col[:, m:m + 1],
                                                   xT[:, m, cols], ALU.add, ALU.add).then_inc(done, 1)
                dve.wait_ge(done, KC)
                dve.sem_inc(done, -KC)
                dve.sem_inc(s["psY_free"], 1)
                for m in range(KC):
                    nc.vector.bn_stats(out=T.bn_stats[:, m, ds(step, 1)].rearrange("p a s -> p (a s)"),
                                       in_=xT[:, m, cols]).then_inc(done, 1)
                dve.wait_ge(done, KC)
                dve.sem_inc(done, -KC)

            split(0)
            with dve.Fori(0, HSTEPS // 2 - 1) as i:
                split(1)
                add(i * 2, 0)
                split(0)
                add(i * 2 + 1, 1)
            split(1)
            add(HSTEPS - 2, 0)
            add(HSTEPS - 1, 1)
            dve.wait_ge(s["psT_free"], 2)
            dve.sem_inc(s["psT_free"], -2)
            dve.wait_ge(s["psY_free"], 2)
            dve.sem_inc(s["psY_free"], -2)


def batchnorm(chip, sb, T, xT, gain, shift, steps, apply):
    nc = chip.nc
    g, b_ = sb("bn_gain", [128, KC]), sb("bn_shift", [128, KC])
    mv, scale, off = sb("bn_mv", [128, KC, 2]), T.bn_scale, T.bn_off
    done, adone, pooled = chip.sem("dve_done"), chip.sem("act_done"), chip.sem("pool_done")
    with nc.Block() as block:

        @block.sync
        def _(sp):
            for out, in_ in ((g, gain), (b_, shift)):
                sp.dma_start(out[:], in_).then_inc(chip.sem("bn_in"), 16)

        @block.gpsimd
        def _(pool):
            pool.wait_ge(chip.sem("bn_aggregated"), 1)
            pool.sem_inc(chip.sem("bn_aggregated"), -1)
            pool.wait_ge(chip.sem("bn_in"), 32)
            pool.sem_inc(chip.sem("bn_in"), -32)

            def do(step):
                step.then_inc(pooled, 1)
                pool.wait_ge(pooled, 1)
                pool.sem_inc(pooled, -1)
            do(nc.gpsimd.tensor_scalar(scale[:], mv[:, :, 1], BN_EPS, None, ALU.add))
            do(nc.gpsimd.tensor_tensor(scale[:], scale[:], T.minus_half[:].to_broadcast([128, KC]), ALU.pow))
            do(nc.gpsimd.tensor_tensor(scale[:], scale[:], g[:], ALU.mult))
            do(nc.gpsimd.tensor_tensor(off[:], mv[:, :, 0], scale[:], ALU.mult))
            do(nc.gpsimd.tensor_tensor(off[:], b_[:], off[:], ALU.subtract))
            if apply:
                pool.sem_inc(chip.sem("bn_scales_v"), 1)
                pool.sem_inc(chip.sem("bn_scales_a"), 1)

        @block.vector
        def _(dve):
            for m in range(KC):
                nc.vector.bn_aggr(out=mv[:, m], in_=T.bn_stats[:, m, 0:steps]).then_inc(done, 1)
            dve.wait_ge(done, KC)
            dve.sem_inc(done, -KC)
            dve.sem_inc(chip.sem("bn_aggregated"), 1)
            if apply:
                dve.wait_ge(chip.sem("bn_scales_v"), 1)
                dve.sem_inc(chip.sem("bn_scales_v"), -1)
                for m in range(3):
                    width = N if m < 2 else N // 2
                    nc.vector.tensor_scalar(xT[:, m, 0:width], xT[:, m, 0:width], scale[:, m:m + 1], off[:, m:m + 1],
                                            ALU.mult, ALU.add).then_inc(done, 1)
                dve.wait_ge(done, 3)
                dve.sem_inc(done, -3)

        @block.scalar
        def _(act):
            if apply:
                act.wait_ge(chip.sem("bn_scales_a"), 1)
                act.sem_inc(chip.sem("bn_scales_a"), -1)
                for m, start in ((3, 0), (2, N // 2)):
                    nc.scalar.activation(xT[:, m, start:N], xT[:, m, start:N], ACT.Identity, bias=off[:, m:m + 1],
                                         scale=scale[:, m:m + 1]).then_inc(adone, 1)
                act.wait_ge(adone, 2)
                act.sem_inc(adone, -2)


def feed_forward(chip, sb, ps, T, xT, w1, b1, w2, b2):
    nc = chip.nc
    cols_n = GROUP * PARTS
    w1_high, w1_low = sb("w1_high", [128, KC, 2 * FF], F32R), sb("w1_low", [128, KC, 2 * FF], F32R)
    w2_high, w2_low = sb("w2_high", [2 * FF, D], F32R), sb("w2_low", [2 * FF, D], F32R)
    b1_col, b2_col = sb("b1_col", [2 * FF, 1]), sb("b2_col", [128, KC])
    psH, psY = ps("psH_f", 2, [128, cols_n]), ps("psY_f", 4, [128, cols_n])
    done, adone = chip.sem("dve_done"), chip.sem("act_done")
    names = ("high_done", "split_ready", "split_free", "psH_ready", "psH_free", "hid_ready", "hid_free", "hid_low_ready",
             "parts_free", "psY_ready", "psY_free")
    s = {n: chip.sem(n) for n in names}

    with ExitStack() as stack:
        w1_raw = stack.enter_context(nc.sbuf_tensor(chip.unique("w1_raw"), [128, KC, 2 * FF], F32))
        w2_raw = stack.enter_context(nc.sbuf_tensor(chip.unique("w2_raw"), [2 * FF, D], F32))
        with nc.Block() as block:

            @block.sync
            def _(sp):
                w1v = w1.rearrange("(c k) n -> k c n", c=KC)
                moves = ((w1_raw[:, :, 0:FF], w1v), (w1_raw[:, :, FF:2 * FF], w1v), (w2_raw[0:FF], w2),
                         (w2_raw[FF:2 * FF], w2), (b1_col[0:FF], b1.unsqueeze(1)), (b1_col[FF:2 * FF], b1.unsqueeze(1)),
                         (b2_col[:], b2))
                for out, in_ in moves:
                    sp.dma_start(out, in_).then_inc(chip.sem("w_in"), 16)
                sp.wait_ge(chip.sem("w_in"), 16 * len(moves))
                sp.sem_inc(chip.sem("w_in"), -(16 * len(moves)))
                sp.sem_inc(chip.sem("w_here"), 1)

            @block.scalar
            def _(act):
                act.wait_ge(chip.sem("w_here"), 1)
                act.sem_inc(chip.sem("w_here"), -1)
                nc.scalar.activation(w1_high[:], w1_raw[:], ACT.Copy).then_inc(adone, 1)
                nc.scalar.activation(w2_high[:], w2_raw[:], ACT.Copy).then_inc(adone, 1)
                act.wait_ge(adone, 2)
                act.sem_inc(adone, -2)
                act.sem_inc(chip.sem("w_high"), 1)

            @block.vector
            def _(dve):
                dve.wait_ge(chip.sem("w_high"), 1)
                dve.sem_inc(chip.sem("w_high"), -1)
                nc.vector.tensor_tensor(w1_low[:], w1_raw[:], w1_high[:], ALU.subtract).then_inc(done, 1)
                nc.vector.tensor_tensor(w2_low[:], w2_raw[:], w2_high[:], ALU.subtract).then_inc(done, 1)
                dve.wait_ge(done, 2)
                dve.sem_inc(done, -2)

    x_high, x_low = sb("ff_x_high", [128, KC, cols_n], F32R), sb("ff_x_low", [128, KC, cols_n], F32R)
    hid, parts_ = sb("hid", [2 * FF, cols_n]), sb("hid_parts", [2 * FF, 2, cols_n], F32R)
    PAIRS = (slice(0, 2), slice(2, 4))
    with nc.Block() as block:

        @block.scalar
        def _(act):
            def split(g, pair):
                act.wait_ge(s["split_free"], 1)
                act.sem_inc(s["split_free"], -1)
                nc.scalar.activation(x_high[:, PAIRS[pair]], xT[:, PAIRS[pair], ds(g * cols_n, cols_n)], ACT.Copy)\
                    .then_inc(s["high_done"], 1)

            def hidden(b):
                act.wait_ge(s["psH_ready"], 1)
                act.sem_inc(s["psH_ready"], -1)
                act.wait_ge(s["hid_free"], 1)
                act.sem_inc(s["hid_free"], -1)
                nc.scalar.activation(hid[:], psH[b][:], ACT.Relu, bias=b1_col[:, 0:1]).then_inc(adone, 1)
                act.wait_ge(s["parts_free"], 1)
                act.sem_inc(s["parts_free"], -1)
                act.wait_ge(adone, 1)
                act.sem_inc(adone, -1)
                act.sem_inc(s["psH_free"], 1)
                nc.scalar.activation(parts_[:, b], hid[:], ACT.Copy).then_inc(s["hid_ready"], 1)

            act.sem_inc(s["split_free"], 2)
            act.sem_inc(s["psH_free"], 2)
            split(0, 0)
            split(0, 1)
            with act.Fori(0, GROUPS // 2 - 1) as i:
                for b in range(2):
                    split(i * 2 + b + 1, 0)
                    split(i * 2 + b + 1, 1)
                    hidden(b)
            split(GROUPS - 1, 0)
            split(GROUPS - 1, 1)
            hidden(0)
            hidden(1)
            act.wait_ge(s["psH_free"], 2)
            act.sem_inc(s["psH_free"], -2)
            act.wait_ge(s["split_free"], 2)
            act.sem_inc(s["split_free"], -2)

        @block.gpsimd
        def _(pool):
            with pool.Fori(0, GROUPS) as g:
                for pair in range(2):
                    pool.wait_ge(s["high_done"], 1)
                    pool.sem_inc(s["high_done"], -1)
                    nc.gpsimd.tensor_tensor(x_low[:, PAIRS[pair]], xT[:, PAIRS[pair], ds(g * cols_n, cols_n)],
                                            x_high[:, PAIRS[pair]], ALU.subtract).then_inc(s["split_ready"], 1)

        @block.tensor
        def _(pe):
            def hidden(b):
                pe.wait_ge(s["psH_free"], 1)
                pe.sem_inc(s["psH_free"], -1)
                for pair in range(2):
                    pe.wait_ge(s["split_ready"], 1)
                    pe.sem_inc(s["split_ready"], -1)
                    parts = [(w, a, c) for c in (2 * pair, 2 * pair + 1)
                             for w, a in ((w1_high, x_high), (w1_low, x_high), (w1_high, x_low))]
                    for n, (w, a, c) in enumerate(parts):
                        last = nc.tensor.matmul(psH[b][:], w[:, c], a[:, c], start=pair == 0 and n == 0,
                                                stop=pair == 1 and n == len(parts) - 1)
                    last.then_inc(s["split_free"] if pair == 0 else chip.sem("pe_done"), 1)
                pe.wait_ge(chip.sem("pe_done"), 1)
                pe.sem_inc(chip.sem("pe_done"), -1)
                pe.sem_inc(s["split_free"], 1)
                pe.sem_inc(s["psH_ready"], 1)

            def outputs(b):
                pe.wait_ge(s["hid_low_ready"], 1)
                pe.sem_inc(s["hid_low_ready"], -1)
                for m in range(KC):
                    pe.wait_ge(s["psY_free"], 1)
                    pe.sem_inc(s["psY_free"], -1)
                    out = slice(m * 128, (m + 1) * 128)
                    nc.tensor.matmul(psY[m][:], w2_high[:, out], parts_[:, b], start=True, stop=False)
                    nc.tensor.matmul(psY[m][:], w2_low[0:FF, out], parts_[0:FF, b], start=False, stop=True)\
                        .then_inc(s["psY_ready"], 1)

            hidden(0)
            with pe.Fori(0, GROUPS // 2 - 1) as i:
                for b in range(2):
                    hidden(1 - b)
                    outputs(b)
            hidden(1)
            outputs(0)
            outputs(1)

        @block.vector
        def _(dve):
            dve.sem_inc(s["psY_free"], 4)
            dve.sem_inc(s["hid_free"], 1)
            dve.sem_inc(s["parts_free"], 2)

            def low(b):
                dve.wait_ge(s["hid_ready"], 1)
                dve.sem_inc(s["hid_ready"], -1)
                nc.vector.tensor_tensor(parts_[FF:2 * FF, b], hid[FF:2 * FF], parts_[FF:2 * FF, b], ALU.subtract)\
                    .then_inc(done, 1)

            def add(g, m):
                cols = ds(g * cols_n, cols_n)
                dve.wait_ge(s["psY_ready"], 1)
                dve.sem_inc(s["psY_ready"], -1)
                nc.vector.scalar_tensor_tensor(xT[:, m, cols], psY[m][:], b2_col[:, m:m + 1], xT[:, m, cols], ALU.add,
                                               ALU.add).then_inc(done, 1)

            def statistics(g, m):
                nc.vector.bn_stats(out=T.bn_stats[:, m, ds(g, 1)].rearrange("p a s -> p (a s)"),
                                   in_=xT[:, m, ds(g * cols_n, cols_n)]).then_inc(done, 1)

            def step(g, b, more):
                add(g, 0)
                add(g, 1)
                dve.wait_ge(done, 1)
                dve.sem_inc(done, -1)
                dve.sem_inc(s["psY_free"], 1)
                statistics(g, 0)
                if more:
                    low(1 - b)
                dve.wait_ge(done, 1)
                dve.sem_inc(done, -1)
                dve.sem_inc(s["psY_free"], 1)
                statistics(g, 1)
                add(g, 2)
                dve.wait_ge(done, 1)
                dve.sem_inc(done, -1)
                if more:
                    dve.wait_ge(done, 1)
                    dve.sem_inc(done, -1)
                    dve.sem_inc(s["hid_free"], 1)
                    dve.sem_inc(s["hid_low_ready"], 1)
                add(g, 3)
                dve.wait_ge(done, 2)
                dve.sem_inc(done, -2)
                dve.sem_inc(s["psY_free"], 1)
                statistics(g, 2)
                dve.wait_ge(done, 1)
                dve.sem_inc(done, -1)
                dve.sem_inc(s["psY_free"], 1)
                dve.sem_inc(s["parts_free"], 1)
                statistics(g, 3)
                dve.wait_ge(done, 2)
                dve.sem_inc(done, -2)

            low(0)
            dve.wait_ge(done, 1)
            dve.sem_inc(done, -1)
            dve.sem_inc(s["hid_free"], 1)
            dve.sem_inc(s["hid_low_ready"], 1)
            with dve.Fori(0, GROUPS // 2 - 1) as i:
                for b in range(2):
                    step(i * 2 + b, b, True)
            step(GROUPS - 2, 0, True)
            step(GROUPS - 1, 1, False)
            dve.wait_ge(s["psY_free"], 4)
            dve.sem_inc(s["psY_free"], -4)
            dve.wait_ge(s["hid_free"], 1)
            dve.sem_inc(s["hid_free"], -1)
            dve.wait_ge(s["parts_free"], 2)
            dve.sem_inc(s["parts_free"], -2)


def finish(chip, sb, ps, T, xT, gain, shift, out):
    nc = chip.nc
    x1 = sb("x1", [PARTS, 2, GROUP, D])
    column = sb("column", [128, 2, 2, KC, PARTS])
    gain_row, shift_row = sb("gain_row", [PARTS, D]), sb("shift_row", [PARTS, D])
    z = sb("z", [PARTS, 2, 2, D])
    stats, mv = sb("stats_z", [PARTS, 2, 6]), sb("mv_z", [PARTS, 2, 2, 2])
    rstd, off = sb("rstd_z", [PARTS, 2, 2]), sb("off_z", [PARTS, 2, 2])
    psZ = ps("psZ", 4, [128, D])
    done, adone, pooled = chip.sem("dve_done"), chip.sem("act_done"), chip.sem("pool_done")
    names = ("column_ready", "column_free", "psZ_ready", "psZ_free", "var_ready", "normed", "z_ready", "z_free", "sum_ready")
    s = {n: chip.sem(n) for n in names}
    x_in, sum_done, stored = (chip.sem2(n) for n in ("x_loaded", "sum_done", "stored"))
    t_in, t_out = tiles_of(T.x1), tiles_of(out)
    PAIRS = TILES // 2

    with nc.Block() as block:

        @block.sync
        def _(sp):
            for o, i_ in ((gain_row, gain), (shift_row, shift)):
                sp.dma_start(o[:], i_.unsqueeze(0).to_broadcast([PARTS, D])).then_inc(chip.sem("bias_in"), 16)
            sp.wait_ge(chip.sem("bias_in"), 32)
            sp.sem_inc(chip.sem("bias_in"), -32)
            sp.sem_inc(chip.sem("gains_here"), 1)
            sp.sem_inc(chip.sem("shifts_here"), 1)

            def load(g, b):
                sp.wait_ge(stored[b], ROWS_DMA)
                sp.sem_inc(stored[b], -ROWS_DMA)
                rows_dma(sp, x1[:, b], t_in[:, ds(g * GROUP, GROUP)], x_in[b])

            def store(g, b):
                sp.wait_ge(sum_done[b], 2)
                sp.sem_inc(sum_done[b], -2)
                rows_dma(sp, t_out[:, ds(g * GROUP, GROUP)], x1[:, b], stored[b])

            for b in range(2):
                sp.sem_inc(stored[b], ROWS_DMA)
                load(b, b)
            with sp.Fori(0, GROUPS // 2 - 1) as i:
                for b in range(2):
                    store(i * 2 + b, b)
                    load(i * 2 + b + 2, b)
            for b in range(2):
                store(GROUPS - 2 + b, b)
            for b in range(2):
                sp.wait_ge(stored[b], ROWS_DMA)
                sp.sem_inc(stored[b], -ROWS_DMA)

        @block.gpsimd
        def _(pool):
            def scales(u):
                pool.wait_ge(s["var_ready"], 1)
                pool.sem_inc(s["var_ready"], -1)
                nc.gpsimd.tensor_scalar(rstd[:, u], mv[:, u, :, 1], LN_EPS, None, ALU.add).then_inc(pooled, 1)
                nc.gpsimd.tensor_scalar(off[:, u], mv[:, u, :, 0], -1.0, None, ALU.mult).then_inc(pooled, 1)
                pool.wait_ge(pooled, 2)
                pool.sem_inc(pooled, -2)
                nc.gpsimd.tensor_tensor(rstd[:, u], rstd[:, u], T.minus_half[0:PARTS].to_broadcast([PARTS, 2]), ALU.pow)\
                    .then_inc(pooled, 1)
                pool.wait_ge(pooled, 1)
                pool.sem_inc(pooled, -1)
                nc.gpsimd.tensor_tensor(off[:, u], off[:, u], rstd[:, u], ALU.mult).then_inc(s["normed"], 1)

            pool.wait_ge(chip.sem("shifts_here"), 1)
            pool.sem_inc(chip.sem("shifts_here"), -1)
            scales(0)

            def shifted(b, u):
                rows = x1[:, b, 2 * u:2 * u + 2]
                nc.gpsimd.tensor_tensor(rows, rows, shift_row[:].unsqueeze(1).to_broadcast([PARTS, 2, D]), ALU.add)\
                    .then_inc(s["sum_ready"], 1)

            with pool.Fori(0, GROUPS // 2 - 1):
                for b in range(2):
                    pool.wait_ge(x_in[b], ROWS_DMA)
                    pool.sem_inc(x_in[b], -ROWS_DMA)
                    for u in range(2):
                        shifted(b, u)
                        scales(1 - u)
            for b in range(2):
                pool.wait_ge(x_in[b], ROWS_DMA)
                pool.sem_inc(x_in[b], -ROWS_DMA)
                for u in range(2):
                    shifted(b, u)
                    if (b, u) != (1, 1):
                        scales(1 - u)

        @block.scalar
        def _(act):
            def columns(pair, u):
                act.wait_ge(s["column_free"], 1)
                act.sem_inc(s["column_free"], -1)
                for k in range(2):
                    for c in range(KC):
                        column_op = nc.scalar.activation(column[:, u, k, c], xT[:, c, ds((pair * 2 + k) * PARTS, PARTS)],
                                                         ACT.Identity, bias=T.bn_off[:, c:c + 1], scale=T.bn_scale[:, c:c + 1])
                        column_op.then_inc(s["column_ready"], 1)

            def norm(u):
                act.wait_ge(s["normed"], 1)
                act.sem_inc(s["normed"], -1)
                act.wait_ge(s["z_free"], 1)
                act.sem_inc(s["z_free"], -1)
                for k in range(2):
                    nc.scalar.activation(z[:, u, k], psZ[2 * u + k][0:PARTS], ACT.Identity, bias=off[:, u, k:k + 1],
                                         scale=rstd[:, u, k:k + 1]).then_inc(adone, 1)
                act.wait_ge(adone, 2)
                act.sem_inc(adone, -2)
                act.sem_inc(s["psZ_free"], 1)
                act.sem_inc(s["z_ready"], 1)

            act.sem_inc(s["psZ_free"], 2)
            columns(0, 0)
            columns(1, 1)
            with act.Fori(0, PAIRS // 2 - 1) as i:
                for u in range(2):
                    norm(u)
                    columns(i * 2 + u + 2, u)
            norm(0)
            norm(1)
            act.wait_ge(s["psZ_free"], 2)
            act.sem_inc(s["psZ_free"], -2)
            act.wait_ge(s["column_free"], 2)
            act.sem_inc(s["column_free"], -2)
            act.wait_ge(s["z_free"], 2)
            act.sem_inc(s["z_free"], -2)

        @block.tensor
        def _(pe):
            with pe.Fori(0, PAIRS // 2):
                for u in range(2):
                    pe.wait_ge(s["psZ_free"], 1)
                    pe.sem_inc(s["psZ_free"], -1)
                    for k in range(2):
                        pe.wait_ge(s["column_ready"], KC)
                        pe.sem_inc(s["column_ready"], -KC)
                        for c in range(KC):
                            last = nc.tensor.transpose(psZ[2 * u + k][0:PARTS, c * 128:(c + 1) * 128], column[:, u, k, c],
                                                       T.ident[:])
                        last.then_inc(s["psZ_ready"], 1)

        @block.vector
        def _(dve):
            dve.wait_ge(chip.sem("gains_here"), 1)
            dve.sem_inc(chip.sem("gains_here"), -1)
            dve.sem_inc(s["z_free"], 2)
            dve.sem_inc(s["column_free"], 2)

            def statistics(u):
                for k in range(2):
                    dve.wait_ge(s["psZ_ready"], 1)
                    dve.sem_inc(s["psZ_ready"], -1)
                    nc.vector.bn_stats(out=stats[:, k], in_=psZ[2 * u + k][0:PARTS]).then_inc(done, 1)
                dve.sem_inc(s["column_free"], 1)
                dve.wait_ge(done, 2)
                dve.sem_inc(done, -2)
                for k in range(2):
                    nc.vector.bn_aggr(out=mv[:, u, k], in_=stats[:, k]).then_inc(done, 1)
                dve.wait_ge(done, 2)
                dve.sem_inc(done, -2)
                dve.sem_inc(s["var_ready"], 1)

            def add(b, u):
                dve.wait_ge(s["z_ready"], 1)
                dve.sem_inc(s["z_ready"], -1)
                nc.vector.tensor_tensor(z[:, u], z[:, u], gain_row[:].unsqueeze(1).to_broadcast([PARTS, 2, D]), ALU.mult)\
                    .then_inc(done, 1)
                dve.wait_ge(s["sum_ready"], 1)
                dve.sem_inc(s["sum_ready"], -1)
                dve.wait_ge(done, 1)
                dve.sem_inc(done, -1)
                rows = x1[:, b, 2 * u:2 * u + 2]
                nc.vector.tensor_tensor(rows, rows, z[:, u], ALU.add).then_inc(done, 1)
                dve.wait_ge(done, 1)
                dve.sem_inc(done, -1)
                dve.sem_inc(sum_done[b], 1)
                dve.sem_inc(s["z_free"], 1)

            statistics(0)
            statistics(1)
            with dve.Fori(0, GROUPS // 2 - 1):
                for b in range(2):
                    for u in range(2):
                        add(b, u)
                        statistics(u)
            for b in range(2):
                for u in range(2):
                    add(b, u)
                    if b == 0:
                        statistics(u)


class Names:
    pass


def program(nc, A, out, scratch):
    ctx = ExitStack()
    with ctx:
        chip = Chip(nc, ctx)

        def allocator(stack):
            def sb(name, shape, dtype=F32):
                return stack.enter_context(nc.sbuf_tensor(chip.unique(name), shape, dtype))

            def ps(name, n, shape):
                size = math.prod(shape[1:])
                banks = -(-size // 512)
                whole = [stack.enter_context(nc.psum_tensor(chip.unique(name), [128, banks * 512], F32)) for k in range(n)]
                pieces = [w[0:shape[0], 0:size] for w in whole]
                return pieces if len(shape) == 2 else [x.rearrange("p (a b) -> p a b", a=shape[1]) for x in pieces]
            return sb, ps

        keep, _ = allocator(ctx)
        T, W = Names(), Names()
        T.messages, T.agg_l0, T.agg, T.x1 = scratch("messages", [N, MSG]), \
            [scratch(f"agg_l0_{k}", [N + PARTS, AGG]) for k in range(2)], scratch("agg", [N + PARTS, D]), scratch("x1_rows", [N, D])
        T.pairs = scratch("sorted_edges", [N, 2], I32)
        xT = keep("xT", [128, KC, N])
        rooms = [xT[0:PARTS, c].rearrange("p (t q) -> p t q", t=TILES) for c in range(KC)]
        T.same_src, T.earlier, T.srcq_i, T.zeros = rooms[0], rooms[1], rooms[2].bitcast(I32), xT[0:PARTS, 3]
        T.ident = keep("ident", [128, 128])
        T.minus_half = keep("minus_half", [128, 1])
        T.dst_ext = keep("dst_ext", [PARTS, TILES + 2], I32)
        T.dst_f = keep("dst_f", [PARTS, TILES + 2])
        T.src_i = keep("src_i", [PARTS, TILES], I32)
        T.spare_i, T.spare = keep("spare_i", [PARTS, 1], I32), keep("spare", [PARTS, 1])
        interaction = ExitStack()
        keep_l0, _ = allocator(interaction)
        W.f2o1_s, W.f2o2_s, W.vec = keep_l0("w_f2o1_s", [128, B]), keep_l0("w_f2o2_s", [B, B]), keep_l0("w_vec", [128, 2, B])
        with ExitStack() as edges:
            sb, _ = allocator(edges)
            W.in2f, W.w1, W.b1, W.w2 = sb("w_in2f", [B, 2, F]), sb("w1", [R, F]), sb("b1", [F, 1]), sb("w2", [F + 1, 6 * F])
            T.src_f = sb("src_f", [PARTS, TILES])
            T.rcut, T.y = sb("rcut", [PARTS, TILES]), sb("y", [PARTS, TILES, 4])
            T.dup, T.tmp80, T.scat_i = sb("dup", [PARTS, TILES]), sb("tmp80", [PARTS, TILES]), sb("scat_i", [PARTS, TILES], I32)
            T.lower = sb("lower", [PARTS, PARTS])
            with chip.stage() as stage:
                setup(chip, *allocator(stage), T, W, A)
            with chip.stage() as stage:
                l0_node_messages(chip, *allocator(stage), A.x, T, W)
            with chip.stage() as stage:
                l0_edges(chip, *allocator(stage), T, W, A.radial, A.dst_tiled)
            with chip.stage() as stage:
                sort_edges(chip, *allocator(stage), T)
        with chip.stage() as stage:
            l0_nodes(chip, *allocator(stage), A.x, T, W, xT)
        interaction.close()

        T.q, T.k, T.v = (scratch(n, [N, D]) for n in ("q", "k", "v"))
        T.same, T.same_next, T.same_neg, T.next_neg = (keep(n, [PARTS, TILES]) for n in ("same", "same_next", "same_neg", "next_neg"))
        T.row_i, T.fix_i, T.carry = keep("row_i", [PARTS, TILES], I32), keep("fix_i", [PARTS, 1], I32), keep("carry", [PARTS, PARTS])
        T.pass_fwd, T.pass_bwd, T.cont = keep("pass_fwd", [HEADS, PARTS]), keep("pass_bwd", [HEADS, PARTS]), \
            keep("cont", [HEADS, PARTS + 1])
        T.weight = keep("weight", [PARTS, HEADS, TILES])
        T.bn_scale, T.bn_off = keep("bn_scale", [128, KC]), keep("bn_off", [128, KC])
        with chip.stage() as stage:
            attention_masks(chip, *allocator(stage), T)
        for layer in range(LAYERS):
            for weight, bias, table, scores in ((A.wk, None, T.k, None), (A.wq, A.bq, T.q, None),
                                                (A.wv, None, T.v, scores_and_softmax)):
                with chip.stage() as stage:
                    project(chip, *allocator(stage), T, xT, weight[layer], None if bias is None else bias[layer], table, scores,
                            normalise=layer > 0 and table is T.k)
            with chip.stage() as stage:
                aggregate(chip, *allocator(stage), T)
            with ExitStack() as norms:
                T.bn_stats = allocator(norms)[0]("bn_stats", [128, KC, HSTEPS, 6])
                with chip.stage() as stage:
                    output_projection(chip, *allocator(stage), T, xT, A.wo[layer], A.bo[layer])
                with chip.stage() as stage:
                    batchnorm(chip, allocator(stage)[0], T, xT, A.g1[layer], A.beta1[layer], HSTEPS, apply=True)
                with chip.stage() as stage:
                    feed_forward(chip, *allocator(stage), T, xT, A.ff1[layer], A.ffb1[layer], A.ff2[layer], A.ffb2[layer])
                with chip.stage() as stage:
                    batchnorm(chip, allocator(stage)[0], T, xT, A.g2[layer], A.beta2[layer], GROUPS, apply=False)
        with chip.stage() as stage:
            finish(chip, *allocator(stage), T, xT, A.ln_g, A.ln_b, out)


def kernel(**inputs):
    import numpy as np
    import concourse.bacc as bacc
    from concourse.bass_utils import run_bass_kernel_spmd

    nc = bacc.Bacc("TRN2", target_bir_lowering=False, num_devices=1)
    g = {k: np.asarray(v) for k, v in inputs.items()}
    laid = {
        "x": g["x"],
        "src": g["src"], "dst": g["dst"],
        "src_tiled": g["src"].reshape(PARTS, TILES).T.reshape(-1),
        "dst_tiled": g["dst"].reshape(PARTS, TILES).T,
        "radial": g["edge_attr_20"].reshape(PARTS, TILES, R).transpose(2, 1, 0).reshape(R, E),
        "y": g["edge_attr_4"], "rcut": g["edge_weight"],
        "in2f_s": g["L0_gnn_w_in2f_s"], "in2f_v": g["L0_gnn_w_in2f_v"],
        "w1": g["L0_gnn_W1"], "b1": g["L0_gnn_b1"],
        "w2": g["L0_gnn_W2"].reshape(F, F, 6).transpose(0, 2, 1).reshape(F, 6 * F),
        "b2": g["L0_gnn_b2"].reshape(F, 6).T.reshape(6 * F),
        "f2o1_s": g["L0_gnn_w_f2o1_s"], "f2o1_vT": g["L0_gnn_w_f2o1_v"].T,
        "f2o2_s": g["L0_gnn_w_f2o2_s"], "f2o2_v": g["L0_gnn_w_f2o2_v"],
        "ln_g": g["L1_gnn_ln_g"], "ln_b": g["L1_gnn_ln_b"], "bq": g["L1_gnn_bq"], "ffb1": g["L1_gnn_b1"],
    }
    for to, name in (("wq", "Wq"), ("wk", "Wk"), ("wv", "Wv"), ("wo", "Wo"), ("ff1", "W1"), ("ff2", "W2")):
        laid[to] = g["L1_gnn_" + name].transpose(0, 2, 1)
    for to, name in (("bo", "bo"), ("ffb2", "b2"), ("g1", "g1"), ("beta1", "beta1"), ("g2", "g2"), ("beta2", "beta2")):
        laid[to] = g["L1_gnn_" + name].reshape(LAYERS, KC, 128).transpose(0, 2, 1)
    arrays, A = {}, Names()
    for name, a in laid.items():
        arrays[f"in_{name}"] = np.ascontiguousarray(a)
        A.__dict__[name] = nc.dram_tensor(f"in_{name}", list(a.shape), mybir.dt.from_np(a.dtype), kind="ExternalInput").ap()
    out = nc.dram_tensor("out", [N, D], F32, kind="ExternalOutput").ap()

    def scratch(name, shape, dtype=F32):
        return nc.dram_tensor(name, shape, dtype).ap()

    program(nc, A, out, scratch)
    return run_bass_kernel_spmd(nc, [arrays], core_ids=[0]).results[0]["out"]
```
